# Optimizing a Trainium2 kernel written in Bass

```python
import numpy as np
import jax
import jax.numpy as jnp

def _softmax(x, axis=-1):
    return jax.nn.softmax(x, axis=axis)

def _gelu(x):
    return jax.nn.gelu(x, approximate=True)

def _silu(x):
    return jax.nn.silu(x)

def _sigmoid(x):
    return jax.nn.sigmoid(x)

def _layernorm(x, axis=-1, eps=1e-05):
    m = jnp.mean(x, axis=axis, keepdims=True)
    v = jnp.var(x, axis=axis, keepdims=True)
    return (x - m) / jnp.sqrt(v + eps)

def _scatter_add(tgt, idx, src, axis=0):
    return tgt.at[idx].add(src)

def _segment_sum(src, seg, n):
    return jax.ops.segment_sum(src, seg, n)
kernel_name = 'mk_adj_ffn_d2_adj_r2_067f51'

def setup_inputs(seed: int=0):
    np.random.seed(seed)
    _w = jnp.asarray

    def _rec_inputs():
        import jax
        import jax.numpy as jnp
        _gk = jax.random.key(seed)
        x = -0.0005963 + 1.001 * jax.random.normal(jax.random.fold_in(_gk, 1), (2048, 256), jnp.float32)
        _w = (1.0 + jnp.arange(2048, dtype=jnp.float32)) ** (-0.5)
        _w = _w / _w.mean()
        _pij = jnp.clip(0.00390625 * _w[:, None] * _w[None, :], 0.0, 1.0)
        _a = jax.random.uniform(jax.random.fold_in(_gk, 2), (2048, 2048)) < _pij
        _af = _a.astype(jnp.float32)
        adj = _af
        return (x, adj)
    x, adj = _rec_inputs()

    def _L0_gnn_setup():
        import jax, jax.numpy as jnp
        import numpy as np
        N = 3072
        D_IN = 256
        D_OUT = 256
        DENSITY = 0.005
        key = jax.random.key(seed)
        ks = jax.random.split(key, 12)
        x = jax.random.normal(ks[0], (N, D_IN), dtype=jnp.float32)
        adj_a = (jax.random.uniform(ks[1], (N, N)) < DENSITY).astype(jnp.float32)
        adj_b = (jax.random.uniform(ks[2], (N, N)) < DENSITY).astype(jnp.float32)
        W_sa = jax.random.normal(ks[3], (D_IN, D_OUT), dtype=jnp.float32) * (1.414 / np.sqrt(D_IN + D_OUT))
        a_sa = jax.random.normal(ks[4], (1, 2 * D_OUT), dtype=jnp.float32) * (1.414 / np.sqrt(1 + 2 * D_OUT))
        stdv = 1.0 / np.sqrt(D_OUT)
        W_gcnb = jax.random.uniform(ks[5], (D_IN, D_OUT), minval=-stdv, maxval=stdv, dtype=jnp.float32)
        b_gcnb = jax.random.uniform(ks[6], (D_OUT,), minval=-stdv, maxval=stdv, dtype=jnp.float32)
        s = 1.0 / np.sqrt(2 * D_IN)
        Wa = jax.random.uniform(ks[7], (1, 2 * D_IN), minval=-s, maxval=s, dtype=jnp.float32)
        ba = jax.random.uniform(ks[8], (1,), minval=-s, maxval=s, dtype=jnp.float32)
        Wb = jax.random.uniform(ks[9], (1, 2 * D_IN), minval=-s, maxval=s, dtype=jnp.float32)
        bb = jax.random.uniform(ks[10], (1,), minval=-s, maxval=s, dtype=jnp.float32)
        return {'x': x, 'adj_a': adj_a, 'adj_b': adj_b, 'W_sa': W_sa, 'a_sa': a_sa, 'W_gcnb': W_gcnb, 'b_gcnb': b_gcnb, 'Wa': Wa, 'ba': ba, 'Wb': Wb, 'bb': bb}
    _L0_gnn_all = _L0_gnn_setup()
    _L0_gnn_in = {k: v for k, v in _L0_gnn_all.items() if k in ('W_sa', 'a_sa', 'W_gcnb', 'b_gcnb', 'Wa', 'ba', 'Wb', 'bb')}
    del _L0_gnn_all

    def _L0_ffn_setup():
        import jax, jax.numpy as jnp
        import numpy as np
        B, S, H, I, E, K = (8, 2048, 256, 1024, 8, 2)
        key = jax.random.key(seed)
        ks = jax.random.split(key, 7)
        sH = 1.0 / np.sqrt(H)
        sI = 1.0 / np.sqrt(I)
        return {'x': jax.random.normal(ks[0], (B, S, H), dtype=jnp.float32), 'gate_w': jax.random.uniform(ks[1], (H, E), jnp.float32, -sH, sH), 'gate_b': jnp.zeros((E,), jnp.float32), 'w1': jax.random.uniform(ks[2], (E, H, I), jnp.float32, -sH, sH), 'b1': jax.random.uniform(ks[3], (E, I), jnp.float32, -sH, sH), 'w2': jax.random.uniform(ks[4], (E, I, H), jnp.float32, -sI, sI), 'b2': jax.random.uniform(ks[5], (E, H), jnp.float32, -sI, sI)}
    _L0_ffn_all = _L0_ffn_setup()
    _L0_ffn_in = {k: v for k, v in _L0_ffn_all.items() if k in ('gate_w', 'gate_b', 'w1', 'b1', 'w2', 'b2')}
    del _L0_ffn_all

    def _L1_gnn_setup():
        import jax, jax.numpy as jnp
        import numpy as np
        N, F, H = (1536, 256, 4)
        D = F // H
        ALPHA = 0.5
        EPS = 1e-06

        def _batchnorm(x, gamma, beta):
            m = jnp.mean(x, axis=0)
            v = jnp.var(x, axis=0)
            return (x - m) * jax.lax.rsqrt(v + EPS) * gamma + beta

        def _masked_softmax(scores, mask):
            s = jnp.where(mask, scores, -jnp.inf)
            att = jax.nn.softmax(s, axis=-1)
            return jnp.where(mask, att, 0.0)

        def _mlp_block(x, Wm, bm, g, b):
            h = jax.nn.elu(x @ Wm.T + bm) + x
            return _batchnorm(h, g, b)
        key = jax.random.key(seed)
        ks = jax.random.split(key, 12)
        X = jax.random.normal(ks[0], (N, F), dtype=jnp.float32)
        eye = jnp.eye(N, dtype=jnp.float32)
        local = (jax.random.uniform(ks[1], (N, N)) < 32.0 / N).astype(jnp.float32)
        local = jnp.clip(local + eye, 0.0, 1.0)
        longr = (jax.random.uniform(ks[2], (N, N)) < 16.0 / N).astype(jnp.float32)
        longr = jnp.clip(longr + eye, 0.0, 1.0)
        W = jax.random.normal(ks[3], (H, D, D), dtype=jnp.float32) * 0.1
        V = jax.random.normal(ks[4], (H, 2, D, 1), dtype=jnp.float32) * 0.1
        return {'X': X, 'local_pattern': local, 'long_range_pattern': longr, 'W': W, 'V': V, 'enc_bn_gamma': jnp.ones((F,), jnp.float32), 'enc_bn_beta': jnp.zeros((F,), jnp.float32), 'enc_mlp_W': jax.random.normal(ks[5], (F, F), dtype=jnp.float32) * 0.02, 'enc_mlp_b': jnp.zeros((F,), jnp.float32), 'enc_mlp_bn_gamma': jnp.ones((F,), jnp.float32), 'enc_mlp_bn_beta': jnp.zeros((F,), jnp.float32), 'dec_mlp_W': jax.random.normal(ks[6], (F, F), dtype=jnp.float32) * 0.02, 'dec_mlp_b': jnp.zeros((F,), jnp.float32), 'dec_mlp_bn_gamma': jnp.ones((F,), jnp.float32), 'dec_mlp_bn_beta': jnp.zeros((F,), jnp.float32)}
    _L1_gnn_all = _L1_gnn_setup()
    _L1_gnn_in = {k: v for k, v in _L1_gnn_all.items() if k in ('W', 'V', 'enc_bn_gamma', 'enc_bn_beta', 'enc_mlp_W', 'enc_mlp_b', 'enc_mlp_bn_gamma', 'enc_mlp_bn_beta', 'dec_mlp_W', 'dec_mlp_b', 'dec_mlp_bn_gamma', 'dec_mlp_bn_beta')}
    del _L1_gnn_all

    def _L1_ffn_setup():
        import jax, jax.numpy as jnp
        import numpy as np
        D_MODEL = 256
        N_EXPERTS = 8
        D_FF = 1024
        TOP_K = 2
        B, S = (2, 1024)
        key = jax.random.key(seed)
        ks = jax.random.split(key, 4)
        init = lambda k, shape, fan_in: jax.random.normal(k, shape, jnp.float32) / np.float32(np.sqrt(fan_in))
        return {'x': jax.random.normal(ks[0], (B, S, D_MODEL), jnp.float32), 'Wg': init(ks[1], (D_MODEL, N_EXPERTS), D_MODEL), 'bg': jnp.zeros((N_EXPERTS,), jnp.float32), 'W1': init(ks[2], (N_EXPERTS, D_MODEL, D_FF), D_MODEL), 'b1': jnp.zeros((N_EXPERTS, D_FF), jnp.float32), 'W2': init(ks[3], (N_EXPERTS, D_FF, D_MODEL), D_FF), 'b2': jnp.zeros((N_EXPERTS, D_MODEL), jnp.float32)}
    _L1_ffn_all = _L1_ffn_setup()
    _L1_ffn_in = {k: v for k, v in _L1_ffn_all.items() if k in ('Wg', 'bg', 'W1', 'b1', 'W2', 'b2')}
    del _L1_ffn_all
    return {'x': x, 'adj': adj, 'L0_gnn_W_sa': _L0_gnn_in['W_sa'], 'L0_gnn_a_sa': _L0_gnn_in['a_sa'], 'L0_gnn_W_gcnb': _L0_gnn_in['W_gcnb'], 'L0_gnn_b_gcnb': _L0_gnn_in['b_gcnb'], 'L0_gnn_Wa': _L0_gnn_in['Wa'], 'L0_gnn_ba': _L0_gnn_in['ba'], 'L0_gnn_Wb': _L0_gnn_in['Wb'], 'L0_gnn_bb': _L0_gnn_in['bb'], 'L0_ffn_gate_w': _L0_ffn_in['gate_w'], 'L0_ffn_gate_b': _L0_ffn_in['gate_b'], 'L0_ffn_w1': _L0_ffn_in['w1'], 'L0_ffn_b1': _L0_ffn_in['b1'], 'L0_ffn_w2': _L0_ffn_in['w2'], 'L0_ffn_b2': _L0_ffn_in['b2'], 'L1_gnn_W': _L1_gnn_in['W'], 'L1_gnn_V': _L1_gnn_in['V'], 'L1_gnn_enc_bn_gamma': _L1_gnn_in['enc_bn_gamma'], 'L1_gnn_enc_bn_beta': _L1_gnn_in['enc_bn_beta'], 'L1_gnn_enc_mlp_W': _L1_gnn_in['enc_mlp_W'], 'L1_gnn_enc_mlp_b': _L1_gnn_in['enc_mlp_b'], 'L1_gnn_enc_mlp_bn_gamma': _L1_gnn_in['enc_mlp_bn_gamma'], 'L1_gnn_enc_mlp_bn_beta': _L1_gnn_in['enc_mlp_bn_beta'], 'L1_gnn_dec_mlp_W': _L1_gnn_in['dec_mlp_W'], 'L1_gnn_dec_mlp_b': _L1_gnn_in['dec_mlp_b'], 'L1_gnn_dec_mlp_bn_gamma': _L1_gnn_in['dec_mlp_bn_gamma'], 'L1_gnn_dec_mlp_bn_beta': _L1_gnn_in['dec_mlp_bn_beta'], 'L1_ffn_Wg': _L1_ffn_in['Wg'], 'L1_ffn_bg': _L1_ffn_in['bg'], 'L1_ffn_W1': _L1_ffn_in['W1'], 'L1_ffn_b1': _L1_ffn_in['b1'], 'L1_ffn_W2': _L1_ffn_in['W2'], 'L1_ffn_b2': _L1_ffn_in['b2']}

def reference(x, adj, L0_gnn_W_sa, L0_gnn_a_sa, L0_gnn_W_gcnb, L0_gnn_b_gcnb, L0_gnn_Wa, L0_gnn_ba, L0_gnn_Wb, L0_gnn_bb, L0_ffn_gate_w, L0_ffn_gate_b, L0_ffn_w1, L0_ffn_b1, L0_ffn_w2, L0_ffn_b2, L1_gnn_W, L1_gnn_V, L1_gnn_enc_bn_gamma, L1_gnn_enc_bn_beta, L1_gnn_enc_mlp_W, L1_gnn_enc_mlp_b, L1_gnn_enc_mlp_bn_gamma, L1_gnn_enc_mlp_bn_beta, L1_gnn_dec_mlp_W, L1_gnn_dec_mlp_b, L1_gnn_dec_mlp_bn_gamma, L1_gnn_dec_mlp_bn_beta, L1_ffn_Wg, L1_ffn_bg, L1_ffn_W1, L1_ffn_b1, L1_ffn_W2, L1_ffn_b2):
    import jax
    import jax.numpy as jnp

    def _L0_gnn_ref(x, adj_a, adj_b, W_sa, a_sa, W_gcnb, b_gcnb, Wa, ba, Wb, bb):
        import jax, jax.numpy as jnp
        import numpy as np
        N = 3072
        D_IN = 256
        D_OUT = 256
        DENSITY = 0.005
        type_sum_a = adj_a @ x
        type_sum_b = adj_b @ x
        attn_a = jax.nn.sigmoid(jnp.concatenate([type_sum_a, x], axis=1) @ Wa.T + ba)
        attn_b = jax.nn.sigmoid(jnp.concatenate([type_sum_b, x], axis=1) @ Wb.T + bb)
        h = x @ W_sa
        Hd = h.shape[1]
        s_left = h @ a_sa[0, :Hd]
        s_right = h @ a_sa[0, Hd:]
        scores = s_left[:, None] + s_right[None, :]
        e = jnp.where(adj_a != 0, jnp.exp(-jax.nn.leaky_relu(scores, 0.01)), 0.0)
        attn = e / (jnp.sum(e, axis=1, keepdims=True) + 1e-05)
        x_a = attn @ h
        x_b = adj_b @ (x @ W_gcnb) + b_gcnb
        return jax.nn.sigmoid(attn_a * x_a + attn_b * x_b)

    def _L0_ffn_ref(x, gate_w, gate_b, w1, b1, w2, b2):
        import jax, jax.numpy as jnp
        import numpy as np
        B, S, H, I, E, K = (8, 2048, 256, 1024, 8, 2)
        gate_probs = jax.nn.softmax(x @ gate_w + gate_b, axis=-1)
        top_v, top_i = jax.lax.top_k(gate_probs, K)
        top_w = jax.nn.softmax(top_v, axis=-1)
        out = jnp.zeros_like(x)
        for e in range(E):
            ce = jnp.sum(jnp.where(top_i == e, top_w, 0.0), axis=-1)
            h = jax.nn.relu(jnp.einsum('bsh,hi->bsi', x, w1[e]) + b1[e])
            ye = jnp.einsum('bsi,ih->bsh', h, w2[e]) + b2[e]
            out = out + ce[..., None] * ye
        return out

    def _L1_gnn_ref(X, local_pattern, long_range_pattern, W, V, enc_bn_gamma, enc_bn_beta, enc_mlp_W, enc_mlp_b, enc_mlp_bn_gamma, enc_mlp_bn_beta, dec_mlp_W, dec_mlp_b, dec_mlp_bn_gamma, dec_mlp_bn_beta):
        import jax, jax.numpy as jnp
        import numpy as np
        N, F, H = (1536, 256, 4)
        D = F // H
        ALPHA = 0.5
        EPS = 1e-06

        def _batchnorm(x, gamma, beta):
            m = jnp.mean(x, axis=0)
            v = jnp.var(x, axis=0)
            return (x - m) * jax.lax.rsqrt(v + EPS) * gamma + beta

        def _masked_softmax(scores, mask):
            s = jnp.where(mask, scores, -jnp.inf)
            att = jax.nn.softmax(s, axis=-1)
            return jnp.where(mask, att, 0.0)

        def _mlp_block(x, Wm, bm, g, b):
            h = jax.nn.elu(x @ Wm.T + bm) + x
            return _batchnorm(h, g, b)
        n = X.shape[0]
        Xh = X.reshape(n, H, D).transpose(1, 0, 2)
        Xw = jnp.einsum('hnd,hde->hne', Xh, W)
        f1 = jnp.einsum('hnd,hd->hn', Xw, V[:, 0, :, 0])
        f2 = jnp.einsum('hnd,hd->hn', Xw, V[:, 1, :, 0])
        sig = jax.nn.sigmoid(f1[:, :, None] + f2[:, None, :])
        lmask = (local_pattern != 0)[None]
        gmask = (long_range_pattern != 0)[None]
        local_att = _masked_softmax(local_pattern[None] * sig, lmask)
        long_att = _masked_softmax(long_range_pattern[None] * sig, gmask)
        att = ALPHA * long_att + (1.0 - ALPHA) * local_att
        Xa = jnp.einsum('hij,hjd->hid', att, Xw)
        Xc = Xa.transpose(1, 0, 2).reshape(n, F)
        Xn = _batchnorm(Xc, enc_bn_gamma, enc_bn_beta)
        emb = _mlp_block(Xn, enc_mlp_W, enc_mlp_b, enc_mlp_bn_gamma, enc_mlp_bn_beta)
        Yh = emb.reshape(n, H, D).transpose(1, 0, 2)
        Y = jnp.einsum('hij,hjd->hid', att, Yh)
        Y = jnp.einsum('hnd,hed->hne', Y, W)
        Yc = Y.transpose(1, 0, 2).reshape(n, F)
        Yc = jax.nn.elu(Yc)
        out = _mlp_block(Yc, dec_mlp_W, dec_mlp_b, dec_mlp_bn_gamma, dec_mlp_bn_beta)
        return out

    def _L1_ffn_ref(x, Wg, bg, W1, b1, W2, b2):
        import jax, jax.numpy as jnp
        import numpy as np
        D_MODEL = 256
        N_EXPERTS = 8
        D_FF = 1024
        TOP_K = 2
        B, S = (2, 1024)
        b, s, d = x.shape
        xt = x.reshape(-1, d)
        logits = xt @ Wg + bg
        probs = jax.nn.softmax(logits, axis=-1)
        top_p, top_i = jax.lax.top_k(probs, TOP_K)
        top_p = top_p / top_p.sum(axis=-1, keepdims=True)
        T = xt.shape[0]
        combine = jnp.zeros((T, N_EXPERTS), x.dtype).at[jnp.arange(T)[:, None], top_i].add(top_p)
        h = jax.nn.relu(jnp.einsum('td,edf->etf', xt, W1) + b1[:, None, :])
        y = jnp.einsum('etf,efd->etd', h, W2) + b2[:, None, :]
        out = jnp.einsum('te,etd->td', combine, y)
        return out.reshape(b, s, d)
    x = x + _L0_gnn_ref(_layernorm(x, axis=-1), adj, adj, L0_gnn_W_sa, L0_gnn_a_sa, L0_gnn_W_gcnb, L0_gnn_b_gcnb, L0_gnn_Wa, L0_gnn_ba, L0_gnn_Wb, L0_gnn_bb)
    x = x + _L0_ffn_ref(_layernorm(x, axis=-1)[None], L0_ffn_gate_w, L0_ffn_gate_b, L0_ffn_w1, L0_ffn_b1, L0_ffn_w2, L0_ffn_b2)[0]
    x = x + _L1_gnn_ref(_layernorm(x, axis=-1), adj, adj, L1_gnn_W, L1_gnn_V, L1_gnn_enc_bn_gamma, L1_gnn_enc_bn_beta, L1_gnn_enc_mlp_W, L1_gnn_enc_mlp_b, L1_gnn_enc_mlp_bn_gamma, L1_gnn_enc_mlp_bn_beta, L1_gnn_dec_mlp_W, L1_gnn_dec_mlp_b, L1_gnn_dec_mlp_bn_gamma, L1_gnn_dec_mlp_bn_beta)
    x = x + _L1_ffn_ref(_layernorm(x, axis=-1)[None], L1_ffn_Wg, L1_ffn_bg, L1_ffn_W1, L1_ffn_b1, L1_ffn_W2, L1_ffn_b2)[0]
    return x

_drawn_inputs = setup_inputs


def setup_inputs(seed=0):
    import zlib

    import numpy as np

    out = dict(_drawn_inputs(seed))
    spreads = {'L0_ffn_gate_b': (0.0, 0.1),
     'L1_gnn_enc_bn_gamma': (1.0, 0.2),
     'L1_gnn_enc_bn_beta': (0.0, 1.463),
     'L1_gnn_enc_mlp_b': (0.0, 0.354),
     'L1_gnn_enc_mlp_bn_gamma': (1.0, 0.2),
     'L1_gnn_enc_mlp_bn_beta': (0.0, 0.1),
     'L1_gnn_dec_mlp_b': (0.0, 0.291),
     'L1_gnn_dec_mlp_bn_gamma': (1.0, 0.2),
     'L1_gnn_dec_mlp_bn_beta': (0.0, 0.1),
     'L1_ffn_bg': (0.0, 0.1),
     'L1_ffn_b1': (0.0, 0.1),
     'L1_ffn_b2': (0.0, 0.1)}
    factors = {'L0_gnn_b_gcnb': 2.782}
    for name, (base, spread) in spreads.items():
        noise = np.random.default_rng([zlib.crc32(name.encode()), seed]).standard_normal(out[name].shape)
        drawn = base * np.exp(spread * noise) if base else spread * noise
        out[name] = jnp.asarray(drawn.astype(out[name].dtype))
    for name, factor in factors.items():
        out[name] = (out[name] * factor).astype(out[name].dtype)
    return out
```

```python
from contextlib import ExitStack

import concourse.bass as bass
from concourse import mybir

F32 = mybir.dt.float32
BF16 = mybir.dt.bfloat16
F32R = mybir.dt.float32r
I32 = mybir.dt.int32
U32 = mybir.dt.uint32
ALU = mybir.AluOpType
ACT = mybir.ActivationFunctionType
AX_X = mybir.AxisListType.X

P = 128
N = 2048
NT = N // P
D = 256
KC = D // P
E = 8
F = 1024
FT = F // P
TOP = 2
BLK = 256
BT = BLK // P
NB = (TOP * N + E * (BLK - 1)) // BLK
H = 4
DH = D // H
LN_EPS = 1e-5
BN_EPS = 1e-6
ds = bass.ds

VEC_NAMES = ["L1_gnn_enc_bn_gamma", "L1_gnn_enc_bn_beta", "L1_gnn_enc_mlp_b", "L1_gnn_enc_mlp_bn_gamma",
             "L1_gnn_enc_mlp_bn_beta", "L1_gnn_dec_mlp_b", "L1_gnn_dec_mlp_bn_gamma", "L1_gnn_dec_mlp_bn_beta"]
VEC_COL = {name: 8 + KC * i for i, name in enumerate(VEC_NAMES)}
VEC_ROWS = 8 + KC * len(VEC_NAMES)


class Shared:
    pass


class Chain:

    def __init__(self, eng, sem):
        self.eng, self.sem, self.count = eng, sem, 0

    def did(self, ins):
        ins.then_inc(self.sem, 1)
        self.count += 1

    def settle(self):
        self.eng.wait_ge(self.sem, self.count)

    def link(self, ins):
        self.did(ins)
        self.settle()


def rstd_of(chain, nc_vector, out, var, tmp, sqrt_wait):
    chain.link(nc_vector.tensor_tensor(tmp, out, out, ALU.mult))
    chain.link(nc_vector.tensor_tensor(tmp, tmp, var, ALU.mult))
    chain.link(nc_vector.tensor_scalar(tmp, tmp, -0.5, 1.5, ALU.mult, ALU.add))
    chain.link(nc_vector.tensor_tensor(out, out, tmp, ALU.mult))


def layer_norm_vector(k, dve, chain, var_ready, std_ready, tile_ready, x_ready=None):
    v = k.nc.vector
    for n in range(NT):
        if x_ready is not None and n % 4 == 0:
            dve.wait_ge(x_ready[n // 4], 16)
        chain.did(v.bn_stats(k.ln_stats[:, n, :], k.x[:, n, :]))
    chain.settle()
    for n in range(NT):
        chain.did(v.bn_aggr(k.ln_mv[:, n, :], k.ln_stats[:, n, :]))
    chain.settle()
    v.tensor_scalar(k.ln_var[:], k.ln_mv[:, :, 1], LN_EPS, None, ALU.add).then_inc(var_ready, 1)
    dve.wait_ge(std_ready, 1)
    chain.link(v.reciprocal(k.ln_rstd[:], k.ln_std[:]))
    rstd_of(chain, v, k.ln_rstd[:], k.ln_var[:], k.ln_tmp[:], None)
    for n in range(NT):
        v.tensor_scalar(k.xn[:, n, :], k.x[:, n, :], k.ln_mv[:, n, 0:1], k.ln_rstd[:, n:n + 1],
                        ALU.subtract, ALU.mult).then_inc(tile_ready, 1)


def layer_norm_sqrt(k, act, var_ready, std_ready):
    act.wait_ge(var_ready, 1)
    k.nc.scalar.activation(k.ln_std[:], k.ln_var[:], ACT.Sqrt).then_inc(std_ready, 1)


def transpose_xn_tensor(k, pe, ps, tile_ready, pair_ps, pair_sb):
    for q in range(NT // 2):
        pe.wait_ge(tile_ready, 2 * q + 2)
        if q >= 2:
            pe.wait_ge(pair_sb, q - 1)
        for c in range(KC):
            for t in range(2):
                ins = k.nc.tensor.transpose(ps[:, q % 2, c * 2 * P + t * P:c * 2 * P + (t + 1) * P],
                                            k.xn[:, 2 * q + t, c * P:(c + 1) * P], k.ident[:])
        ins.then_inc(pair_ps, 1)


def transpose_xn_scalar(k, act, ps, pair_ps, pair_sb):
    for q in range(NT // 2):
        act.wait_ge(pair_ps, q + 1)
        k.nc.scalar.activation(k.xnT[:, :, q * 2 * P:(q + 1) * 2 * P],
                               ps[:, q % 2, :].rearrange("p (c t) -> p c t", c=KC), ACT.Copy).then_inc(pair_sb, 1)


def phase_load(k, I):
    nc = k.nc
    RING = 4
    with ExitStack() as ctx:
        adj_rows = ctx.enter_context(nc.sbuf_tensor("adj_rows", [P, RING, N], F32))
        vec_rows = ctx.enter_context(nc.sbuf_tensor("vec_rows", [VEC_ROWS, P], F32))
        b1_rows = ctx.enter_context(nc.sbuf_tensor("b1_rows", [E * FT, 2, P], F32))
        zero_rows = ctx.enter_context(nc.sbuf_tensor("zero_rows", [P, BT, D], F32))
        b1_cols = ctx.enter_context(nc.sbuf_tensor("b1_cols", [P, 2, E * FT], F32))
        ps_adj = ctx.enter_context(nc.psum_tensor("ps_adj", [P, 4, 512], F32))
        ps_xn = ctx.enter_context(nc.psum_tensor("ps_xn_a", [P, 2, 512], F32))
        ps_vec = ctx.enter_context(nc.psum_tensor("ps_vec", [P, 512], F32))
        x_in = [k.sem(f"x_in{q}") for q in range(4)]
        small_in, rows_in = k.sem("small_in"), k.sem("rows_in")
        adj_in = [k.sem(f"adj_in{u}") for u in range(RING)]
        consts, adj_ps, adj_sb_act, adj_sb_dve = k.sem("consts"), k.sem("adj_ps"), k.sem("adj_sb_act"), k.sem("adj_sb_dve")
        vec_ps, vec_sb, b1_sb, b1_out = k.sem("vec_ps"), k.sem("vec_sb"), k.sem("b1_sb"), k.sem("b1_out")
        dve_done, var_ready, std_ready = k.sem("dve_done_a"), k.sem("var_a"), k.sem("std_a")
        tile_ready, pair_ps, pair_sb = k.sem("tile_a"), k.sem("pair_ps_a"), k.sem("pair_sb_a")
        zeros_ready, zero_out = k.sem("zeros_ready"), k.sem("zero_out")
        GR = NT // 4

        rows = [("L0_gnn_Wa", 0, 4), ("L0_gnn_Wb", 4, 4)] + [(n, VEC_COL[n], KC) for n in VEC_NAMES]
        small = [
            (k.w_cat[:, :, 0:D], I["L0_gnn_W_sa"].rearrange("(c p) n -> p c n", p=P)),
            (k.w_cat[:, :, D:2 * D], I["L0_gnn_W_gcnb"].rearrange("(c p) n -> p c n", p=P)),
            (k.a_sa[:], I["L0_gnn_a_sa"].to_broadcast([P, 2 * D])),
            (k.b_gcnb[:], I["L0_gnn_b_gcnb"].rearrange("(o n) -> o n", o=1).to_broadcast([P, D])),
            (k.type_bias[:, 0:1], I["L0_gnn_ba"].rearrange("(o n) -> o n", o=1).to_broadcast([P, 1])),
            (k.type_bias[:, 1:2], I["L0_gnn_bb"].rearrange("(o n) -> o n", o=1).to_broadcast([P, 1])),
            (k.gate_w[:, 0], I["L0_ffn_gate_w"].rearrange("(c p) e -> p c e", p=P)),
            (k.gate_w[:, 1], I["L1_ffn_Wg"].rearrange("(c p) e -> p c e", p=P)),
            (k.gate_b[:, 0], I["L0_ffn_gate_b"].rearrange("(o e) -> o e", o=1).to_broadcast([P, E])),
            (k.gate_b[:, 1], I["L1_ffn_bg"].rearrange("(o e) -> o e", o=1).to_broadcast([P, E])),
        ]
        xv = I["x"].rearrange("(n p) d -> p n d", p=P)

        with nc.Block() as block:
            @block.sync
            def _(sp):
                for q in range(4):
                    sp.dma_start(k.x[:, 4 * q:4 * q + 4, :], xv[:, 4 * q:4 * q + 4, :]).then_inc(x_in[q], 16)

                def load(i, u, first):
                    if not first:
                        sp.wait_ge(adj_ps, (i - RING + 1) * GR)
                    sp.dma_start(adj_rows[:, u, :], I["adj"][ds(i * P, P), :]).then_inc(adj_in[u], 16)
                for u in range(RING):
                    load(u, u, True)
                with sp.Fori(1, NT // RING) as g:
                    for u in range(RING):
                        load(g * RING + u, u, False)
                sp.wait_ge(b1_sb, 2)
                sp.dma_start(k.b1_dram, b1_cols[:]).then_inc(b1_out, 16)
                sp.wait_ge(b1_out, 16)

            @block.gpsimd
            def _(pool):
                g = nc.gpsimd
                g.memset(k.ident[:], 0.0).then_inc(consts, 1)
                g.memset(k.ones[:], 1.0).then_inc(consts, 1)
                pool.wait_ge(consts, 2)
                g.affine_select(out=k.ident[:], in_=k.ident[:], compare_op=ALU.not_equal, fill=1.0, base=0,
                                pattern=[[-1, P]], channel_multiplier=1).then_inc(consts, 1)
                g.affine_select(out=k.before[:], in_=k.ones[:], compare_op=ALU.is_gt, fill=0.0, base=0,
                                pattern=[[1, P]], channel_multiplier=-1).then_inc(consts, 1)
                g.iota(k.iota_i[:], pattern=[[1, 32]], base=0, channel_multiplier=0).then_inc(consts, 1)
                pool.wait_ge(consts, 5)
                g.tensor_copy(k.iota[:], k.iota_i[:]).then_inc(consts, 1)
                g.memset(zero_rows[:], 0.0).then_inc(zeros_ready, 1)
                pool.wait_ge(zeros_ready, 1)
                for b in range(NB):
                    pool.dma_start(k.slots_in[b * BLK:(b + 1) * BLK, :].rearrange("(s p) d -> p s d", p=P),
                                   zero_rows[:]).then_inc(zero_out, 16)
                pool.wait_ge(zero_out, 16 * NB)

            @block.scalar
            def _(act):
                for name, row, count in rows:
                    src = rows_of(I, name, count)
                    act.dma_start(vec_rows[row:row + count, :], src).then_inc(rows_in, 16)
                act.dma_start(b1_rows[:, 0, :], I["L0_ffn_b1"].rearrange("e (m p) -> (e m) p", p=P)).then_inc(rows_in, 16)
                act.dma_start(b1_rows[:, 1, :], I["L1_ffn_b1"].rearrange("e (m p) -> (e m) p", p=P)).then_inc(rows_in, 16)
                for dst, src in small:
                    act.dma_start(dst, src).then_inc(small_in, 16)
                layer_norm_sqrt(k, act, var_ready, std_ready)
                transpose_xn_scalar(k, act, ps_xn, pair_ps, pair_sb)
                act.wait_ge(vec_ps, 1)
                nc.scalar.activation(k.vec[:], ps_vec[:, 0:VEC_ROWS], ACT.Copy).then_inc(vec_sb, 1)
                for l in range(2):
                    nc.scalar.activation(b1_cols[:, l, :], ps_vec[:, 128 + 64 * l:192 + 64 * l], ACT.Copy).then_inc(b1_sb, 1)

                def evac(i, u):
                    for g in (0, 2):
                        act.wait_ge(vec_sb, 1)
                        act.wait_ge(adj_ps, i * GR + g + 1)
                        nc.scalar.activation(k.adjT[:, 4 * g:4 * g + 4, ds(i * P, P)],
                                             ps_adj[:, g, :].rearrange("p (j t) -> p j t", j=4), ACT.Copy).then_inc(adj_sb_act, 1)
                with act.Fori(0, NT) as i:
                    evac(i, 0)
                act.wait_ge(small_in, 16 * len(small))

            @block.tensor
            def _(pe):
                pe.wait_ge(consts, 3)
                transpose_xn_tensor(k, pe, ps_xn, tile_ready, pair_ps, pair_sb)
                pe.wait_ge(rows_in, 16 * (len(rows) + 2))
                nc.tensor.transpose(ps_vec[:, 0:VEC_ROWS], vec_rows[:], k.ident[0:VEC_ROWS, 0:VEC_ROWS])
                nc.tensor.transpose(ps_vec[:, 128:192], b1_rows[:, 0, :], k.ident[0:64, 0:64])
                nc.tensor.transpose(ps_vec[:, 192:256], b1_rows[:, 1, :], k.ident[0:64, 0:64]).then_inc(vec_ps, 1)

                def turn(i, u, loads, first):
                    pe.wait_ge(adj_in[u], 16 * loads)
                    for g in range(GR):
                        if not first:
                            pe.wait_ge(adj_sb_act if g % 2 == 0 else adj_sb_dve, 2 * (i - 1) + g // 2 + 1)
                        for j in range(4):
                            ins = nc.tensor.transpose(ps_adj[:, g, j * P:(j + 1) * P],
                                                      adj_rows[:, u, (4 * g + j) * P:(4 * g + j + 1) * P], k.ident[:])
                        ins.then_inc(adj_ps, 1)
                for u in range(RING):
                    turn(u, u, 1, u == 0)
                with pe.Fori(1, NT // RING) as g4:
                    for u in range(RING):
                        turn(g4 * RING + u, u, g4 + 1, False)

            @block.vector
            def _(dve):
                chain = Chain(dve, dve_done)
                layer_norm_vector(k, dve, chain, var_ready, std_ready, tile_ready, x_in)

                with dve.Fori(0, NT) as i:
                    for g in (1, 3):
                        dve.wait_ge(adj_ps, i * GR + g + 1)
                        nc.vector.tensor_copy(k.adjT[:, 4 * g:4 * g + 4, ds(i * P, P)],
                                              ps_adj[:, g, :].rearrange("p (j t) -> p j t", j=4)).then_inc(adj_sb_dve, 1)


def rows_of(I, name, count):
    src = I[name]
    if len(src.shape) == 2:
        return src.rearrange("o (r p) -> (o r) p", p=P)
    return src.rearrange("(r p) -> r p", p=P)


def phase_gnn0(k, I):
    nc = k.nc
    HALF = NT // 2
    HW_ = HALF * P
    W = D + 2
    RING = 4
    with ExitStack() as ctx:
        def sb(name, shape, dt=F32):
            return ctx.enter_context(nc.sbuf_tensor(name, shape, dt))
        hA = sb("hA", [P, NT, D + 1])
        conv = sb("conv", [P, 4, W])
        conv_part = sb("conv_part", [P, 3, NT, W], BF16)
        rest = sb("conv_rest", [P, 4, W])
        own = sb("own", [P, NT, 2])
        s_right = sb("s_right", [P, NT])
        s_left = sb("s_left", [P, N])
        vec6 = sb("vec6", [P, KC, 6])
        left_w = sb("left_w", [P, KC, P])
        junk = sb("junk", [P, D])
        left_col = sb("left_col", [P, KC])
        zbuf = k.xnT[:, :, 0:HW_]
        b = k.xn[:, 0:HALF, :]
        a = k.xn[:, HALF:HALF + 2, :]
        ebuf = sb("ebuf", [P, RING, HW_])
        gate = sb("gate", [P, HALF, 2])
        inv = sb("inv", [P, HALF])
        dve_done, act_done = k.sem("dve_done_b"), k.sem("act_done_b")
        vec_ready, proj_ps, proj_sb = k.sem("vec_ready"), k.sem("proj_ps"), k.sem("proj_sb")
        left_ps, left_sb = k.sem("left_ps"), k.sem("left_sb")
        z_ready, leaky_ready, exp_ready = k.sem("z_ready"), k.sem("leaky_ready"), k.sem("exp_ready")
        edge_ready, edge_used = k.sem("edge_ready"), k.sem("edge_used")
        conv_ps, conv_sb, att_sb = k.sem("conv_ps"), k.sem("conv_sb"), k.sem("att_sb")
        type_ready, gate_ready = k.sem("type_ready"), k.sem("gate_ready")
        mix_ready, sig_ready, half_done, half_chain = k.sem("mix_ready"), k.sem("sig_ready"), k.sem("half_done"), k.sem("half_chain")

        with ExitStack() as pctx, nc.Block() as block:
            ps_h = pctx.enter_context(nc.psum_tensor("ps_h", [P, 2, 512], F32))
            ps_s = pctx.enter_context(nc.psum_tensor("ps_s", [P, 2, 512], F32))
            ps_left = pctx.enter_context(nc.psum_tensor("ps_left", [P, 4, 512], F32))

            @block.vector
            def _(dve):
                v = nc.vector
                chain = Chain(dve, dve_done)
                for c in range(KC):
                    chain.did(v.tensor_tensor_reduce(out=junk[:], in0=k.w_cat[:, c, 0:D], in1=k.a_sa[:, 0:D], scale=1.0,
                                                     scalar=0.0, op0=ALU.mult, op1=ALU.add, accum_out=left_col[:, c:c + 1]))
                    chain.settle()
                    chain.link(v.tensor_tensor_reduce(out=junk[:], in0=k.w_cat[:, c, 0:D], in1=k.a_sa[:, D:2 * D], scale=1.0,
                                                      scalar=0.0, op0=ALU.mult, op1=ALU.add, accum_out=vec6[:, c, 0:1]))
                for c in range(KC):
                    chain.did(v.tensor_copy(vec6[:, c, 1:2], k.vec[:, c:c + 1]))
                    chain.did(v.tensor_copy(vec6[:, c, 2:3], k.vec[:, 4 + c:5 + c]))
                    chain.did(v.tensor_copy(vec6[:, c, 3:4], k.vec[:, 2 + c:3 + c]))
                    chain.did(v.tensor_copy(vec6[:, c, 4:5], k.vec[:, 6 + c:7 + c]))
                    chain.did(v.tensor_scalar(left_w[:, c, :], k.ones[:], left_col[:, c:c + 1], None, ALU.mult))
                chain.did(v.memset(vec6[:, :, 5:6], 0.0))
                chain.settle()
                v.memset(hA[:, :, D:D + 1], 1.0).then_inc(vec_ready, 1)
                for n in range(NT):
                    dve.wait_ge(proj_ps, n + 1)
                    chain.did(v.tensor_copy(conv[:, n % 4, 0:D], ps_h[:, n % 2, D:2 * D]))
                    chain.did(v.tensor_copy(s_right[:, n:n + 1], ps_s[:, n % 2, 0:1]))
                    chain.did(v.tensor_copy(conv[:, n % 4, D:W], ps_s[:, n % 2, 1:3]))
                    chain.did(v.tensor_copy(hA[:, n, 0:D], ps_h[:, n % 2, 0:D]))
                    v.tensor_copy(own[:, n, :], ps_s[:, n % 2, 3:5]).then_inc(proj_sb, 1)
                    if n % 4 == 3:
                        four = slice(n - 3, n + 1)
                        chain.settle()
                        chain.link(v.tensor_copy(conv_part[:, 0, four], conv[:]))
                        chain.link(v.tensor_tensor(rest[:], conv[:], conv_part[:, 0, four], ALU.subtract))
                        chain.link(v.tensor_copy(conv_part[:, 1, four], rest[:]))
                        chain.link(v.tensor_tensor(rest[:], rest[:], conv_part[:, 1, four], ALU.subtract))
                        chain.link(v.tensor_copy(conv_part[:, 2, four], rest[:]))

            @block.tensor
            def _(pe):
                pe.wait_ge(vec_ready, 1)
                for n in range(NT):
                    if n >= 2:
                        pe.wait_ge(proj_sb, n - 1)
                    for c in range(KC):
                        nc.tensor.matmul(ps_h[:, n % 2, :], k.xnT[:, c, n * P:(n + 1) * P], k.w_cat[:, c, :],
                                         start=(c == 0), stop=(c == KC - 1))
                    for c in range(KC):
                        ins = nc.tensor.matmul(ps_s[:, n % 2, 0:6], k.xnT[:, c, n * P:(n + 1) * P], vec6[:, c, :],
                                               start=(c == 0), stop=(c == KC - 1))
                    ins.then_inc(proj_ps, 1)
                for q in range(4):
                    for c in range(KC):
                        ins = nc.tensor.matmul(ps_left[:, q, :], left_w[:, c, :], k.xnT[:, c, q * 512:(q + 1) * 512],
                                               start=(c == 0), stop=(c == KC - 1))
                    ins.then_inc(left_ps, 1)

            @block.scalar
            def _(act):
                for q in range(4):
                    act.wait_ge(left_ps, q + 1)
                    nc.scalar.activation(s_left[:, q * 512:(q + 1) * 512], ps_left[:, q, :], ACT.Copy).then_inc(left_sb, 1)

        with ExitStack() as pctx, nc.Block() as block:
            ps = pctx.enter_context(nc.psum_tensor("ps_half", [P, HALF, 512], F32))

            @block.tensor
            def _(pe):
                with pe.Fori(0, 2) as half:
                    for j in range(NT):
                        for i in range(HALF):
                            for part in range(3):
                                ins = nc.tensor.matmul(ps[:, i, 0:W], k.adjT[:, j, ds(half * HW_ + i * P, P)],
                                                       conv_part[:, part, j, :], start=(j == 0 and part == 0),
                                                       stop=(j == NT - 1 and part == 2))
                            if j == NT - 1:
                                ins.then_inc(conv_ps, 1)
                    for j in range(NT):
                        pe.wait_ge(edge_ready, half * NT + j + 1)
                        for i in range(HALF):
                            if j == 0:
                                pe.wait_ge(conv_sb, half * HALF + i + 1)
                            ins = nc.tensor.matmul(ps[:, i, 0:D + 1], ebuf[:, j % RING, i * P:(i + 1) * P], hA[:, j, :],
                                                   start=(j == 0), stop=(j == NT - 1))
                        ins.then_inc(edge_used, 1)
                    pe.wait_ge(att_sb, (half + 1) * HALF)

            @block.scalar
            def _(act):
                with act.Fori(0, 2) as half:
                    def z_of(j):
                        act.wait_ge(left_sb, 4)
                        if j >= 2:
                            act.wait_ge(leaky_ready, half * NT + j - 1)
                        nc.scalar.activation(zbuf[:, j % 2, :], s_left[:, ds(half * HW_, HW_)], ACT.Identity,
                                             bias=s_right[:, j:j + 1]).then_inc(z_ready, 1)

                    def exp_of(j):
                        act.wait_ge(leaky_ready, half * NT + j + 1)
                        nc.scalar.activation(ebuf[:, j % RING, :], ebuf[:, j % RING, :], ACT.Exp, scale=-1.0).then_inc(exp_ready, 1)

                    z_of(0)
                    for j in range(NT):
                        if j + 1 < NT:
                            z_of(j + 1)
                        exp_of(j)
                        if j == 1:
                            act.wait_ge(type_ready, half + 1)
                            nc.scalar.activation(gate[:], gate[:], ACT.Tanh, scale=0.5).then_inc(gate_ready, 1)
                    for i in range(HALF):
                        act.wait_ge(mix_ready, half * HALF + i + 1)
                        nc.scalar.activation(a[:, i % 2, :], a[:, i % 2, :], ACT.Tanh, scale=0.5).then_inc(sig_ready, 1)

            @block.vector
            def _(dve):
                v = nc.vector
                with dve.Fori(0, 2) as half:
                    def leaky(j):
                        dve.wait_ge(z_ready, half * NT + j + 1)
                        if j >= RING:
                            dve.wait_ge(edge_used, half * NT + j - RING + 1)
                        v.scalar_tensor_tensor(out=ebuf[:, j % RING, :], in0=zbuf[:, j % 2, :], scalar=0.01,
                                               in1=zbuf[:, j % 2, :], op0=ALU.mult, op1=ALU.max).then_inc(leaky_ready, 1)

                    def mask(j):
                        dve.wait_ge(exp_ready, half * NT + j + 1)
                        v.tensor_tensor(ebuf[:, j % RING, :], ebuf[:, j % RING, :], k.adjT[:, j, ds(half * HW_, HW_)],
                                        ALU.mult).then_inc(edge_ready, 1)

                    def conv_out():
                        for i in range(HALF):
                            dve.wait_ge(conv_ps, half * HALF + i + 1)
                            v.tensor_tensor(b[:, i, :], ps[:, i, 0:D], k.b_gcnb[:], ALU.add)
                            v.tensor_tensor(gate[:, i, :], ps[:, i, D:W], own[:, ds(half * HALF + i, 1), :].rearrange("p o w -> p (o w)"),
                                            ALU.add).then_inc(conv_sb, 1)
                        dve.wait_ge(conv_sb, (half + 1) * HALF)
                        v.tensor_tensor(gate[:], gate[:], k.type_bias[:].rearrange("p (o w) -> p o w", o=1).to_broadcast([P, HALF, 2]),
                                        ALU.add).then_inc(type_ready, 1)

                    leaky(0)
                    for j in range(NT):
                        if j == 1:
                            conv_out()
                        if j + 1 < NT:
                            leaky(j + 1)
                        mask(j)
                    dve.wait_ge(gate_ready, half + 1)
                    v.tensor_scalar(gate[:], gate[:], 0.5, 0.5, ALU.mult, ALU.add).then_inc(half_chain, 1)
                    dve.wait_ge(edge_used, (half + 1) * NT)
                    v.tensor_scalar(inv[:], ps[:, :, D:D + 1].rearrange("p i o -> p (i o)"), 1e-5, None, ALU.add).then_inc(half_chain, 1)
                    dve.wait_ge(half_chain, half * 4 + 2)
                    v.reciprocal(inv[:], inv[:]).then_inc(half_chain, 1)
                    dve.wait_ge(half_chain, half * 4 + 3)
                    v.tensor_tensor(inv[:], inv[:], gate[:, :, 0], ALU.mult).then_inc(half_chain, 1)
                    dve.wait_ge(half_chain, half * 4 + 4)

                    def mix(i):
                        if i >= 2:
                            dve.wait_ge(half_done, half * HALF * 2 + (i - 1) * 2)
                        v.tensor_scalar(a[:, i % 2, :], ps[:, i, 0:D], inv[:, i:i + 1], None, ALU.mult).then_inc(att_sb, 1)
                        dve.wait_ge(att_sb, half * HALF + i + 1)
                        v.scalar_tensor_tensor(out=a[:, i % 2, :], in0=b[:, i, :], scalar=gate[:, i, 1:2], in1=a[:, i % 2, :],
                                               op0=ALU.mult, op1=ALU.add).then_inc(mix_ready, 1)

                    def residual(i):
                        row = k.x[:, ds(half * HALF + i, 1), :].rearrange("p o d -> p (o d)")
                        dve.wait_ge(sig_ready, half * HALF + i + 1)
                        v.scalar_tensor_tensor(out=row, in0=a[:, i % 2, :], scalar=0.5, in1=row, op0=ALU.mult, op1=ALU.add).then_inc(half_done, 1)
                        dve.wait_ge(half_done, half * HALF * 2 + i * 2 + 1)
                        v.tensor_scalar(row, row, 0.5, None, ALU.add).then_inc(half_done, 1)

                    mix(0)
                    for i in range(HALF):
                        if i + 1 < HALF:
                            mix(i + 1)
                        residual(i)


def block_norm(k, name):
    nc = k.nc
    with ExitStack() as ctx, nc.Block() as block:
        ps_xn = ctx.enter_context(nc.psum_tensor("ps_xn_" + name, [P, 2, 512], F32))
        dve_done, var_ready, std_ready = k.sem("dve_done_" + name), k.sem("var_" + name), k.sem("std_" + name)
        tile_ready, pair_ps, pair_sb = k.sem("tile_" + name), k.sem("pair_ps_" + name), k.sem("pair_sb_" + name)

        @block.vector
        def _(dve):
            layer_norm_vector(k, dve, Chain(dve, dve_done), var_ready, std_ready, tile_ready)

        @block.scalar
        def _(act):
            layer_norm_sqrt(k, act, var_ready, std_ready)
            transpose_xn_scalar(k, act, ps_xn, pair_ps, pair_sb)

        @block.tensor
        def _(pe):
            transpose_xn_tensor(k, pe, ps_xn, tile_ready, pair_ps, pair_sb)


def phase_route(k, layer):
    nc = k.nc
    name = f"r{layer}"
    with ExitStack() as ctx:
        def sb(nm, shape, dt=F32):
            return ctx.enter_context(nc.sbuf_tensor(f"{nm}_{name}", shape, dt))
        prob = sb("prob", [P, NT, E])
        stat = sb("stat", [P, NT])
        top = sb("top", [P, NT, E])
        top_i = sb("top_i", [P, NT, E], U32)
        pick = sb("pick", [P, NT, TOP])
        hot = sb("hot", [P, TOP, NT, E])
        both = sb("both", [P, NT, E])
        ahead = sb("ahead", [P, 2, NT, E])
        total = sb("total", [P, NT, E])
        blocks = sb("blocks", [P, E])
        ends = sb("ends", [P, 2, E])
        cmp8 = sb("cmp8", [P, E, E])
        cmpb = sb("cmpb", [P, NB, E])
        slot_f = sb("slot_f", [P, TOP, NT])
        expert_f = sb("expert_f", [P, NB])
        ps_l = ctx.enter_context(nc.psum_tensor("ps_l" + name, [P, 512], F32))
        ps_c = ctx.enter_context(nc.psum_tensor("ps_c" + name, [P, 2, 512], F32))
        logit_ps, shifted, exped = k.sem("logit_ps_" + name), k.sem("shifted_" + name), k.sem("exped_" + name)
        hot_ready, count_ps, diff_ready, diff_exp = (k.sem(s + name) for s in ("hot_", "count_ps_", "diff_", "diff_exp_"))
        dve_done, slots_ready, scattered = k.sem("dve_done_" + name), k.sem("slots_" + name), k.sem("scattered_" + name)
        flat = lambda t: t.rearrange("p n e -> p (n e)")
        with nc.Block() as block:
            @block.tensor
            def _(pe):
                for n in range(NT):
                    for c in range(KC):
                        ins = nc.tensor.matmul(ps_l[:, n * E:(n + 1) * E], k.xnT[:, c, n * P:(n + 1) * P],
                                               k.gate_w[:, layer, c, :], start=(c == 0), stop=(c == KC - 1))
                ins.then_inc(logit_ps, 1)
                pe.wait_ge(hot_ready, 1)
                nc.tensor.matmul(ps_c[:, 0, 0:NT * E], k.before[:], flat(both[:]), start=True, stop=True)
                nc.tensor.matmul(ps_c[:, 1, 0:NT * E], k.ones[:], flat(both[:]), start=True, stop=True).then_inc(count_ps, 1)

            @block.scalar
            def _(act):
                act.wait_ge(shifted, 1)
                nc.scalar.activation(flat(prob[:]), flat(prob[:]), ACT.Exp).then_inc(exped, 1)
                if layer == 0:
                    act.wait_ge(diff_ready, 1)
                    nc.scalar.activation(k.pair_w[:, :, 1], k.pair_w[:, :, 1], ACT.Exp).then_inc(diff_exp, 1)

            @block.vector
            def _(dve):
                v = nc.vector
                chain = Chain(dve, dve_done)
                link = chain.link
                dve.wait_ge(logit_ps, 1)
                over_e = lambda t: t.rearrange("p (n o) -> p n o", o=1).to_broadcast([P, NT, E])
                link(v.tensor_tensor(prob[:], ps_l[:, 0:NT * E].rearrange("p (n e) -> p n e", e=E),
                                     k.gate_b[:, layer, :].rearrange("p (o e) -> p o e", o=1).to_broadcast([P, NT, E]), ALU.add))
                link(v.tensor_reduce(stat[:], prob[:], AX_X, ALU.max))
                v.tensor_tensor(prob[:], prob[:], over_e(stat[:]), ALU.subtract).then_inc(shifted, 1)
                dve.wait_ge(exped, 1)
                link(v.tensor_reduce(stat[:], prob[:], AX_X, ALU.add))
                link(v.reciprocal(stat[:], stat[:]))
                link(v.tensor_tensor(prob[:], prob[:], over_e(stat[:]), ALU.mult))
                for n in range(NT):
                    chain.did(v.max(top[:, n, :], prob[:, n, :]))
                chain.settle()
                for n in range(NT):
                    chain.did(v.max_index(top_i[:, n, :], top[:, n, :], prob[:, n, :]))
                chain.settle()
                link(v.tensor_copy(pick[:], top_i[:, :, 0:TOP]))
                for c in range(TOP):
                    chain.did(v.tensor_tensor(hot[:, c], pick[:, :, c:c + 1].to_broadcast([P, NT, E]),
                                              k.iota[:, 0:E].rearrange("p (o e) -> p o e", o=1).to_broadcast([P, NT, E]), ALU.is_equal))
                chain.settle()
                v.tensor_tensor(both[:], hot[:, 0], hot[:, 1], ALU.add).then_inc(hot_ready, 1)
                if layer == 0:
                    v.tensor_tensor(k.pair_w[:, :, 1], top[:, :, 1], top[:, :, 0], ALU.subtract).then_inc(diff_ready, 1)
                    dve.wait_ge(diff_exp, 1)
                    link(v.tensor_scalar(stat[:], k.pair_w[:, :, 1], 1.0, None, ALU.add))
                    link(v.reciprocal(k.pair_w[:, :, 0], stat[:]))
                    link(v.tensor_tensor(k.pair_w[:, :, 1], k.pair_w[:, :, 1], k.pair_w[:, :, 0], ALU.mult))
                else:
                    link(v.tensor_tensor(stat[:], top[:, :, 0], top[:, :, 1], ALU.add))
                    link(v.reciprocal(stat[:], stat[:]))
                    for c in range(TOP):
                        chain.did(v.tensor_tensor(k.pair_w[:, :, c], top[:, :, c], stat[:], ALU.mult))
                dve.wait_ge(count_ps, 1)
                chain.did(v.tensor_copy(total[:], ps_c[:, 1, 0:NT * E].rearrange("p (n e) -> p n e", e=E)))
                link(v.tensor_copy(ahead[:, 0], ps_c[:, 1, 0:NT * E].rearrange("p (n e) -> p n e", e=E)))
                side = 0
                for sh in (1, 2, 4, 8):
                    chain.did(v.tensor_copy(ahead[:, 1 - side, 0:sh], ahead[:, side, 0:sh]))
                    link(v.tensor_tensor(ahead[:, 1 - side, sh:NT], ahead[:, side, sh:NT], ahead[:, side, 0:NT - sh], ALU.add))
                    side = 1 - side
                link(v.tensor_scalar(expert_f[:, 0:E], k.iota[:, 0:E], float(BLK), None, ALU.mult))
                link(v.tensor_tensor(cmp8[:], ahead[:, side, NT - 1, :].rearrange("p (e o) -> p e o", o=1).to_broadcast([P, E, E]),
                                     expert_f[:, 0:E].rearrange("p (o b) -> p o b", o=1).to_broadcast([P, E, E]), ALU.is_gt))
                link(v.tensor_reduce(blocks[:], cmp8[:], AX_X, ALU.add))
                link(v.tensor_copy(ends[:, 0], blocks[:]))
                es = 0
                for sh in (1, 2, 4):
                    chain.did(v.tensor_copy(ends[:, 1 - es, 0:sh], ends[:, es, 0:sh]))
                    link(v.tensor_tensor(ends[:, 1 - es, sh:E], ends[:, es, sh:E], ends[:, es, 0:E - sh], ALU.add))
                    es = 1 - es
                link(v.tensor_tensor(blocks[:], ends[:, es], blocks[:], ALU.subtract))
                link(v.tensor_scalar(blocks[:], blocks[:], float(BLK), None, ALU.mult))
                link(v.tensor_tensor(total[:], ahead[:, side], total[:], ALU.subtract))
                link(v.tensor_tensor(total[:], total[:], blocks[:].rearrange("p (o e) -> p o e", o=1).to_broadcast([P, NT, E]), ALU.add))
                link(v.tensor_tensor(total[:], total[:], ps_c[:, 0, 0:NT * E].rearrange("p (n e) -> p n e", e=E), ALU.add))
                for c in range(TOP):
                    link(v.tensor_tensor(hot[:, c], hot[:, c], total[:], ALU.mult))
                    link(v.tensor_reduce(slot_f[:, c, :], hot[:, c], AX_X, ALU.add))
                v.tensor_copy(k.slot[:], slot_f[:]).then_inc(slots_ready, 1)
                link(v.tensor_tensor(cmpb[:], k.iota[:, 0:NB].rearrange("p (b o) -> p b o", o=1).to_broadcast([P, NB, E]),
                                     ends[:, es].rearrange("p (o e) -> p o e", o=1).to_broadcast([P, NB, E]), ALU.is_ge))
                link(v.tensor_reduce(expert_f[:], cmpb[:], AX_X, ALU.add))
                link(v.tensor_scalar(expert_f[:], expert_f[:], float(E - 1), None, ALU.min))
                link(v.tensor_copy(k.expert[:], expert_f[:]))

            @block.gpsimd
            def _(pool):
                pool.wait_ge(slots_ready, 1)
                for n in range(NT):
                    for c in range(TOP):
                        pool.indirect_dma_start(out=k.slots_in, out_offset=bass.IndirectOffsetOnAxis(ap=k.slot[:, c, n:n + 1], axis=0),
                                                in_=k.xn[:, n, :], in_offset=None).then_inc(scattered, 16)
                pool.wait_ge(scattered, 16 * TOP * NT)


def split_products(nc, out, w_parts, x_parts, start, stop):
    (w_hi, w_lo), (x_hi, x_lo) = w_parts, x_parts
    nc.tensor.matmul(out, w_hi, x_hi, start=start, stop=False)
    nc.tensor.matmul(out, w_hi, x_lo, start=False, stop=False)
    return nc.tensor.matmul(out, w_lo, x_hi, start=False, stop=stop)


def phase_experts(k, layer, w1, w2, b2):
    nc = k.nc
    name = f"x{layer}"
    HC = FT // 2
    PAIRS = FT // 2
    with ExitStack() as ctx:
        def sb(nm, shape, dt=F32):
            return ctx.enter_context(nc.sbuf_tensor(f"{nm}_{name}", shape, dt))
        w1_sb = k.xn[:].rearrange("p (u c m) d -> p u c (m d)", u=2, c=KC)
        w2_sb = k.xnT[:].rearrange("p u (m d) -> p u m d", d=D)
        w1_hi, w1_lo = sb("w1_hi", [P, KC, F], F32R), sb("w1_lo", [P, KC, F], F32R)
        w2_hi, w2_lo = sb("w2_hi", [P, FT, D], F32R), sb("w2_lo", [P, FT, D], F32R)
        b1_sb = sb("b1", [P, 2, FT])
        b2_sb = sb("b2", [P, 2, D])
        rows = sb("rows", [P, 2, BT, D])
        rows_hi, rows_lo = sb("rows_hi", [P, 2, KC, BLK], F32R), sb("rows_lo", [P, 2, KC, BLK], F32R)
        hid = sb("hid", [P, FT, BLK])
        hid_hi, hid_lo = sb("hid_hi", [P, FT, BLK], F32R), sb("hid_lo", [P, FT, BLK], F32R)
        res = sb("res", [P, 2, BT, D])
        ps_t = ctx.enter_context(nc.psum_tensor("ps_t" + name, [P, 512], F32))
        ps_h = ctx.enter_context(nc.psum_tensor("ps_h" + name, [P, FT, BLK], F32))
        ps_y = ctx.enter_context(nc.psum_tensor("ps_y" + name, [P, BT, 512], F32))
        rows_in = [k.sem(f"rows_in{u}_{name}") for u in range(2)]
        w1_in = [k.sem(f"w1_in{u}_{name}") for u in range(2)]
        w2_in = [k.sem(f"w2_in{u}_{name}") for u in range(2)]
        res_out = [k.sem(f"res_out{u}_{name}") for u in range(2)]
        turned, rows_high, rows_split = (k.sem(s + name) for s in ("turned_", "rows_high_", "rows_split_"))
        w1_high, w1_split, w2_high, w2_split = (k.sem(s + name) for s in ("w1_high_", "w1_split_", "w2_high_", "w2_split_"))
        hid_ps, hid_full, hid_high, hid_split = (k.sem(s + name) for s in ("hid_ps_", "hid_full_", "hid_high_", "hid_split_"))
        y_ps, y_sb = k.sem("y_ps_" + name), k.sem("y_sb_" + name)

        def run(step, eng):
            step(0, 0, 0, False, False)
            step(1, 1, 0, True, False)
            with eng.Fori(1, NB // 2) as g:
                step(g * 2, 0, g, True, True)
                step(g * 2 + 1, 1, g, True, True)
            if NB % 2:
                step(NB - 1, 0, NB // 2, True, True)

        with nc.Block() as block:
            @block.sync
            def _(sp):
                def step(b, u, past, one, two):
                    if two:
                        sp.wait_ge(turned, b - 1)
                    sp.dma_start(rows[:, u], k.slots_in[ds(b * BLK, BLK), :].rearrange("(s p) d -> p s d", p=P)).then_inc(rows_in[u], 16)
                    e = sp.value_load(k.expert[0:1, ds(b, 1)], min_val=0, max_val=E - 1)
                    if two:
                        sp.wait_ge(w1_split, (b - 1) * 2)
                    sp.dma_start(w1_sb[:, u], w1[ds(e, 1)].rearrange("o (c p) f -> p (o c) f", p=P)).then_inc(w1_in[u], 16)
                    if two:
                        sp.wait_ge(hid_full, (b - 1) * FT)
                    sp.dma_start(b1_sb[:, u, :], k.b1_dram[:, layer, ds(e * FT, FT)]).then_inc(w1_in[u], 16)
                    if two:
                        sp.wait_ge(w2_split, (b - 1) * 2)
                    sp.dma_start(w2_sb[:, u], w2[ds(e, 1)].rearrange("o (m p) d -> p (o m) d", p=P)).then_inc(w2_in[u], 16)
                    if two:
                        sp.wait_ge(y_sb, (b - 1) * BT)
                    sp.dma_start(b2_sb[:, u, :], b2[ds(e, 1), :].to_broadcast([P, D])).then_inc(w2_in[u], 16)
                run(step, sp)

            @block.tensor
            def _(pe):
                def turn(b, u, past, one):
                    pe.wait_ge(rows_in[u], 16 * (past + 1))
                    if one:
                        pe.wait_ge(rows_split, b)
                    for c in range(KC):
                        for s in range(BT):
                            ins = nc.tensor.transpose(ps_t[:, c * BLK + s * P:c * BLK + (s + 1) * P],
                                                      rows[:, u, s, c * P:(c + 1) * P], k.ident[:])
                    ins.then_inc(turned, 1)

                def products(b, u, past, one, more):
                    pe.wait_ge(rows_split, b + 1)
                    for m in range(FT):
                        if m % HC == 0:
                            pe.wait_ge(w1_split, b * 2 + m // HC + 1)
                        if one and m % 2 == 0:
                            pe.wait_ge(hid_full, (b - 1) * FT + m + 2)
                        part = slice(m * P, (m + 1) * P)
                        for c in range(KC):
                            ins = split_products(nc, ps_h[:, m, :], (w1_hi[:, c, part], w1_lo[:, c, part]),
                                                 (rows_hi[:, u, c, :], rows_lo[:, u, c, :]), c == 0, c == KC - 1)
                        if m % 2 == 1:
                            ins.then_inc(hid_ps, 1)
                    if more:
                        turn(b + 1, 1 - u, past + u, True)
                    for m in range(FT):
                        if m % HC == 0:
                            pe.wait_ge(w2_split, b * 2 + m // HC + 1)
                        if m % 2 == 0:
                            pe.wait_ge(hid_split, b * PAIRS + m // 2 + 1)
                        for s in range(BT):
                            if one and m == 0:
                                pe.wait_ge(y_sb, (b - 1) * BT + s + 1)
                            part = slice(s * P, (s + 1) * P)
                            ins = split_products(nc, ps_y[:, s, 0:D], (hid_hi[:, m, part], hid_lo[:, m, part]),
                                                 (w2_hi[:, m, :], w2_lo[:, m, :]), m == 0, m == FT - 1)
                        if m % HC == HC - 1:
                            ins.then_inc(y_ps, 1)

                turn(0, 0, 0, False)
                products(0, 0, 0, False, True)
                products(1, 1, 0, True, True)
                with pe.Fori(1, NB // 2) as g:
                    products(g * 2, 0, g, True, True)
                    products(g * 2 + 1, 1, g, True, True)
                products(NB - 1, 0, NB // 2, True, False)

            @block.scalar
            def _(act):
                def high_w1(b, u, past, one):
                    act.wait_ge(w1_in[u], 32 * (past + 1))
                    for h in range(2):
                        if one:
                            act.wait_ge(hid_ps, (b - 1) * PAIRS + 2 * h + 2)
                        chunk = slice(h * HC * P, (h + 1) * HC * P)
                        nc.scalar.activation(w1_hi[:, :, chunk], w1_sb[:, u, :, chunk], ACT.Copy).then_inc(w1_high, 1)

                def high_w2(b, u, past, h, one):
                    act.wait_ge(w2_in[u], 32 * (past + 1))
                    if one:
                        act.wait_ge(y_ps, (b - 1) * 2 + h + 1)
                    chunk = slice(h * HC, (h + 1) * HC)
                    nc.scalar.activation(w2_hi[:, chunk, :], w2_sb[:, u, chunk, :], ACT.Copy).then_inc(w2_high, 1)

                def high_rows(b, u, two):
                    act.wait_ge(turned, b + 1)
                    if two:
                        act.wait_ge(hid_ps, (b - 1) * PAIRS)
                    nc.scalar.activation(rows_hi[:, u].rearrange("p c t -> p (c t)"), ps_t[:], ACT.Copy).then_inc(rows_high, 1)

                def step(b, u, past, one, two, more=True):
                    for m in range(FT):
                        if m % 2 == 0:
                            act.wait_ge(hid_ps, b * PAIRS + m // 2 + 1)
                            if one:
                                act.wait_ge(hid_split, (b - 1) * PAIRS + m // 2 + 1)
                        nc.scalar.activation(hid[:, m, :], ps_h[:, m, :], ACT.Relu, bias=b1_sb[:, u, m:m + 1]).then_inc(hid_full, 1)
                        if m == 3:
                            high_w2(b, u, past, 1, one)
                    if more:
                        high_rows(b + 1, 1 - u, one)
                        high_w1(b + 1, 1 - u, past + u, True)
                        high_w2(b + 1, 1 - u, past + u, 0, True)

                high_rows(0, 0, False)
                high_w1(0, 0, 0, False)
                high_w2(0, 0, 0, 0, False)
                step(0, 0, 0, False, False)
                step(1, 1, 0, True, False)
                with act.Fori(1, NB // 2) as g:
                    step(g * 2, 0, g, True, True)
                    step(g * 2 + 1, 1, g, True, True)
                step(NB - 1, 0, NB // 2, True, True, more=False)

            @block.vector
            def _(dve):
                v = nc.vector

                def low_rows(b, u):
                    dve.wait_ge(rows_high, b + 1)
                    hi, lo = (t[:, u].rearrange("p c t -> p (c t)") for t in (rows_hi, rows_lo))
                    v.tensor_tensor(lo, ps_t[:], hi.bitcast(F32), ALU.subtract).then_inc(rows_split, 1)

                def low_w1(b, u, past):
                    for h in range(2):
                        dve.wait_ge(w1_high, b * 2 + h + 1)
                        chunk = slice(h * HC * P, (h + 1) * HC * P)
                        v.tensor_tensor(w1_lo[:, :, chunk], w1_sb[:, u, :, chunk], w1_hi[:, :, chunk].bitcast(F32),
                                        ALU.subtract).then_inc(w1_split, 1)

                def low_w2(b, u, h):
                    dve.wait_ge(w2_high, b * 2 + h + 1)
                    chunk = slice(h * HC, (h + 1) * HC)
                    v.tensor_tensor(w2_lo[:, chunk, :], w2_sb[:, u, chunk, :], w2_hi[:, chunk, :].bitcast(F32),
                                    ALU.subtract).then_inc(w2_split, 1)

                def step(b, u, past, one, two, more=True):
                    for q in range(PAIRS):
                        pair = slice(2 * q, 2 * q + 2)
                        dve.wait_ge(hid_full, b * FT + 2 * q + 2)
                        if one and q == 0:
                            dve.wait_ge(y_ps, b * 2)
                        v.tensor_copy(hid_hi[:, pair, :], hid[:, pair, :]).then_inc(hid_high, 1)
                        dve.wait_ge(hid_high, b * PAIRS + q + 1)
                        v.tensor_tensor(hid_lo[:, pair, :], hid[:, pair, :], hid_hi[:, pair, :].bitcast(F32),
                                        ALU.subtract).then_inc(hid_split, 1)
                        if q == 1:
                            low_w2(b, u, 1)
                    if more:
                        low_rows(b + 1, 1 - u)
                        low_w1(b + 1, 1 - u, past + u)
                        low_w2(b + 1, 1 - u, 0)
                    dve.wait_ge(w2_in[u], 32 * (past + 1))
                    dve.wait_ge(y_ps, b * 2 + 2)
                    if two:
                        dve.wait_ge(res_out[u], 16 * past)
                    for s in range(BT):
                        v.tensor_tensor(res[:, u, s, :], ps_y[:, s, 0:D], b2_sb[:, u, :], ALU.add).then_inc(y_sb, 1)

                low_rows(0, 0)
                low_w1(0, 0, 0)
                low_w2(0, 0, 0)
                step(0, 0, 0, False, False)
                step(1, 1, 0, True, False)
                with dve.Fori(1, NB // 2) as g:
                    step(g * 2, 0, g, True, True)
                    step(g * 2 + 1, 1, g, True, True)
                step(NB - 1, 0, NB // 2, True, True, more=False)

            @block.gpsimd
            def _(pool):
                def step(b, u, past, one, two):
                    pool.wait_ge(y_sb, (b + 1) * BT)
                    pool.dma_start(k.slots_out[ds(b * BLK, BLK), :].rearrange("(s p) d -> p s d", p=P), res[:, u]).then_inc(res_out[u], 16)
                run(step, pool)
                pool.wait_ge(res_out[0], 16 * (NB // 2 + 1))
                pool.wait_ge(res_out[1], 16 * (NB // 2))


def phase_combine(k, layer, out=None):
    nc = k.nc
    name = f"c{layer}"
    RING = 4
    with ExitStack() as ctx, nc.Block() as block:
        got = ctx.enter_context(nc.sbuf_tensor("got_" + name, [P, RING, TOP, D], F32))
        fetched = [k.sem(f"fetched{u}_{name}") for u in range(RING)]
        added, stored = k.sem("added_" + name), k.sem("stored_" + name)

        @block.gpsimd
        def _(pool):
            for n in range(NT):
                if n >= RING:
                    pool.wait_ge(added, TOP * (n - RING + 1))
                for c in range(TOP):
                    pool.indirect_dma_start(out=got[:, n % RING, c, :], out_offset=None, in_=k.slots_out,
                                            in_offset=bass.IndirectOffsetOnAxis(ap=k.slot[:, c, n:n + 1], axis=0)).then_inc(fetched[n % RING], 16)

        @block.vector
        def _(dve):
            for n in range(NT):
                dve.wait_ge(fetched[n % RING], 32 * (n // RING + 1))
                for c in range(TOP):
                    if c:
                        dve.wait_ge(added, TOP * n + c)
                    nc.vector.scalar_tensor_tensor(out=k.x[:, n, :], in0=got[:, n % RING, c, :], scalar=k.pair_w[:, n, c:c + 1],
                                                   in1=k.x[:, n, :], op0=ALU.mult, op1=ALU.add).then_inc(added, 1)

        if out is not None:
            ov = out.rearrange("(n p) d -> p n d", p=P)

            @block.sync
            def _(sp):
                for q in range(4):
                    sp.wait_ge(added, TOP * 4 * (q + 1))
                    sp.dma_start(ov[:, 4 * q:4 * q + 4, :], k.x[:, 4 * q:4 * q + 4, :]).then_inc(stored, 16)
                sp.wait_ge(stored, 64)


def phase_gnn1_project(k, I, g):
    nc = k.nc
    with ExitStack() as ctx, nc.Block() as block:
        def sb(name, shape, dt=F32):
            return ctx.enter_context(nc.sbuf_tensor(name, shape, dt))
        head_w = sb("head_w", [P, KC, DH])
        head_v = sb("head_v", [P, KC, 2, DH])
        score_v = sb("score_v", [P, KC, 2])
        junk = sb("junk1", [P, DH])
        f1w = sb("f1w", [P, H, P])
        own_w = sb("own_w", [P, KC, P + 2])
        mlp_rows = sb("mlp_rows", [P, 2, KC, D])
        ps_w = ctx.enter_context(nc.psum_tensor("ps_w", [P, 2, 512], F32))
        ps_p = ctx.enter_context(nc.psum_tensor("ps_p", [P, 2, 512], F32))
        ps_f = ctx.enter_context(nc.psum_tensor("ps_f", [P, 4, 512], F32))
        w_in, zeroed, dve_done, w_ready = k.sem("w_in_p"), k.sem("zeroed_p"), k.sem("dve_done_p"), k.sem("w_ready_p")
        turned, turned_sb, proj_ps, proj_sb = k.sem("turned_p"), k.sem("turned_sb_p"), k.sem("proj_ps_p"), k.sem("proj_sb_p")
        f1_ps, f1_sb, ones_ready = k.sem("f1_ps"), k.sem("f1_sb"), k.sem("ones_ready_p")
        g.f1_sb = f1_sb
        WIN = 6

        @block.sync
        def _(sp):
            sp.dma_start(head_w[:], I["L1_gnn_W"].rearrange("(c g) d e -> (g d) c e", g=2)).then_inc(w_in, 16)
            for half in range(2):
                sp.dma_start(head_v[half * DH:(half + 1) * DH].rearrange("p c s e -> p c (s e)"),
                             I["L1_gnn_V"].rearrange("(c g) s e o -> g c (s e o)", g=2)[half:half + 1].to_broadcast([DH, KC, 2 * DH])).then_inc(w_in, 16)
            sp.dma_start(mlp_rows[:, 0], I["L1_gnn_enc_mlp_W"].rearrange("(c p) n -> p c n", p=P)).then_inc(w_in, 16)
            sp.dma_start(mlp_rows[:, 1], I["L1_gnn_dec_mlp_W"].rearrange("(c p) n -> p c n", p=P)).then_inc(w_in, 16)

        @block.gpsimd
        def _(pool):
            nc.gpsimd.memset(f1w[:], 0.0).then_inc(zeroed, 1)
            nc.gpsimd.memset(own_w[:], 0.0).then_inc(zeroed, 1)
            nc.gpsimd.memset(g.near[:, :, DH:2 * DH], 1.0).then_inc(ones_ready, 1)
            pool.wait_ge(ones_ready, 1)

        @block.vector
        def _(dve):
            v = nc.vector
            chain = Chain(dve, dve_done)
            dve.wait_ge(w_in, 16 * (WIN - 1))
            dve.wait_ge(zeroed, 2)
            for c in range(KC):
                for s in range(2):
                    chain.link(v.tensor_tensor_reduce(out=junk[:], in0=head_w[:, c, :], in1=head_v[:, c, s, :], scale=1.0, scalar=0.0,
                                                      op0=ALU.mult, op1=ALU.add, accum_out=score_v[:, c, s:s + 1]))
            for c in range(KC):
                for q in range(2):
                    part = slice(q * DH, (q + 1) * DH)
                    chain.did(v.tensor_copy(own_w[part, c, q * DH:(q + 1) * DH], head_w[part, c, :]))
                    chain.did(v.tensor_copy(own_w[part, c, P + q:P + q + 1], score_v[part, c, 1:2]))
                    chain.did(v.tensor_scalar(f1w[part, 2 * c + q, :], k.ones[part, :], score_v[part, c, 0:1], None, ALU.mult))
            chain.settle()
            v.engine_nop().then_inc(w_ready, 1)
            for n in range(NT):
                dve.wait_ge(proj_ps, n + 1)
                pv = ps_p[:, n % 2, 0:KC * (P + 2)].rearrange("p (c w) -> p c w", c=KC)
                v.tensor_copy(k.xn[:, n, :].rearrange("p (c w) -> p c w", c=KC), pv[:, :, 0:P]).then_inc(dve_done, 1)
                v.tensor_scalar(g.f2_half[:, n, :].rearrange("p (c w) -> p c w", c=KC), pv[:, :, P:P + 2], 0.5, None,
                                ALU.mult).then_inc(proj_sb, 1)

        @block.tensor
        def _(pe):
            pe.wait_ge(w_in, 16 * (WIN - 1))
            pe.wait_ge(w_ready, 1)
            for l in range(2):
                if l:
                    pe.wait_ge(turned_sb, l)
                for kc in range(KC):
                    for oc in range(KC):
                        ins = nc.tensor.transpose(ps_w[:, 0, kc * D + oc * P:kc * D + (oc + 1) * P], mlp_rows[:, l, oc, kc * P:(kc + 1) * P], k.ident[:])
                ins.then_inc(turned, 1)
            for c in range(KC):
                ins = nc.tensor.transpose(ps_w[:, 1, c * P:(c + 1) * P], own_w[:, c, 0:P], k.ident[:])
            ins.then_inc(turned, 1)
            for n in range(NT):
                if n >= 2:
                    pe.wait_ge(proj_sb, n - 1)
                for c in range(KC):
                    ins = nc.tensor.matmul(ps_p[:, n % 2, c * (P + 2):(c + 1) * (P + 2)], k.xnT[:, c, n * P:(n + 1) * P], own_w[:, c, :],
                                           start=True, stop=True)
                ins.then_inc(proj_ps, 1)
            for h in range(H):
                for q in range(4):
                    if h:
                        pe.wait_ge(f1_sb, 4 * (h - 1) + q + 1)
                    nc.tensor.matmul(ps_f[:, q, :], f1w[:, h, :], k.xnT[:, h // 2, q * 512:(q + 1) * 512],
                                     start=True, stop=True).then_inc(f1_ps, 1)

        @block.scalar
        def _(act):
            s = nc.scalar
            for l in range(2):
                act.wait_ge(turned, l + 1)
                s.activation(g.mlp_wT[:, l].rearrange("p c n -> p (c n)"), ps_w[:, 0, :], ACT.Copy).then_inc(turned_sb, 1)
            act.wait_ge(turned, 3)
            s.activation(g.head_wT[:].rearrange("p c n -> p (c n)"), ps_w[:, 1, 0:KC * P], ACT.Copy).then_inc(turned_sb, 1)
            for h in range(H):
                for q in range(4):
                    act.wait_ge(f1_ps, 4 * h + q + 1)
                    s.activation(g.f1[:, h, q * 512:(q + 1) * 512], ps_f[:, q, :], ACT.Copy).then_inc(f1_sb, 1)


def phase_attend(k, g, name, first):
    nc = k.nc
    with ExitStack() as ctx, nc.Block() as block:
        ps = ctx.enter_context(nc.psum_tensor("ps_att_" + name, [P, 2, N], F32))
        tanh_ready, exp_ready, edge_ready, edge_free = (k.sem(s + name) for s in ("tanh_", "exp_", "edge_r_", "edge_f_"))
        near_ready, sum_free, inv_done = k.sem("near_" + name), k.sem("sum_free_" + name), k.sem("inv_" + name)
        divided = k.sem("divided_" + name)

        @block.scalar
        def _(act):
            with act.Fori(0, H // 2) as hp:
                def tanh_of(q, j):
                    s = hp * (2 * NT) + (q * NT + j)
                    slot = j % g.RING
                    act.wait_ge(g.f1_sb, 4 * H)
                    act.wait_ge(edge_free, s + 1)
                    nc.scalar.activation(g.edge[:, slot, :], g.f1[:, ds(hp * 2 + q, 1), :].rearrange("p o t -> p (o t)"), ACT.Tanh,
                                         scale=0.5, bias=g.f2_half[:, j, ds(hp * 2 + q, 1)]).then_inc(tanh_ready, 1)

                def exp_of(q, j):
                    act.wait_ge(tanh_ready, hp * (2 * NT) + (q * NT + j + 1))
                    nc.scalar.activation(g.edge[:, j % g.RING, :], g.edge[:, j % g.RING, :], ACT.Exp, scale=0.5).then_inc(exp_ready, 1)

                steps = [(q, j) for q in range(2) for j in range(NT)]
                tanh_of(0, 0)
                for i, (q, j) in enumerate(steps):
                    if i + 1 < len(steps):
                        tanh_of(*steps[i + 1])
                    exp_of(q, j)

        @block.gpsimd
        def _(pool):
            with pool.Fori(0, H // 2) as hp:
                for q in range(2):
                    for j in range(NT):
                        s = hp * (2 * NT) + (q * NT + j)
                        pool.wait_ge(edge_free, s + 1)
                        nc.gpsimd.tensor_copy(g.near[:, j % g.RING, 0:DH], k.xn[:, j, ds((hp * 2 + q) * DH, DH)]).then_inc(near_ready, 1)

        @block.tensor
        def _(pe):
            pe.sem_inc(edge_free, g.RING)
            with pe.Fori(0, H // 2) as hp:
                for q in range(2):
                    pe.wait_ge(sum_free, hp * 2 + (q + 1))
                    for j in range(NT):
                        s = hp * (2 * NT) + (q * NT + j)
                        pe.wait_ge(near_ready, s + 1)
                        pe.wait_ge(edge_ready, s + 1)
                        for i in range(4):
                            ins = nc.tensor.matmul(ps[:, q, i * 512:(i + 1) * 512], g.near[:, j % g.RING, :],
                                                   g.edge[:, j % g.RING, i * 512:(i + 1) * 512], start=(j == 0), stop=(j == NT - 1))
                        ins.then_inc(edge_free, 1)

        @block.vector
        def _(dve):
            v = nc.vector
            dve.sem_inc(sum_free, 2)
            chain = Chain(dve, inv_done)
            CH = 256

            def copy_out(hp, q):
                dve.wait_ge(edge_free, (2 * hp + q + 1) * NT + g.RING)
                rows = slice(q * DH, (q + 1) * DH)
                if first:
                    chain.did(v.tensor_scalar(g.inv[rows, hp, :], ps[DH:2 * DH, q, :], 1e-30, None, ALU.max))
                    v.tensor_copy(k.xnT[rows, hp, :], ps[0:DH, q, :]).then_inc(sum_free, 1)
                else:
                    v.tensor_tensor(k.xnT[rows, hp, :], ps[0:DH, q, :], g.inv[rows, hp, :], ALU.mult).then_inc(sum_free, 1)

            def invert(hp, piece):
                part = slice(piece * CH, (piece + 1) * CH)
                chain.did(v.reciprocal(g.inv[:, hp, part], g.inv[:, hp, part]))

            def divide(hp):
                chain.settle()
                dve.wait_ge(sum_free, 2 * hp + 4)
                v.tensor_tensor(k.xnT[:, hp, :], k.xnT[:, hp, :], g.inv[:, hp, :], ALU.mult).then_inc(divided, 1)

            for h in range(H):
                for j in range(NT):
                    dve.wait_ge(exp_ready, h * NT + j + 1)
                    v.tensor_tensor(g.edge[:, j % g.RING, :], g.edge[:, j % g.RING, :], k.adjT[:, j, :], ALU.mult).then_inc(edge_ready, 1)
                    if h and j == 2:
                        copy_out((h - 1) // 2, (h - 1) % 2)
                        chain.settle()
                    if first and h == 2 and 4 <= j < 4 + N // CH:
                        invert(0, j - 4)
                    if first and h == 2 and j == 4 + N // CH:
                        divide(0)
            copy_out(1, 1)
            if first:
                chain.settle()
                for piece in range(N // CH):
                    invert(1, piece)
                divide(1)


def phase_mlp(k, g, name, layer, pre_gamma, bias, gamma):
    nc = k.nc
    with ExitStack() as ctx, nc.Block() as block:
        stats = ctx.enter_context(nc.sbuf_tensor("stats_" + name, [P, KC, 4, 6], F32))
        mv = ctx.enter_context(nc.sbuf_tensor("mv_" + name, [P, KC, 2], F32))
        var = ctx.enter_context(nc.sbuf_tensor("var_" + name, [P, KC], F32))
        std = ctx.enter_context(nc.sbuf_tensor("std_" + name, [P, KC], F32))
        tmp = ctx.enter_context(nc.sbuf_tensor("tmp_" + name, [P, KC], F32))
        scale = ctx.enter_context(nc.sbuf_tensor("scale_" + name, [P, KC], F32))
        shift = ctx.enter_context(nc.sbuf_tensor("shift_" + name, [P, KC], F32))
        ps = ctx.enter_context(nc.psum_tensor("ps_mlp_" + name, [P, KC, N], F32))
        dve_done, var_ready, std_ready = k.sem("dve_done_" + name), k.sem("var_" + name), k.sem("std_" + name)
        neg_ready, neg_exp, x_ready, mlp_ps = k.sem("neg_" + name), k.sem("neg_exp_" + name), k.sem("x_ready_" + name), k.sem("mlp_ps_" + name)
        low, high = g.edge[:, 0:KC, :], g.edge[:, KC:2 * KC, :]
        pre_elu = pre_gamma is None

        @block.vector
        def _(dve):
            v = nc.vector
            chain = Chain(dve, dve_done)
            link = chain.link
            norms = [0]

            def batch_norm(col):
                for c in range(KC):
                    for q in range(4):
                        chain.did(v.bn_stats(stats[:, c, q, :], k.xnT[:, c, q * 512:(q + 1) * 512]))
                chain.settle()
                for c in range(KC):
                    chain.did(v.bn_aggr(mv[:, c, :], stats[:, c]))
                chain.settle()
                v.tensor_scalar(var[:], mv[:, :, 1], BN_EPS, None, ALU.add).then_inc(var_ready, 1)
                norms[0] += 1
                dve.wait_ge(std_ready, norms[0])
                link(v.reciprocal(scale[:], std[:]))
                rstd_of(chain, v, scale[:], var[:], tmp[:], None)
                link(v.tensor_tensor(scale[:], scale[:], k.vec[:, col:col + KC], ALU.mult))
                link(v.tensor_tensor(shift[:], mv[:, :, 0], scale[:], ALU.mult))
                link(v.tensor_tensor(shift[:], k.vec[:, col + KC:col + 2 * KC], shift[:], ALU.subtract))
                for c in range(KC):
                    chain.did(v.tensor_scalar(k.xnT[:, c, :], k.xnT[:, c, :], scale[:, c:c + 1], shift[:, c:c + 1], ALU.mult, ALU.add))
                chain.settle()

            if pre_elu:
                for c in range(KC):
                    v.tensor_scalar(low[:, c, :], k.xnT[:, c, :], 0.0, None, ALU.min).then_inc(neg_ready, 1)
                for c in range(KC):
                    link(v.tensor_scalar(k.xnT[:, c, :], k.xnT[:, c, :], 0.0, None, ALU.max))
                    dve.wait_ge(neg_exp, c + 1)
                    link(v.scalar_tensor_tensor(out=k.xnT[:, c, :], in0=low[:, c, :], scalar=-1.0, in1=k.xnT[:, c, :], op0=ALU.add, op1=ALU.add))
            else:
                batch_norm(pre_gamma)
            v.engine_nop().then_inc(x_ready, 1)
            done = KC if pre_elu else 0
            dve.wait_ge(mlp_ps, KC)
            for c in range(KC):
                v.tensor_scalar(low[:, c, :], ps[:, c, :], k.vec[:, bias + c:bias + c + 1], 0.0, ALU.add, ALU.min).then_inc(neg_ready, 1)
            for c in range(KC):
                link(v.tensor_scalar(high[:, c, :], ps[:, c, :], k.vec[:, bias + c:bias + c + 1], 0.0, ALU.add, ALU.max))
                link(v.tensor_tensor(k.xnT[:, c, :], k.xnT[:, c, :], high[:, c, :], ALU.add))
                dve.wait_ge(neg_exp, done + c + 1)
                link(v.scalar_tensor_tensor(out=k.xnT[:, c, :], in0=low[:, c, :], scalar=-1.0, in1=k.xnT[:, c, :], op0=ALU.add, op1=ALU.add))
            batch_norm(gamma)

        @block.scalar
        def _(act):
            s = nc.scalar
            done = 0
            if pre_elu:
                for c in range(KC):
                    act.wait_ge(neg_ready, c + 1)
                    s.activation(low[:, c, :], low[:, c, :], ACT.Exp).then_inc(neg_exp, 1)
                done = KC
            else:
                act.wait_ge(var_ready, 1)
                s.activation(std[:], var[:], ACT.Sqrt).then_inc(std_ready, 1)
            for c in range(KC):
                act.wait_ge(neg_ready, done + c + 1)
                s.activation(low[:, c, :], low[:, c, :], ACT.Exp).then_inc(neg_exp, 1)
            act.wait_ge(var_ready, 1 if pre_elu else 2)
            s.activation(std[:], var[:], ACT.Sqrt).then_inc(std_ready, 1)

        @block.tensor
        def _(pe):
            pe.wait_ge(x_ready, 1)
            for oc in range(KC):
                for q in range(4):
                    for kc in range(KC):
                        ins = nc.tensor.matmul(ps[:, oc, q * 512:(q + 1) * 512], g.mlp_wT[:, layer, kc, oc * P:(oc + 1) * P],
                                               k.xnT[:, kc, q * 512:(q + 1) * 512], start=(kc == 0), stop=(kc == KC - 1))
                ins.then_inc(mlp_ps, 1)


def phase_back(k, g):
    nc = k.nc
    with ExitStack() as ctx, nc.Block() as block:
        ps = ctx.enter_context(nc.psum_tensor("ps_back", [P, 4, 512], F32))
        back_ps, back_sb = k.sem("back_ps"), k.sem("back_sb")

        @block.tensor
        def _(pe):
            for n in range(NT):
                if n >= 4:
                    pe.wait_ge(back_sb, n - 3)
                for c in range(KC):
                    ins = nc.tensor.matmul(ps[:, n % 4, c * P:(c + 1) * P], k.xnT[:, c, n * P:(n + 1) * P], g.head_wT[:, c, :],
                                           start=True, stop=True)
                ins.then_inc(back_ps, 1)

        @block.scalar
        def _(act):
            for n in range(NT):
                act.wait_ge(back_ps, n + 1)
                nc.scalar.activation(k.xn[:, n, :], ps[:, n % 4, 0:D], ACT.Copy).then_inc(back_sb, 1)


def phase_residual(k):
    nc = k.nc
    with ExitStack() as ctx, nc.Block() as block:
        ps = ctx.enter_context(nc.psum_tensor("ps_res", [P, 4, 512], F32))
        res_ps, res_sb = k.sem("res_ps"), k.sem("res_sb")

        @block.tensor
        def _(pe):
            for n in range(NT):
                if n >= 4:
                    pe.wait_ge(res_sb, n - 3)
                for c in range(KC):
                    ins = nc.tensor.transpose(ps[:, n % 4, c * P:(c + 1) * P], k.xnT[:, c, n * P:(n + 1) * P], k.ident[:])
                ins.then_inc(res_ps, 1)

        @block.vector
        def _(dve):
            for n in range(NT):
                dve.wait_ge(res_ps, n + 1)
                nc.vector.tensor_tensor(k.x[:, n, :], k.x[:, n, :], ps[:, n % 4, 0:D], ALU.add).then_inc(res_sb, 1)


def gnn1(k, I):
    nc = k.nc
    with ExitStack() as ctx:
        def sb(name, shape, dt=F32):
            return ctx.enter_context(nc.sbuf_tensor(name, shape, dt))
        g = Shared()
        g.RING = 4
        g.f1 = sb("f1", [P, H, N])
        g.f2_half = sb("f2_half", [P, NT, H])
        g.mlp_wT = sb("mlp_wT", [P, 2, KC, D])
        g.head_wT = sb("head_wT", [P, KC, P])
        g.near = sb("near", [P, g.RING, 2 * DH])
        phase_gnn1_project(k, I, g)
        g.edge = sb("edge", [P, g.RING, N])
        g.inv = sb("inv1", [P, KC, N])
        phase_attend(k, g, "enc", True)
        phase_mlp(k, g, "enc_mlp", 0, VEC_COL["L1_gnn_enc_bn_gamma"], VEC_COL["L1_gnn_enc_mlp_b"], VEC_COL["L1_gnn_enc_mlp_bn_gamma"])
        phase_back(k, g)
        phase_attend(k, g, "dec", False)
        phase_mlp(k, g, "dec_mlp", 1, None, VEC_COL["L1_gnn_dec_mlp_b"], VEC_COL["L1_gnn_dec_mlp_bn_gamma"])
        phase_residual(k)


def build(nc, I, out, stop=99):
    with ExitStack() as ctx:
        def sb(name, shape, dt=F32):
            return ctx.enter_context(nc.sbuf_tensor(name, shape, dt))
        k = Shared()
        k.nc, k.sems = nc, []

        def new_sem(name):
            k.sems.append(nc.alloc_semaphore(name=name))
            return k.sems[-1]

        def clear_sems():
            nc.clear_and_free_semaphores(k.sems)
            nc.all_engine_barrier()
            k.sems = []

        k.sem = new_sem
        k.slots_in = nc.dram_tensor("slots_in", [NB * BLK, D], F32).ap()
        k.slots_out = nc.dram_tensor("slots_out", [NB * BLK, D], F32).ap()
        k.b1_dram = nc.dram_tensor("b1_dram", [P, 2, E * FT], F32).ap()
        k.x = sb("x", [P, NT, D])
        k.xn = sb("xn", [P, NT, D])
        k.xnT = sb("xnT", [P, KC, N])
        k.adjT = sb("adjT", [P, NT, N], BF16)
        k.ident, k.ones, k.before = sb("ident", [P, P]), sb("ones", [P, P]), sb("before", [P, P])
        k.iota_i, k.iota = sb("iota_i", [P, 32], I32), sb("iota", [P, 32])
        k.vec = sb("vec", [P, VEC_ROWS])
        k.gate_w, k.gate_b = sb("gate_w", [P, 2, KC, E]), sb("gate_b", [P, 2, E])
        k.ln_stats, k.ln_mv = sb("ln_stats", [P, NT, 6]), sb("ln_mv", [P, NT, 2])
        k.ln_var, k.ln_std, k.ln_rstd, k.ln_tmp = (sb(n, [P, NT]) for n in ("ln_var", "ln_std", "ln_rstd", "ln_tmp"))
        k.pair_w = sb("pair_w", [P, NT, TOP])
        k.slot = sb("slot", [P, TOP, NT], I32)
        k.expert = sb("expert", [P, NB], I32)

        with ExitStack() as gctx:
            k.w_cat = gctx.enter_context(nc.sbuf_tensor("w_cat", [P, KC, 2 * D], F32))
            k.a_sa = gctx.enter_context(nc.sbuf_tensor("a_sa", [P, 2 * D], F32))
            k.b_gcnb = gctx.enter_context(nc.sbuf_tensor("b_gcnb", [P, D], F32))
            k.type_bias = gctx.enter_context(nc.sbuf_tensor("type_bias", [P, 2], F32))
            phase_load(k, I)
            if stop > 1:
                phase_gnn0(k, I)
        if stop > 2:
            block_norm(k, "n1")
            phase_route(k, 0)
        if stop > 3:
            phase_experts(k, 0, I["L0_ffn_w1"], I["L0_ffn_w2"], I["L0_ffn_b2"])
        if stop > 4:
            phase_combine(k, 0)
            clear_sems()
        if stop > 5:
            block_norm(k, "n2")
            gnn1(k, I)
        if stop > 6:
            block_norm(k, "n3")
            phase_route(k, 1)
            phase_experts(k, 1, I["L1_ffn_W1"], I["L1_ffn_W2"], I["L1_ffn_b2"])
            phase_combine(k, 1, out)


INPUTS = ["x", "adj", "L0_gnn_W_sa", "L0_gnn_a_sa", "L0_gnn_W_gcnb", "L0_gnn_b_gcnb", "L0_gnn_Wa", "L0_gnn_ba", "L0_gnn_Wb", "L0_gnn_bb",
          "L0_ffn_gate_w", "L0_ffn_gate_b", "L0_ffn_w1", "L0_ffn_b1", "L0_ffn_w2", "L0_ffn_b2", "L1_gnn_W", "L1_gnn_V",
          "L1_gnn_enc_bn_gamma", "L1_gnn_enc_bn_beta", "L1_gnn_enc_mlp_W", "L1_gnn_enc_mlp_b", "L1_gnn_enc_mlp_bn_gamma",
          "L1_gnn_enc_mlp_bn_beta", "L1_gnn_dec_mlp_W", "L1_gnn_dec_mlp_b", "L1_gnn_dec_mlp_bn_gamma", "L1_gnn_dec_mlp_bn_beta",
          "L1_ffn_Wg", "L1_ffn_bg", "L1_ffn_W1", "L1_ffn_b1", "L1_ffn_W2", "L1_ffn_b2"]


def kernel(**inputs):
    import numpy as np
    import concourse.bacc as bacc
    from concourse.bass_utils import run_bass_kernel_spmd

    nc = bacc.Bacc("TRN2", target_bir_lowering=False, num_devices=1)
    arrays, aps = {}, {}
    for name in INPUTS:
        a = np.ascontiguousarray(inputs[name])
        arrays[f"in_{name}"] = a
        aps[name] = nc.dram_tensor(f"in_{name}", a.shape, mybir.dt.from_np(a.dtype), kind="ExternalInput").ap()
    out = nc.dram_tensor("out", (N, D), F32, kind="ExternalOutput").ap()
    build(nc, aps, out)
    result = run_bass_kernel_spmd(nc, [arrays], core_ids=[0])
    return result.results[0]["out"]
```

```python
from contextlib import ExitStack

import concourse.bass as bass
from concourse import mybir

F32 = mybir.dt.float32
BF16 = mybir.dt.bfloat16
F32R = mybir.dt.float32r
I32 = mybir.dt.int32
U32 = mybir.dt.uint32
ALU = mybir.AluOpType
ACT = mybir.ActivationFunctionType
AX_X = mybir.AxisListType.X

P = 128
N = 2048
NT = N // P
D = 256
KC = D // P
E = 8
F = 1024
FT = F // P
TOP = 2
BLK = 256
BT = BLK // P
NB = (TOP * N + E * (BLK - 1)) // BLK
ST = NB * BT
H = 4
DH = D // H
LN_EPS = 1e-5
BN_EPS = 1e-6
ds = bass.ds

VEC_NAMES = ["L1_gnn_enc_bn_gamma", "L1_gnn_enc_bn_beta", "L1_gnn_enc_mlp_b", "L1_gnn_enc_mlp_bn_gamma",
             "L1_gnn_enc_mlp_bn_beta", "L1_gnn_dec_mlp_b", "L1_gnn_dec_mlp_bn_gamma", "L1_gnn_dec_mlp_bn_beta"]
VEC_COL = {name: 8 + KC * i for i, name in enumerate(VEC_NAMES)}
VEC_ROWS = 8 + KC * len(VEC_NAMES)


class Shared:
    pass


class Chain:

    def __init__(self, eng, sem):
        self.eng, self.sem, self.count = eng, sem, 0

    def did(self, ins):
        ins.then_inc(self.sem, 1)
        self.count += 1

    def settle(self):
        self.eng.wait_ge(self.sem, self.count)

    def link(self, ins):
        self.did(ins)
        self.settle()


def rstd_of(chain, nc_vector, out, var, tmp, sqrt_wait):
    chain.link(nc_vector.tensor_tensor(tmp, out, out, ALU.mult))
    chain.link(nc_vector.tensor_tensor(tmp, tmp, var, ALU.mult))
    chain.link(nc_vector.tensor_scalar(tmp, tmp, -0.5, 1.5, ALU.mult, ALU.add))
    chain.link(nc_vector.tensor_tensor(out, out, tmp, ALU.mult))


def layer_norm_vector(k, dve, chain, var_ready, std_ready, tile_ready, x_ready=None):
    v = k.nc.vector
    for n in range(NT):
        if x_ready is not None and n % 4 == 0:
            dve.wait_ge(x_ready[n // 4], 16)
        chain.did(v.bn_stats(k.ln_stats[:, n, :], k.x[:, n, :]))
    chain.settle()
    for n in range(NT):
        chain.did(v.bn_aggr(k.ln_mv[:, n, :], k.ln_stats[:, n, :]))
    chain.settle()
    v.tensor_scalar(k.ln_var[:], k.ln_mv[:, :, 1], LN_EPS, None, ALU.add).then_inc(var_ready, 1)
    dve.wait_ge(std_ready, 1)
    chain.link(v.reciprocal(k.ln_rstd[:], k.ln_std[:]))
    rstd_of(chain, v, k.ln_rstd[:], k.ln_var[:], k.ln_tmp[:], None)
    for n in range(NT):
        v.tensor_scalar(k.xn[:, n, :], k.x[:, n, :], k.ln_mv[:, n, 0:1], k.ln_rstd[:, n:n + 1],
                        ALU.subtract, ALU.mult).then_inc(tile_ready, 1)


def layer_norm_sqrt(k, act, var_ready, std_ready):
    act.wait_ge(var_ready, 1)
    k.nc.scalar.activation(k.ln_std[:], k.ln_var[:], ACT.Sqrt).then_inc(std_ready, 1)


def transpose_xn_tensor(k, pe, ps, tile_ready, pair_ps, pair_sb):
    for q in range(NT // 2):
        pe.wait_ge(tile_ready, 2 * q + 2)
        if q >= 2:
            pe.wait_ge(pair_sb, q - 1)
        for c in range(KC):
            for t in range(2):
                ins = k.nc.tensor.transpose(ps[:, q % 2, c * 2 * P + t * P:c * 2 * P + (t + 1) * P],
                                            k.xn[:, 2 * q + t, c * P:(c + 1) * P], k.ident[:])
        ins.then_inc(pair_ps, 1)


def transpose_xn_scalar(k, act, ps, pair_ps, pair_sb):
    for q in range(NT // 2):
        act.wait_ge(pair_ps, q + 1)
        k.nc.scalar.activation(k.xnT[:, :, q * 2 * P:(q + 1) * 2 * P],
                               ps[:, q % 2, :].rearrange("p (c t) -> p c t", c=KC), ACT.Copy).then_inc(pair_sb, 1)


def phase_load(k, I):
    nc = k.nc
    RING = 4
    with ExitStack() as ctx:
        adj_rows = ctx.enter_context(nc.sbuf_tensor("adj_rows", [P, RING, N], F32))
        vec_rows = ctx.enter_context(nc.sbuf_tensor("vec_rows", [VEC_ROWS, P], F32))
        b1_rows = ctx.enter_context(nc.sbuf_tensor("b1_rows", [E * FT, 2, P], F32))
        iota_i = ctx.enter_context(nc.sbuf_tensor("iota_i", [P, P], I32))
        lane_i = ctx.enter_context(nc.sbuf_tensor("lane_i", [P, 1], I32))
        tile_i = ctx.enter_context(nc.sbuf_tensor("tile_i", [P, TOP * NT], I32))
        spare_i = ctx.enter_context(nc.sbuf_tensor("spare_i", [P, ST], I32))
        b1_cols = ctx.enter_context(nc.sbuf_tensor("b1_cols", [P, 2, E * FT], F32))
        ps_adj = ctx.enter_context(nc.psum_tensor("ps_adj", [P, 4, 512], F32))
        ps_xn = ctx.enter_context(nc.psum_tensor("ps_xn_a", [P, 2, 512], F32))
        ps_vec = ctx.enter_context(nc.psum_tensor("ps_vec", [P, 512], F32))
        x_in = [k.sem(f"x_in{q}") for q in range(4)]
        small_in, rows_in = k.sem("small_in"), k.sem("rows_in")
        adj_in = [k.sem(f"adj_in{u}") for u in range(RING)]
        consts, adj_ps, adj_sb_act, adj_sb_dve = k.sem("consts"), k.sem("adj_ps"), k.sem("adj_sb_act"), k.sem("adj_sb_dve")
        vec_ps, vec_sb, b1_sb, b1_out = k.sem("vec_ps"), k.sem("vec_sb"), k.sem("b1_sb"), k.sem("b1_out")
        dve_done, var_ready, std_ready = k.sem("dve_done_a"), k.sem("var_a"), k.sem("std_a")
        tile_ready, pair_ps, pair_sb = k.sem("tile_a"), k.sem("pair_ps_a"), k.sem("pair_sb_a")
        GR = NT // 4

        rows = [("L0_gnn_Wa", 0, 4), ("L0_gnn_Wb", 4, 4)] + [(n, VEC_COL[n], KC) for n in VEC_NAMES]
        small = [
            (k.w_cat[:, :, 0:D], I["L0_gnn_W_sa"].rearrange("(c p) n -> p c n", p=P)),
            (k.w_cat[:, :, D:2 * D], I["L0_gnn_W_gcnb"].rearrange("(c p) n -> p c n", p=P)),
            (k.a_sa[:], I["L0_gnn_a_sa"].to_broadcast([P, 2 * D])),
            (k.b_gcnb[:], I["L0_gnn_b_gcnb"].rearrange("(o n) -> o n", o=1).to_broadcast([P, D])),
            (k.type_bias[:, 0:1], I["L0_gnn_ba"].rearrange("(o n) -> o n", o=1).to_broadcast([P, 1])),
            (k.type_bias[:, 1:2], I["L0_gnn_bb"].rearrange("(o n) -> o n", o=1).to_broadcast([P, 1])),
            (k.gate_w[:, 0], I["L0_ffn_gate_w"].rearrange("(c p) e -> p c e", p=P)),
            (k.gate_w[:, 1], I["L1_ffn_Wg"].rearrange("(c p) e -> p c e", p=P)),
            (k.gate_b[:, 0], I["L0_ffn_gate_b"].rearrange("(o e) -> o e", o=1).to_broadcast([P, E])),
            (k.gate_b[:, 1], I["L1_ffn_bg"].rearrange("(o e) -> o e", o=1).to_broadcast([P, E])),
        ]
        xv = I["x"].rearrange("(n p) d -> p n d", p=P)

        with nc.Block() as block:
            @block.sync
            def _(sp):
                for q in range(4):
                    sp.dma_start(k.x[:, 4 * q:4 * q + 4, :], xv[:, 4 * q:4 * q + 4, :]).then_inc(x_in[q], 16)

                def load(i, u, first):
                    if not first:
                        sp.wait_ge(adj_ps, (i - RING + 1) * GR)
                    sp.dma_start(adj_rows[:, u, :], I["adj"][ds(i * P, P), :]).then_inc(adj_in[u], 16)
                for u in range(RING):
                    load(u, u, True)
                with sp.Fori(1, NT // RING) as g:
                    for u in range(RING):
                        load(g * RING + u, u, False)
                sp.wait_ge(b1_sb, 2)
                sp.dma_start(k.b1_dram, b1_cols[:]).then_inc(b1_out, 16)
                sp.wait_ge(b1_out, 16)

            @block.gpsimd
            def _(pool):
                g = nc.gpsimd
                g.memset(k.ident[:], 0.0).then_inc(consts, 1)
                g.memset(k.ones[:], 1.0).then_inc(consts, 1)
                pool.wait_ge(consts, 2)
                g.affine_select(out=k.ident[:], in_=k.ident[:], compare_op=ALU.not_equal, fill=1.0, base=0,
                                pattern=[[-1, P]], channel_multiplier=1).then_inc(consts, 1)
                g.affine_select(out=k.before[:], in_=k.ones[:], compare_op=ALU.is_gt, fill=0.0, base=0,
                                pattern=[[1, P]], channel_multiplier=-1).then_inc(consts, 1)
                g.iota(iota_i[:], pattern=[[1, P]], base=0, channel_multiplier=0).then_inc(consts, 1)
                g.iota(lane_i[:], pattern=[[1, 1]], base=1, channel_multiplier=1).then_inc(consts, 1)
                g.iota(tile_i[:], pattern=[[1, TOP * NT]], base=0, channel_multiplier=0).then_inc(consts, 1)
                g.iota(spare_i[:], pattern=[[P, ST]], base=TOP * N + 1, channel_multiplier=1).then_inc(consts, 1)
                pool.wait_ge(consts, 8)
                g.tensor_copy(k.iota[:], iota_i[:]).then_inc(consts, 1)
                g.tensor_copy(k.lane_id[:], lane_i[:]).then_inc(consts, 1)
                g.tensor_copy(k.tile_id[:].rearrange("p c n -> p (c n)"), tile_i[:]).then_inc(consts, 1)
                g.tensor_copy(k.spare[:], spare_i[:]).then_inc(consts, 1)

            @block.scalar
            def _(act):
                for name, row, count in rows:
                    src = rows_of(I, name, count)
                    act.dma_start(vec_rows[row:row + count, :], src).then_inc(rows_in, 16)
                act.dma_start(b1_rows[:, 0, :], I["L0_ffn_b1"].rearrange("e (m p) -> (e m) p", p=P)).then_inc(rows_in, 16)
                act.dma_start(b1_rows[:, 1, :], I["L1_ffn_b1"].rearrange("e (m p) -> (e m) p", p=P)).then_inc(rows_in, 16)
                for dst, src in small:
                    act.dma_start(dst, src).then_inc(small_in, 16)
                layer_norm_sqrt(k, act, var_ready, std_ready)
                transpose_xn_scalar(k, act, ps_xn, pair_ps, pair_sb)
                act.wait_ge(vec_ps, 1)
                nc.scalar.activation(k.vec[:], ps_vec[:, 0:VEC_ROWS], ACT.Copy).then_inc(vec_sb, 1)
                for l in range(2):
                    nc.scalar.activation(b1_cols[:, l, :], ps_vec[:, 128 + 64 * l:192 + 64 * l], ACT.Copy).then_inc(b1_sb, 1)

                def evac(i, u):
                    for g in (0, 2):
                        act.wait_ge(vec_sb, 1)
                        act.wait_ge(adj_ps, i * GR + g + 1)
                        nc.scalar.activation(k.adjT[:, 4 * g:4 * g + 4, ds(i * P, P)],
                                             ps_adj[:, g, :].rearrange("p (j t) -> p j t", j=4), ACT.Copy).then_inc(adj_sb_act, 1)
                with act.Fori(0, NT) as i:
                    evac(i, 0)
                act.wait_ge(small_in, 16 * len(small))

            @block.tensor
            def _(pe):
                pe.wait_ge(consts, 3)
                transpose_xn_tensor(k, pe, ps_xn, tile_ready, pair_ps, pair_sb)
                pe.wait_ge(rows_in, 16 * (len(rows) + 2))
                nc.tensor.transpose(ps_vec[:, 0:VEC_ROWS], vec_rows[:], k.ident[0:VEC_ROWS, 0:VEC_ROWS])
                nc.tensor.transpose(ps_vec[:, 128:192], b1_rows[:, 0, :], k.ident[0:64, 0:64])
                nc.tensor.transpose(ps_vec[:, 192:256], b1_rows[:, 1, :], k.ident[0:64, 0:64]).then_inc(vec_ps, 1)

                def turn(i, u, loads, first):
                    pe.wait_ge(adj_in[u], 16 * loads)
                    for g in range(GR):
                        if not first:
                            pe.wait_ge(adj_sb_act if g % 2 == 0 else adj_sb_dve, 2 * (i - 1) + g // 2 + 1)
                        for j in range(4):
                            ins = nc.tensor.transpose(ps_adj[:, g, j * P:(j + 1) * P],
                                                      adj_rows[:, u, (4 * g + j) * P:(4 * g + j + 1) * P], k.ident[:])
                        ins.then_inc(adj_ps, 1)
                for u in range(RING):
                    turn(u, u, 1, u == 0)
                with pe.Fori(1, NT // RING) as g4:
                    for u in range(RING):
                        turn(g4 * RING + u, u, g4 + 1, False)

            @block.vector
            def _(dve):
                chain = Chain(dve, dve_done)
                layer_norm_vector(k, dve, chain, var_ready, std_ready, tile_ready, x_in)

                with dve.Fori(0, NT) as i:
                    for g in (1, 3):
                        dve.wait_ge(adj_ps, i * GR + g + 1)
                        nc.vector.tensor_copy(k.adjT[:, 4 * g:4 * g + 4, ds(i * P, P)],
                                              ps_adj[:, g, :].rearrange("p (j t) -> p j t", j=4)).then_inc(adj_sb_dve, 1)


def rows_of(I, name, count):
    src = I[name]
    if len(src.shape) == 2:
        return src.rearrange("o (r p) -> (o r) p", p=P)
    return src.rearrange("(r p) -> r p", p=P)


def phase_gnn0(k, I):
    nc = k.nc
    HALF = NT // 2
    HW_ = HALF * P
    W = D + 2
    RING = 4
    with ExitStack() as ctx:
        def sb(name, shape, dt=F32):
            return ctx.enter_context(nc.sbuf_tensor(name, shape, dt))
        hA = sb("hA", [P, NT, D + 1])
        conv = sb("conv", [P, 4, W])
        conv_part = sb("conv_part", [P, 3, NT, W], BF16)
        rest = sb("conv_rest", [P, 4, W])
        own = sb("own", [P, NT, 2])
        s_right = sb("s_right", [P, NT])
        s_left = sb("s_left", [P, N])
        vec6 = sb("vec6", [P, KC, 6])
        left_w = sb("left_w", [P, KC, P])
        junk = sb("junk", [P, D])
        left_col = sb("left_col", [P, KC])
        zbuf = k.xnT[:, :, 0:HW_]
        b = k.xn[:, 0:HALF, :]
        a = k.xn[:, HALF:HALF + 2, :]
        ebuf = sb("ebuf", [P, RING, HW_])
        gate = sb("gate", [P, HALF, 2])
        inv = sb("inv", [P, HALF])
        dve_done, act_done = k.sem("dve_done_b"), k.sem("act_done_b")
        vec_ready, proj_ps, proj_sb = k.sem("vec_ready"), k.sem("proj_ps"), k.sem("proj_sb")
        left_ps, left_sb = k.sem("left_ps"), k.sem("left_sb")
        z_ready, leaky_ready, exp_ready = k.sem("z_ready"), k.sem("leaky_ready"), k.sem("exp_ready")
        edge_ready, edge_used = k.sem("edge_ready"), k.sem("edge_used")
        conv_ps, conv_sb, att_sb = k.sem("conv_ps"), k.sem("conv_sb"), k.sem("att_sb")
        type_ready, gate_ready = k.sem("type_ready"), k.sem("gate_ready")
        mix_ready, sig_ready, half_done, half_chain = k.sem("mix_ready"), k.sem("sig_ready"), k.sem("half_done"), k.sem("half_chain")

        with ExitStack() as pctx, nc.Block() as block:
            ps_h = pctx.enter_context(nc.psum_tensor("ps_h", [P, 2, 512], F32))
            ps_s = pctx.enter_context(nc.psum_tensor("ps_s", [P, 2, 512], F32))
            ps_left = pctx.enter_context(nc.psum_tensor("ps_left", [P, 4, 512], F32))

            @block.vector
            def _(dve):
                v = nc.vector
                chain = Chain(dve, dve_done)
                for c in range(KC):
                    chain.did(v.tensor_tensor_reduce(out=junk[:], in0=k.w_cat[:, c, 0:D], in1=k.a_sa[:, 0:D], scale=1.0,
                                                     scalar=0.0, op0=ALU.mult, op1=ALU.add, accum_out=left_col[:, c:c + 1]))
                    chain.settle()
                    chain.link(v.tensor_tensor_reduce(out=junk[:], in0=k.w_cat[:, c, 0:D], in1=k.a_sa[:, D:2 * D], scale=1.0,
                                                      scalar=0.0, op0=ALU.mult, op1=ALU.add, accum_out=vec6[:, c, 0:1]))
                for c in range(KC):
                    chain.did(v.tensor_copy(vec6[:, c, 1:2], k.vec[:, c:c + 1]))
                    chain.did(v.tensor_copy(vec6[:, c, 2:3], k.vec[:, 4 + c:5 + c]))
                    chain.did(v.tensor_copy(vec6[:, c, 3:4], k.vec[:, 2 + c:3 + c]))
                    chain.did(v.tensor_copy(vec6[:, c, 4:5], k.vec[:, 6 + c:7 + c]))
                    chain.did(v.tensor_scalar(left_w[:, c, :], k.ones[:], left_col[:, c:c + 1], None, ALU.mult))
                chain.did(v.memset(vec6[:, :, 5:6], 0.0))
                chain.settle()
                v.memset(hA[:, :, D:D + 1], 1.0).then_inc(vec_ready, 1)
                for n in range(NT):
                    dve.wait_ge(proj_ps, n + 1)
                    chain.did(v.tensor_copy(conv[:, n % 4, 0:D], ps_h[:, n % 2, D:2 * D]))
                    chain.did(v.tensor_copy(s_right[:, n:n + 1], ps_s[:, n % 2, 0:1]))
                    chain.did(v.tensor_copy(conv[:, n % 4, D:W], ps_s[:, n % 2, 1:3]))
                    chain.did(v.tensor_copy(hA[:, n, 0:D], ps_h[:, n % 2, 0:D]))
                    v.tensor_copy(own[:, n, :], ps_s[:, n % 2, 3:5]).then_inc(proj_sb, 1)
                    if n % 4 == 3:
                        four = slice(n - 3, n + 1)
                        chain.settle()
                        chain.link(v.tensor_copy(conv_part[:, 0, four], conv[:]))
                        chain.link(v.tensor_tensor(rest[:], conv[:], conv_part[:, 0, four], ALU.subtract))
                        chain.link(v.tensor_copy(conv_part[:, 1, four], rest[:]))
                        chain.link(v.tensor_tensor(rest[:], rest[:], conv_part[:, 1, four], ALU.subtract))
                        chain.link(v.tensor_copy(conv_part[:, 2, four], rest[:]))

            @block.tensor
            def _(pe):
                pe.wait_ge(vec_ready, 1)
                for n in range(NT):
                    if n >= 2:
                        pe.wait_ge(proj_sb, n - 1)
                    for c in range(KC):
                        nc.tensor.matmul(ps_h[:, n % 2, :], k.xnT[:, c, n * P:(n + 1) * P], k.w_cat[:, c, :],
                                         start=(c == 0), stop=(c == KC - 1))
                    for c in range(KC):
                        ins = nc.tensor.matmul(ps_s[:, n % 2, 0:6], k.xnT[:, c, n * P:(n + 1) * P], vec6[:, c, :],
                                               start=(c == 0), stop=(c == KC - 1))
                    ins.then_inc(proj_ps, 1)
                for q in range(4):
                    for c in range(KC):
                        ins = nc.tensor.matmul(ps_left[:, q, :], left_w[:, c, :], k.xnT[:, c, q * 512:(q + 1) * 512],
                                               start=(c == 0), stop=(c == KC - 1))
                    ins.then_inc(left_ps, 1)

            @block.scalar
            def _(act):
                for q in range(4):
                    act.wait_ge(left_ps, q + 1)
                    nc.scalar.activation(s_left[:, q * 512:(q + 1) * 512], ps_left[:, q, :], ACT.Copy).then_inc(left_sb, 1)

        with ExitStack() as pctx, nc.Block() as block:
            ps = pctx.enter_context(nc.psum_tensor("ps_half", [P, HALF, 512], F32))

            @block.tensor
            def _(pe):
                with pe.Fori(0, 2) as half:
                    for j in range(NT):
                        for i in range(HALF):
                            for part in range(3):
                                ins = nc.tensor.matmul(ps[:, i, 0:W], k.adjT[:, j, ds(half * HW_ + i * P, P)],
                                                       conv_part[:, part, j, :], start=(j == 0 and part == 0),
                                                       stop=(j == NT - 1 and part == 2))
                            if j == NT - 1:
                                ins.then_inc(conv_ps, 1)
                    for j in range(NT):
                        pe.wait_ge(edge_ready, half * NT + j + 1)
                        for i in range(HALF):
                            if j == 0:
                                pe.wait_ge(conv_sb, half * HALF + i + 1)
                            ins = nc.tensor.matmul(ps[:, i, 0:D + 1], ebuf[:, j % RING, i * P:(i + 1) * P], hA[:, j, :],
                                                   start=(j == 0), stop=(j == NT - 1))
                        ins.then_inc(edge_used, 1)
                    pe.wait_ge(att_sb, (half + 1) * HALF)

            @block.scalar
            def _(act):
                with act.Fori(0, 2) as half:
                    def z_of(j):
                        act.wait_ge(left_sb, 4)
                        if j >= 2:
                            act.wait_ge(leaky_ready, half * NT + j - 1)
                        nc.scalar.activation(zbuf[:, j % 2, :], s_left[:, ds(half * HW_, HW_)], ACT.Identity,
                                             bias=s_right[:, j:j + 1]).then_inc(z_ready, 1)

                    def exp_of(j):
                        act.wait_ge(leaky_ready, half * NT + j + 1)
                        nc.scalar.activation(ebuf[:, j % RING, :], ebuf[:, j % RING, :], ACT.Exp, scale=-1.0).then_inc(exp_ready, 1)

                    z_of(0)
                    for j in range(NT):
                        if j + 1 < NT:
                            z_of(j + 1)
                        exp_of(j)
                        if j == 1:
                            act.wait_ge(type_ready, half + 1)
                            nc.scalar.activation(gate[:], gate[:], ACT.Tanh, scale=0.5).then_inc(gate_ready, 1)
                    for i in range(HALF):
                        act.wait_ge(mix_ready, half * HALF + i + 1)
                        nc.scalar.activation(a[:, i % 2, :], a[:, i % 2, :], ACT.Tanh, scale=0.5).then_inc(sig_ready, 1)

            @block.vector
            def _(dve):
                v = nc.vector
                with dve.Fori(0, 2) as half:
                    def leaky(j):
                        dve.wait_ge(z_ready, half * NT + j + 1)
                        if j >= RING:
                            dve.wait_ge(edge_used, half * NT + j - RING + 1)
                        v.scalar_tensor_tensor(out=ebuf[:, j % RING, :], in0=zbuf[:, j % 2, :], scalar=0.01,
                                               in1=zbuf[:, j % 2, :], op0=ALU.mult, op1=ALU.max).then_inc(leaky_ready, 1)

                    def mask(j):
                        dve.wait_ge(exp_ready, half * NT + j + 1)
                        v.tensor_tensor(ebuf[:, j % RING, :], ebuf[:, j % RING, :], k.adjT[:, j, ds(half * HW_, HW_)],
                                        ALU.mult).then_inc(edge_ready, 1)

                    def conv_out():
                        for i in range(HALF):
                            dve.wait_ge(conv_ps, half * HALF + i + 1)
                            v.tensor_tensor(b[:, i, :], ps[:, i, 0:D], k.b_gcnb[:], ALU.add)
                            v.tensor_tensor(gate[:, i, :], ps[:, i, D:W], own[:, ds(half * HALF + i, 1), :].rearrange("p o w -> p (o w)"),
                                            ALU.add).then_inc(conv_sb, 1)
                        dve.wait_ge(conv_sb, (half + 1) * HALF)
                        v.tensor_tensor(gate[:], gate[:], k.type_bias[:].rearrange("p (o w) -> p o w", o=1).to_broadcast([P, HALF, 2]),
                                        ALU.add).then_inc(type_ready, 1)

                    leaky(0)
                    for j in range(NT):
                        if j == 1:
                            conv_out()
                        if j + 1 < NT:
                            leaky(j + 1)
                        mask(j)
                    dve.wait_ge(gate_ready, half + 1)
                    v.tensor_scalar(gate[:], gate[:], 0.5, 0.5, ALU.mult, ALU.add).then_inc(half_chain, 1)
                    dve.wait_ge(edge_used, (half + 1) * NT)
                    v.tensor_scalar(inv[:], ps[:, :, D:D + 1].rearrange("p i o -> p (i o)"), 1e-5, None, ALU.add).then_inc(half_chain, 1)
                    dve.wait_ge(half_chain, half * 4 + 2)
                    v.reciprocal(inv[:], inv[:]).then_inc(half_chain, 1)
                    dve.wait_ge(half_chain, half * 4 + 3)
                    v.tensor_tensor(inv[:], inv[:], gate[:, :, 0], ALU.mult).then_inc(half_chain, 1)
                    dve.wait_ge(half_chain, half * 4 + 4)

                    def mix(i):
                        if i >= 2:
                            dve.wait_ge(half_done, half * HALF * 2 + (i - 1) * 2)
                        v.tensor_scalar(a[:, i % 2, :], ps[:, i, 0:D], inv[:, i:i + 1], None, ALU.mult).then_inc(att_sb, 1)
                        dve.wait_ge(att_sb, half * HALF + i + 1)
                        v.scalar_tensor_tensor(out=a[:, i % 2, :], in0=b[:, i, :], scalar=gate[:, i, 1:2], in1=a[:, i % 2, :],
                                               op0=ALU.mult, op1=ALU.add).then_inc(mix_ready, 1)

                    def residual(i):
                        row = k.x[:, ds(half * HALF + i, 1), :].rearrange("p o d -> p (o d)")
                        dve.wait_ge(sig_ready, half * HALF + i + 1)
                        v.scalar_tensor_tensor(out=row, in0=a[:, i % 2, :], scalar=0.5, in1=row, op0=ALU.mult, op1=ALU.add).then_inc(half_done, 1)
                        dve.wait_ge(half_done, half * HALF * 2 + i * 2 + 1)
                        v.tensor_scalar(row, row, 0.5, None, ALU.add).then_inc(half_done, 1)

                    mix(0)
                    for i in range(HALF):
                        if i + 1 < HALF:
                            mix(i + 1)
                        residual(i)


def block_norm(k, name):
    nc = k.nc
    with ExitStack() as ctx, nc.Block() as block:
        ps_xn = ctx.enter_context(nc.psum_tensor("ps_xn_" + name, [P, 2, 512], F32))
        dve_done, var_ready, std_ready = k.sem("dve_done_" + name), k.sem("var_" + name), k.sem("std_" + name)
        tile_ready, pair_ps, pair_sb = k.sem("tile_" + name), k.sem("pair_ps_" + name), k.sem("pair_sb_" + name)

        @block.vector
        def _(dve):
            layer_norm_vector(k, dve, Chain(dve, dve_done), var_ready, std_ready, tile_ready)

        @block.scalar
        def _(act):
            layer_norm_sqrt(k, act, var_ready, std_ready)
            transpose_xn_scalar(k, act, ps_xn, pair_ps, pair_sb)

        @block.tensor
        def _(pe):
            transpose_xn_tensor(k, pe, ps_xn, tile_ready, pair_ps, pair_sb)


def phase_route(k, layer):
    nc = k.nc
    name = f"r{layer}"
    with ExitStack() as ctx:
        def sb(nm, shape, dt=F32):
            return ctx.enter_context(nc.sbuf_tensor(f"{nm}_{name}", shape, dt))
        prob = sb("prob", [P, NT, E])
        stat = sb("stat", [P, NT])
        top = sb("top", [P, NT, E])
        top_i = sb("top_i", [P, NT, E], U32)
        pick = sb("pick", [P, NT, TOP])
        hot = sb("hot", [P, TOP, NT, E])
        both = sb("both", [P, NT, E])
        ahead = sb("ahead", [P, 2, NT, E])
        total = sb("total", [P, NT, E])
        blocks = sb("blocks", [P, E])
        ends = sb("ends", [P, 2, E])
        cmp8 = sb("cmp8", [P, E, E])
        cmpb = sb("cmpb", [P, NB, E])
        slot_f, place = sb("slot_f", [P, TOP, NT]), sb("place", [P, TOP, NT])
        step_f = sb("step_f", [P, ST + 1])
        reach = sb("reach", [P, TOP, NT, ST + 1])
        at_tile = sb("at_tile", [P, TOP, NT, ST])
        tile_hot = sb("tile_hot", [P, TOP, NT, 2, ST], BF16)
        lane_hot = sb("lane_hot", [P, TOP, NT, P], BF16)
        holder, token_f, wrap = sb("holder", [P, ST]), sb("token_f", [P, ST]), sb("wrap", [P, ST])
        ps_i = ctx.enter_context(nc.psum_tensor("ps_i" + name, [P, 512], F32))
        expert_f = sb("expert_f", [P, NB])
        ps_l = ctx.enter_context(nc.psum_tensor("ps_l" + name, [P, 512], F32))
        ps_c = ctx.enter_context(nc.psum_tensor("ps_c" + name, [P, 2, 512], F32))
        logit_ps, shifted, exped = k.sem("logit_ps_" + name), k.sem("shifted_" + name), k.sem("exped_" + name)
        hot_ready, count_ps, diff_ready, diff_exp = (k.sem(s + name) for s in ("hot_", "count_ps_", "diff_", "diff_exp_"))
        dve_done, lanes_ready, holder_ps = k.sem("dve_done_" + name), k.sem("lanes_" + name), k.sem("holder_ps_" + name)
        xn_out = k.sem("xn_out_" + name)
        flat = lambda t: t.rearrange("p n e -> p (n e)")
        with nc.Block() as block:
            @block.tensor
            def _(pe):
                for n in range(NT):
                    for c in range(KC):
                        ins = nc.tensor.matmul(ps_l[:, n * E:(n + 1) * E], k.xnT[:, c, n * P:(n + 1) * P],
                                               k.gate_w[:, layer, c, :], start=(c == 0), stop=(c == KC - 1))
                ins.then_inc(logit_ps, 1)
                pe.wait_ge(hot_ready, 1)
                nc.tensor.matmul(ps_c[:, 0, 0:NT * E], k.before[:], flat(both[:]), start=True, stop=True)
                nc.tensor.matmul(ps_c[:, 1, 0:NT * E], k.ones[:], flat(both[:]), start=True, stop=True).then_inc(count_ps, 1)
                for c in range(TOP):
                    pe.wait_ge(lanes_ready, c + 1)
                    for n in range(NT):
                        ins = nc.tensor.matmul(ps_i[:, 0:2 * ST], lane_hot[:, c, n, :], tile_hot[:, c, n].rearrange("p h t -> p (h t)"),
                                               start=(c == 0 and n == 0), stop=(c == TOP - 1 and n == NT - 1))
                ins.then_inc(holder_ps, 1)

            @block.scalar
            def _(act):
                act.wait_ge(shifted, 1)
                nc.scalar.activation(flat(prob[:]), flat(prob[:]), ACT.Exp).then_inc(exped, 1)
                if layer == 0:
                    act.wait_ge(diff_ready, 1)
                    nc.scalar.activation(k.pair_w[:, :, 1], k.pair_w[:, :, 1], ACT.Exp).then_inc(diff_exp, 1)

            @block.vector
            def _(dve):
                v = nc.vector
                chain = Chain(dve, dve_done)
                link = chain.link
                dve.wait_ge(logit_ps, 1)
                over_e = lambda t: t.rearrange("p (n o) -> p n o", o=1).to_broadcast([P, NT, E])
                link(v.tensor_tensor(prob[:], ps_l[:, 0:NT * E].rearrange("p (n e) -> p n e", e=E),
                                     k.gate_b[:, layer, :].rearrange("p (o e) -> p o e", o=1).to_broadcast([P, NT, E]), ALU.add))
                link(v.tensor_reduce(stat[:], prob[:], AX_X, ALU.max))
                v.tensor_tensor(prob[:], prob[:], over_e(stat[:]), ALU.subtract).then_inc(shifted, 1)
                dve.wait_ge(exped, 1)
                link(v.tensor_reduce(stat[:], prob[:], AX_X, ALU.add))
                link(v.reciprocal(stat[:], stat[:]))
                link(v.tensor_tensor(prob[:], prob[:], over_e(stat[:]), ALU.mult))
                for n in range(NT):
                    chain.did(v.max(top[:, n, :], prob[:, n, :]))
                chain.settle()
                for n in range(NT):
                    chain.did(v.max_index(top_i[:, n, :], top[:, n, :], prob[:, n, :]))
                chain.settle()
                link(v.tensor_copy(pick[:], top_i[:, :, 0:TOP]))
                for c in range(TOP):
                    chain.did(v.tensor_tensor(hot[:, c], pick[:, :, c:c + 1].to_broadcast([P, NT, E]),
                                              k.iota[:, 0:E].rearrange("p (o e) -> p o e", o=1).to_broadcast([P, NT, E]), ALU.is_equal))
                chain.settle()
                v.tensor_tensor(both[:], hot[:, 0], hot[:, 1], ALU.add).then_inc(hot_ready, 1)
                if layer == 0:
                    v.tensor_tensor(k.pair_w[:, :, 1], top[:, :, 1], top[:, :, 0], ALU.subtract).then_inc(diff_ready, 1)
                    dve.wait_ge(diff_exp, 1)
                    link(v.tensor_scalar(stat[:], k.pair_w[:, :, 1], 1.0, None, ALU.add))
                    link(v.reciprocal(k.pair_w[:, :, 0], stat[:]))
                    link(v.tensor_tensor(k.pair_w[:, :, 1], k.pair_w[:, :, 1], k.pair_w[:, :, 0], ALU.mult))
                else:
                    link(v.tensor_tensor(stat[:], top[:, :, 0], top[:, :, 1], ALU.add))
                    link(v.reciprocal(stat[:], stat[:]))
                    for c in range(TOP):
                        chain.did(v.tensor_tensor(k.pair_w[:, :, c], top[:, :, c], stat[:], ALU.mult))
                dve.wait_ge(count_ps, 1)
                chain.did(v.tensor_copy(total[:], ps_c[:, 1, 0:NT * E].rearrange("p (n e) -> p n e", e=E)))
                link(v.tensor_copy(ahead[:, 0], ps_c[:, 1, 0:NT * E].rearrange("p (n e) -> p n e", e=E)))
                side = 0
                for sh in (1, 2, 4, 8):
                    chain.did(v.tensor_copy(ahead[:, 1 - side, 0:sh], ahead[:, side, 0:sh]))
                    link(v.tensor_tensor(ahead[:, 1 - side, sh:NT], ahead[:, side, sh:NT], ahead[:, side, 0:NT - sh], ALU.add))
                    side = 1 - side
                link(v.tensor_scalar(expert_f[:, 0:E], k.iota[:, 0:E], float(BLK), None, ALU.mult))
                link(v.tensor_tensor(cmp8[:], ahead[:, side, NT - 1, :].rearrange("p (e o) -> p e o", o=1).to_broadcast([P, E, E]),
                                     expert_f[:, 0:E].rearrange("p (o b) -> p o b", o=1).to_broadcast([P, E, E]), ALU.is_gt))
                link(v.tensor_reduce(blocks[:], cmp8[:], AX_X, ALU.add))
                link(v.tensor_copy(ends[:, 0], blocks[:]))
                es = 0
                for sh in (1, 2, 4):
                    chain.did(v.tensor_copy(ends[:, 1 - es, 0:sh], ends[:, es, 0:sh]))
                    link(v.tensor_tensor(ends[:, 1 - es, sh:E], ends[:, es, sh:E], ends[:, es, 0:E - sh], ALU.add))
                    es = 1 - es
                link(v.tensor_tensor(blocks[:], ends[:, es], blocks[:], ALU.subtract))
                link(v.tensor_scalar(blocks[:], blocks[:], float(BLK), None, ALU.mult))
                link(v.tensor_tensor(total[:], ahead[:, side], total[:], ALU.subtract))
                link(v.tensor_tensor(total[:], total[:], blocks[:].rearrange("p (o e) -> p o e", o=1).to_broadcast([P, NT, E]), ALU.add))
                link(v.tensor_tensor(total[:], total[:], ps_c[:, 0, 0:NT * E].rearrange("p (n e) -> p n e", e=E), ALU.add))
                for c in range(TOP):
                    link(v.tensor_tensor(hot[:, c], hot[:, c], total[:], ALU.mult))
                    link(v.tensor_reduce(slot_f[:, c, :], hot[:, c], AX_X, ALU.add))
                chain.did(v.tensor_scalar(step_f[:], k.iota[:, 0:ST + 1], float(P), None, ALU.mult))
                chain.settle()
                over = lambda t, n: t.rearrange("p c (n o) -> p c n o", o=1).to_broadcast([P, TOP, NT, n])
                link(v.tensor_tensor(reach[:], over(slot_f[:], ST + 1),
                                     step_f[:].rearrange("p (c n t) -> p c n t", c=1, n=1).to_broadcast([P, TOP, NT, ST + 1]), ALU.is_ge))
                chain.did(v.tensor_tensor(at_tile[:], reach[:, :, :, 0:ST], reach[:, :, :, 1:ST + 1], ALU.subtract))
                link(v.tensor_reduce(place[:], reach[:], AX_X, ALU.add))
                chain.did(v.tensor_scalar(tile_hot[:, :, :, 0, :], at_tile[:], k.lane_id[:, 0:1], None, ALU.mult))
                chain.did(v.tensor_tensor(tile_hot[:, :, :, 1, :], at_tile[:], over(k.tile_id[:], ST), ALU.mult))
                link(v.tensor_scalar(place[:], place[:], -float(P), float(P), ALU.mult, ALU.add))
                link(v.tensor_tensor(place[:], place[:], slot_f[:], ALU.add))
                for c in range(TOP):
                    v.tensor_tensor(lane_hot[:, c], place[:, c, :].rearrange("p (n o) -> p n o", o=1).to_broadcast([P, NT, P]),
                                    k.iota[:].rearrange("p (o t) -> p o t", o=1).to_broadcast([P, NT, P]), ALU.is_equal).then_inc(lanes_ready, 1)
                link(v.tensor_tensor(cmpb[:], k.iota[:, 0:NB].rearrange("p (b o) -> p b o", o=1).to_broadcast([P, NB, E]),
                                     ends[:, es].rearrange("p (o e) -> p o e", o=1).to_broadcast([P, NB, E]), ALU.is_ge))
                link(v.tensor_reduce(expert_f[:], cmpb[:], AX_X, ALU.add))
                link(v.tensor_scalar(expert_f[:], expert_f[:], float(E - 1), None, ALU.min))
                link(v.tensor_copy(k.expert[:], expert_f[:]))
                dve.wait_ge(holder_ps, 1)
                link(v.tensor_copy(token_f[:], ps_i[:, 0:ST]))
                link(v.scalar_tensor_tensor(out=holder[:], in0=ps_i[:, ST:2 * ST], scalar=float(P), in1=token_f[:], op0=ALU.mult, op1=ALU.add))
                link(v.tensor_scalar(wrap[:], holder[:], 0.0, None, ALU.is_equal))
                link(v.tensor_tensor(wrap[:], wrap[:], k.spare[:], ALU.mult))
                chain.did(v.scalar_tensor_tensor(out=k.row_of[:], in0=wrap[:], scalar=-1.0, in1=holder[:], op0=ALU.add, op1=ALU.add))
                link(v.tensor_scalar(token_f[:], holder[:], -1.0, 0.0, ALU.add, ALU.max))
                link(v.tensor_scalar(wrap[:], token_f[:], float(N), -float(N), ALU.is_ge, ALU.mult))
                link(v.tensor_tensor(token_f[:], token_f[:], wrap[:], ALU.add))
                link(v.tensor_copy(k.token_of[:], token_f[:]))

            @block.sync
            def _(sp):
                sp.dma_start(k.xn_dram.rearrange("(n p) d -> p n d", p=P), k.xn[:]).then_inc(xn_out, 16)
                sp.wait_ge(xn_out, 16)


def split_products(nc, out, w_parts, x_parts, start, stop):
    (w_hi, w_lo), (x_hi, x_lo) = w_parts, x_parts
    nc.tensor.matmul(out, w_hi, x_hi, start=start, stop=False)
    nc.tensor.matmul(out, w_hi, x_lo, start=False, stop=False)
    return nc.tensor.matmul(out, w_lo, x_hi, start=False, stop=stop)


def phase_experts(k, layer, w1, w2, b2):
    nc = k.nc
    name = f"x{layer}"
    HC = FT // 2
    PAIRS = FT // 2
    with ExitStack() as ctx:
        def sb(nm, shape, dt=F32):
            return ctx.enter_context(nc.sbuf_tensor(f"{nm}_{name}", shape, dt))
        w1_sb = k.xn[:].rearrange("p (u c m) d -> p u c (m d)", u=2, c=KC)
        w2_sb = k.xnT[:].rearrange("p u (m d) -> p u m d", d=D)
        w1_hi, w1_lo = sb("w1_hi", [P, KC, F], F32R), sb("w1_lo", [P, KC, F], F32R)
        w2_hi, w2_lo = sb("w2_hi", [P, FT, D], F32R), sb("w2_lo", [P, FT, D], F32R)
        b1_sb = sb("b1", [P, 2, FT])
        b2_sb = sb("b2", [P, 2, D])
        rows = sb("rows", [P, 2, BT, D])
        token_now, row_now = sb("token_now", [P, 2, BT], I32), sb("row_now", [P, 2, BT], I32)
        rows_hi, rows_lo = sb("rows_hi", [P, 2, KC, BLK], F32R), sb("rows_lo", [P, 2, KC, BLK], F32R)
        hid = sb("hid", [P, FT, BLK])
        hid_hi, hid_lo = sb("hid_hi", [P, FT, BLK], F32R), sb("hid_lo", [P, FT, BLK], F32R)
        res = sb("res", [P, 2, BT, D])
        ps_t = ctx.enter_context(nc.psum_tensor("ps_t" + name, [P, 512], F32))
        ps_h = ctx.enter_context(nc.psum_tensor("ps_h" + name, [P, FT, BLK], F32))
        ps_y = ctx.enter_context(nc.psum_tensor("ps_y" + name, [P, BT, 512], F32))
        rows_in = [k.sem(f"rows_in{u}_{name}") for u in range(2)]
        w1_in = [k.sem(f"w1_in{u}_{name}") for u in range(2)]
        w2_in = [k.sem(f"w2_in{u}_{name}") for u in range(2)]
        res_out = [k.sem(f"res_out{u}_{name}") for u in range(2)]
        turned, rows_high, rows_split = (k.sem(s + name) for s in ("turned_", "rows_high_", "rows_split_"))
        w1_high, w1_split, w2_high, w2_split = (k.sem(s + name) for s in ("w1_high_", "w1_split_", "w2_high_", "w2_split_"))
        hid_ps, hid_full, hid_high, hid_split = (k.sem(s + name) for s in ("hid_ps_", "hid_full_", "hid_high_", "hid_split_"))
        y_ps, y_sb = k.sem("y_ps_" + name), k.sem("y_sb_" + name)
        picked, rows_picked = k.sem("picked_" + name), k.sem("rows_picked_" + name)

        def run(step, eng):
            step(0, 0, 0, False, False)
            step(1, 1, 0, True, False)
            with eng.Fori(1, NB // 2) as g:
                step(g * 2, 0, g, True, True)
                step(g * 2 + 1, 1, g, True, True)
            if NB % 2:
                step(NB - 1, 0, NB // 2, True, True)

        with nc.Block() as block:
            @block.sync
            def _(sp):
                def step(b, u, past, one, two):
                    e = sp.value_load(k.expert[0:1, ds(b, 1)], min_val=0, max_val=E - 1)
                    if two:
                        sp.wait_ge(w1_split, (b - 1) * 2)
                    sp.dma_start(w1_sb[:, u], w1[ds(e, 1)].rearrange("o (c p) f -> p (o c) f", p=P)).then_inc(w1_in[u], 16)
                    if two:
                        sp.wait_ge(hid_full, (b - 1) * FT)
                    sp.dma_start(b1_sb[:, u, :], k.b1_dram[:, layer, ds(e * FT, FT)]).then_inc(w1_in[u], 16)
                    if two:
                        sp.wait_ge(w2_split, (b - 1) * 2)
                    sp.dma_start(w2_sb[:, u], w2[ds(e, 1)].rearrange("o (m p) d -> p (o m) d", p=P)).then_inc(w2_in[u], 16)
                    if two:
                        sp.wait_ge(y_sb, (b - 1) * BT)
                    sp.dma_start(b2_sb[:, u, :], b2[ds(e, 1), :].to_broadcast([P, D])).then_inc(w2_in[u], 16)
                run(step, sp)

            @block.tensor
            def _(pe):
                def turn(b, u, past, one):
                    pe.wait_ge(rows_in[u], 16 * BT * (past + 1))
                    if one:
                        pe.wait_ge(rows_split, b)
                    for c in range(KC):
                        for s in range(BT):
                            ins = nc.tensor.transpose(ps_t[:, c * BLK + s * P:c * BLK + (s + 1) * P],
                                                      rows[:, u, s, c * P:(c + 1) * P], k.ident[:])
                    ins.then_inc(turned, 1)

                def products(b, u, past, one, more):
                    pe.wait_ge(rows_split, b + 1)
                    for m in range(FT):
                        if m % HC == 0:
                            pe.wait_ge(w1_split, b * 2 + m // HC + 1)
                        if one and m % 2 == 0:
                            pe.wait_ge(hid_full, (b - 1) * FT + m + 2)
                        part = slice(m * P, (m + 1) * P)
                        for c in range(KC):
                            ins = split_products(nc, ps_h[:, m, :], (w1_hi[:, c, part], w1_lo[:, c, part]),
                                                 (rows_hi[:, u, c, :], rows_lo[:, u, c, :]), c == 0, c == KC - 1)
                        if m % 2 == 1:
                            ins.then_inc(hid_ps, 1)
                    if more:
                        turn(b + 1, 1 - u, past + u, True)
                    for m in range(FT):
                        if m % HC == 0:
                            pe.wait_ge(w2_split, b * 2 + m // HC + 1)
                        if m % 2 == 0:
                            pe.wait_ge(hid_split, b * PAIRS + m // 2 + 1)
                        for s in range(BT):
                            if one and m == 0:
                                pe.wait_ge(y_sb, (b - 1) * BT + s + 1)
                            part = slice(s * P, (s + 1) * P)
                            ins = split_products(nc, ps_y[:, s, 0:D], (hid_hi[:, m, part], hid_lo[:, m, part]),
                                                 (w2_hi[:, m, :], w2_lo[:, m, :]), m == 0, m == FT - 1)
                        if m % HC == HC - 1:
                            ins.then_inc(y_ps, 1)

                turn(0, 0, 0, False)
                products(0, 0, 0, False, True)
                products(1, 1, 0, True, True)
                with pe.Fori(1, NB // 2) as g:
                    products(g * 2, 0, g, True, True)
                    products(g * 2 + 1, 1, g, True, True)
                products(NB - 1, 0, NB // 2, True, False)

            @block.scalar
            def _(act):
                def high_w1(b, u, past, one):
                    act.wait_ge(w1_in[u], 32 * (past + 1))
                    for h in range(2):
                        if one:
                            act.wait_ge(hid_ps, (b - 1) * PAIRS + 2 * h + 2)
                        chunk = slice(h * HC * P, (h + 1) * HC * P)
                        nc.scalar.activation(w1_hi[:, :, chunk], w1_sb[:, u, :, chunk], ACT.Copy).then_inc(w1_high, 1)

                def high_w2(b, u, past, h, one):
                    act.wait_ge(w2_in[u], 32 * (past + 1))
                    if one:
                        act.wait_ge(y_ps, (b - 1) * 2 + h + 1)
                    chunk = slice(h * HC, (h + 1) * HC)
                    nc.scalar.activation(w2_hi[:, chunk, :], w2_sb[:, u, chunk, :], ACT.Copy).then_inc(w2_high, 1)

                def high_rows(b, u, two):
                    act.wait_ge(turned, b + 1)
                    if two:
                        act.wait_ge(hid_ps, (b - 1) * PAIRS)
                    nc.scalar.activation(rows_hi[:, u].rearrange("p c t -> p (c t)"), ps_t[:], ACT.Copy).then_inc(rows_high, 1)

                def step(b, u, past, one, two, more=True):
                    for m in range(FT):
                        if m % 2 == 0:
                            act.wait_ge(hid_ps, b * PAIRS + m // 2 + 1)
                            if one:
                                act.wait_ge(hid_split, (b - 1) * PAIRS + m // 2 + 1)
                        nc.scalar.activation(hid[:, m, :], ps_h[:, m, :], ACT.Relu, bias=b1_sb[:, u, m:m + 1]).then_inc(hid_full, 1)
                        if m == 3:
                            high_w2(b, u, past, 1, one)
                    if more:
                        high_rows(b + 1, 1 - u, one)
                        high_w1(b + 1, 1 - u, past + u, True)
                        high_w2(b + 1, 1 - u, past + u, 0, True)

                high_rows(0, 0, False)
                high_w1(0, 0, 0, False)
                high_w2(0, 0, 0, 0, False)
                step(0, 0, 0, False, False)
                step(1, 1, 0, True, False)
                with act.Fori(1, NB // 2) as g:
                    step(g * 2, 0, g, True, True)
                    step(g * 2 + 1, 1, g, True, True)
                step(NB - 1, 0, NB // 2, True, True, more=False)

            @block.vector
            def _(dve):
                v = nc.vector

                def low_rows(b, u):
                    dve.wait_ge(rows_high, b + 1)
                    hi, lo = (t[:, u].rearrange("p c t -> p (c t)") for t in (rows_hi, rows_lo))
                    v.tensor_tensor(lo, ps_t[:], hi.bitcast(F32), ALU.subtract).then_inc(rows_split, 1)

                def low_w1(b, u, past):
                    for h in range(2):
                        dve.wait_ge(w1_high, b * 2 + h + 1)
                        chunk = slice(h * HC * P, (h + 1) * HC * P)
                        v.tensor_tensor(w1_lo[:, :, chunk], w1_sb[:, u, :, chunk], w1_hi[:, :, chunk].bitcast(F32),
                                        ALU.subtract).then_inc(w1_split, 1)

                def low_w2(b, u, h):
                    dve.wait_ge(w2_high, b * 2 + h + 1)
                    chunk = slice(h * HC, (h + 1) * HC)
                    v.tensor_tensor(w2_lo[:, chunk, :], w2_sb[:, u, chunk, :], w2_hi[:, chunk, :].bitcast(F32),
                                    ALU.subtract).then_inc(w2_split, 1)

                def step(b, u, past, one, two, more=True):
                    for q in range(PAIRS):
                        pair = slice(2 * q, 2 * q + 2)
                        dve.wait_ge(hid_full, b * FT + 2 * q + 2)
                        if one and q == 0:
                            dve.wait_ge(y_ps, b * 2)
                        v.tensor_copy(hid_hi[:, pair, :], hid[:, pair, :]).then_inc(hid_high, 1)
                        dve.wait_ge(hid_high, b * PAIRS + q + 1)
                        v.tensor_tensor(hid_lo[:, pair, :], hid[:, pair, :], hid_hi[:, pair, :].bitcast(F32),
                                        ALU.subtract).then_inc(hid_split, 1)
                        if q == 1:
                            low_w2(b, u, 1)
                    if more:
                        low_rows(b + 1, 1 - u)
                        low_w1(b + 1, 1 - u, past + u)
                        low_w2(b + 1, 1 - u, 0)
                    dve.wait_ge(w2_in[u], 32 * (past + 1))
                    dve.wait_ge(y_ps, b * 2 + 2)
                    if two:
                        dve.wait_ge(res_out[u], 16 * BT * past)
                    for s in range(BT):
                        v.tensor_tensor(res[:, u, s, :], ps_y[:, s, 0:D], b2_sb[:, u, :], ALU.add).then_inc(y_sb, 1)

                low_rows(0, 0)
                low_w1(0, 0, 0)
                low_w2(0, 0, 0)
                step(0, 0, 0, False, False)
                step(1, 1, 0, True, False)
                with dve.Fori(1, NB // 2) as g:
                    step(g * 2, 0, g, True, True)
                    step(g * 2 + 1, 1, g, True, True)
                step(NB - 1, 0, NB // 2, True, True, more=False)

            @block.gpsimd
            def _(pool):
                def pick_tokens(b, u, two):
                    if two:
                        pool.wait_ge(turned, b - 1)
                    nc.gpsimd.tensor_copy(token_now[:, u, :], k.token_of[:, ds(b * BT, BT)]).then_inc(picked, 1)

                def gather(b, u):
                    for s in range(BT):
                        pool.indirect_dma_start(out=rows[:, u, s, :], out_offset=None, in_=k.xn_dram,
                                                in_offset=bass.IndirectOffsetOnAxis(ap=token_now[:, u, s:s + 1], axis=0)).then_inc(rows_in[u], 16)

                def step(b, u, past, two, left=3):
                    pool.wait_ge(picked, b + (3 if left >= 2 else 1 + left))
                    if two:
                        pool.wait_ge(res_out[u], 16 * BT * past)
                    nc.gpsimd.tensor_copy(row_now[:, u, :], k.row_of[:, ds(b * BT, BT)]).then_inc(rows_picked, 1)
                    if left >= 2:
                        gather(b + 2, u)
                    pool.wait_ge(rows_picked, b + 1)
                    pool.wait_ge(y_sb, (b + 1) * BT)
                    if left >= 3:
                        pick_tokens(b + 3, 1 - u, True)
                    for s in range(BT):
                        pool.indirect_dma_start(out=k.results, out_offset=bass.IndirectOffsetOnAxis(ap=row_now[:, u, s:s + 1], axis=0),
                                                in_=res[:, u, s, :], in_offset=None).then_inc(res_out[u], 16)

                pick_tokens(0, 0, False)
                pick_tokens(1, 1, False)
                pool.wait_ge(picked, 2)
                gather(0, 0)
                gather(1, 1)
                pick_tokens(2, 0, True)
                step(0, 0, 0, False)
                step(1, 1, 0, False)
                with pool.Fori(1, NB // 2 - 1) as g:
                    step(g * 2, 0, g, True)
                    step(g * 2 + 1, 1, g, True)
                for b in range(NB // 2 * 2 - 2, NB):
                    step(b, b % 2, b // 2, True, left=min(3, NB - 1 - b))
                pool.wait_ge(res_out[0], 16 * BT * (NB // 2 + 1))
                pool.wait_ge(res_out[1], 16 * BT * (NB // 2))


def phase_combine(k, layer, out=None):
    nc = k.nc
    name = f"c{layer}"
    RING, FOUR = 2, 4
    with ExitStack() as ctx, nc.Block() as block:
        got = ctx.enter_context(nc.sbuf_tensor("got_" + name, [P, RING, TOP, FOUR, D], F32))
        fetched = [k.sem(f"fetched{u}_{name}") for u in range(RING)]
        added, stored = k.sem("added_" + name), k.sem("stored_" + name)
        results = k.results[0:TOP * N, :].rearrange("(c n p) d -> p c n d", c=TOP, p=P)

        @block.scalar
        def _(act):
            for q in range(NT // FOUR):
                if q >= RING:
                    act.wait_ge(added, TOP * FOUR * (q - RING + 1))
                for c in range(TOP):
                    act.dma_start(got[:, q % RING, c], results[:, c, FOUR * q:FOUR * q + FOUR, :]).then_inc(fetched[q % RING], 16)

        @block.vector
        def _(dve):
            for q in range(NT // FOUR):
                dve.wait_ge(fetched[q % RING], 16 * TOP * (q // RING + 1))
                for c in range(TOP):
                    for t in range(FOUR):
                        n = FOUR * q + t
                        if c:
                            dve.wait_ge(added, TOP * FOUR * q + t + 1)
                        nc.vector.scalar_tensor_tensor(out=k.x[:, n, :], in0=got[:, q % RING, c, t, :], scalar=k.pair_w[:, n, c:c + 1],
                                                       in1=k.x[:, n, :], op0=ALU.mult, op1=ALU.add).then_inc(added, 1)

        if out is not None:
            ov = out.rearrange("(n p) d -> p n d", p=P)

            @block.sync
            def _(sp):
                for q in range(4):
                    sp.wait_ge(added, TOP * 4 * (q + 1))
                    sp.dma_start(ov[:, 4 * q:4 * q + 4, :], k.x[:, 4 * q:4 * q + 4, :]).then_inc(stored, 16)
                sp.wait_ge(stored, 64)


def phase_gnn1_project(k, I, g):
    nc = k.nc
    with ExitStack() as ctx, nc.Block() as block:
        def sb(name, shape, dt=F32):
            return ctx.enter_context(nc.sbuf_tensor(name, shape, dt))
        head_w = sb("head_w", [P, KC, DH])
        head_v = sb("head_v", [P, KC, 2, DH])
        score_v = sb("score_v", [P, KC, 2])
        junk = sb("junk1", [P, DH])
        f1w = sb("f1w", [P, H, P])
        own_w = sb("own_w", [P, KC, P + 2])
        mlp_rows = sb("mlp_rows", [P, 2, KC, D])
        ps_w = ctx.enter_context(nc.psum_tensor("ps_w", [P, 2, 512], F32))
        ps_p = ctx.enter_context(nc.psum_tensor("ps_p", [P, 2, 512], F32))
        ps_f = ctx.enter_context(nc.psum_tensor("ps_f", [P, 4, 512], F32))
        x_away = k.sem("x_away")
        w_in, zeroed, dve_done, w_ready = k.sem("w_in_p"), k.sem("zeroed_p"), k.sem("dve_done_p"), k.sem("w_ready_p")
        turned, turned_sb, proj_ps, proj_sb = k.sem("turned_p"), k.sem("turned_sb_p"), k.sem("proj_ps_p"), k.sem("proj_sb_p")
        f1_ps, f1_sb, ones_ready = k.sem("f1_ps"), k.sem("f1_sb"), k.sem("ones_ready_p")
        g.f1_sb = f1_sb
        WIN = 6

        @block.sync
        def _(sp):
            sp.dma_start(head_w[:], I["L1_gnn_W"].rearrange("(c g) d e -> (g d) c e", g=2)).then_inc(w_in, 16)
            for half in range(2):
                sp.dma_start(head_v[half * DH:(half + 1) * DH].rearrange("p c s e -> p c (s e)"),
                             I["L1_gnn_V"].rearrange("(c g) s e o -> g c (s e o)", g=2)[half:half + 1].to_broadcast([DH, KC, 2 * DH])).then_inc(w_in, 16)
            sp.dma_start(mlp_rows[:, 0], I["L1_gnn_enc_mlp_W"].rearrange("(c p) n -> p c n", p=P)).then_inc(w_in, 16)
            sp.dma_start(mlp_rows[:, 1], I["L1_gnn_dec_mlp_W"].rearrange("(c p) n -> p c n", p=P)).then_inc(w_in, 16)
            sp.dma_start(k.x_dram, k.x[:]).then_inc(x_away, 16)
            sp.wait_ge(x_away, 16)

        @block.gpsimd
        def _(pool):
            nc.gpsimd.memset(f1w[:], 0.0).then_inc(zeroed, 1)
            nc.gpsimd.memset(own_w[:], 0.0).then_inc(zeroed, 1)
            nc.gpsimd.memset(g.near[:, :, DH:2 * DH], 1.0).then_inc(ones_ready, 1)
            pool.wait_ge(ones_ready, 1)

        @block.vector
        def _(dve):
            v = nc.vector
            chain = Chain(dve, dve_done)
            dve.wait_ge(w_in, 16 * (WIN - 1))
            dve.wait_ge(zeroed, 2)
            for c in range(KC):
                for s in range(2):
                    chain.link(v.tensor_tensor_reduce(out=junk[:], in0=head_w[:, c, :], in1=head_v[:, c, s, :], scale=1.0, scalar=0.0,
                                                      op0=ALU.mult, op1=ALU.add, accum_out=score_v[:, c, s:s + 1]))
            for c in range(KC):
                for q in range(2):
                    part = slice(q * DH, (q + 1) * DH)
                    chain.did(v.tensor_copy(own_w[part, c, q * DH:(q + 1) * DH], head_w[part, c, :]))
                    chain.did(v.tensor_copy(own_w[part, c, P + q:P + q + 1], score_v[part, c, 1:2]))
                    chain.did(v.tensor_scalar(f1w[part, 2 * c + q, :], k.ones[part, :], score_v[part, c, 0:1], None, ALU.mult))
            chain.settle()
            v.engine_nop().then_inc(w_ready, 1)
            for n in range(NT):
                dve.wait_ge(proj_ps, n + 1)
                pv = ps_p[:, n % 2, 0:KC * (P + 2)].rearrange("p (c w) -> p c w", c=KC)
                v.tensor_copy(k.xn[:, n, :].rearrange("p (c w) -> p c w", c=KC), pv[:, :, 0:P]).then_inc(dve_done, 1)
                v.tensor_scalar(g.f2_half[:, n, :].rearrange("p (c w) -> p c w", c=KC), pv[:, :, P:P + 2], 0.5, None,
                                ALU.mult).then_inc(proj_sb, 1)

        @block.tensor
        def _(pe):
            pe.wait_ge(w_in, 16 * (WIN - 1))
            pe.wait_ge(w_ready, 1)
            for l in range(2):
                if l:
                    pe.wait_ge(turned_sb, l)
                for kc in range(KC):
                    for oc in range(KC):
                        ins = nc.tensor.transpose(ps_w[:, 0, kc * D + oc * P:kc * D + (oc + 1) * P], mlp_rows[:, l, oc, kc * P:(kc + 1) * P], k.ident[:])
                ins.then_inc(turned, 1)
            for c in range(KC):
                ins = nc.tensor.transpose(ps_w[:, 1, c * P:(c + 1) * P], own_w[:, c, 0:P], k.ident[:])
            ins.then_inc(turned, 1)
            for n in range(NT):
                if n >= 2:
                    pe.wait_ge(proj_sb, n - 1)
                for c in range(KC):
                    ins = nc.tensor.matmul(ps_p[:, n % 2, c * (P + 2):(c + 1) * (P + 2)], k.xnT[:, c, n * P:(n + 1) * P], own_w[:, c, :],
                                           start=True, stop=True)
                ins.then_inc(proj_ps, 1)
            for h in range(H):
                for q in range(4):
                    if h:
                        pe.wait_ge(f1_sb, 4 * (h - 1) + q + 1)
                    nc.tensor.matmul(ps_f[:, q, :], f1w[:, h, :], k.xnT[:, h // 2, q * 512:(q + 1) * 512],
                                     start=True, stop=True).then_inc(f1_ps, 1)

        @block.scalar
        def _(act):
            s = nc.scalar
            for l in range(2):
                act.wait_ge(turned, l + 1)
                s.activation(g.mlp_wT[:, l].rearrange("p c n -> p (c n)"), ps_w[:, 0, :], ACT.Copy).then_inc(turned_sb, 1)
            act.wait_ge(turned, 3)
            s.activation(g.head_wT[:].rearrange("p c n -> p (c n)"), ps_w[:, 1, 0:KC * P], ACT.Copy).then_inc(turned_sb, 1)
            for h in range(H):
                for q in range(4):
                    act.wait_ge(f1_ps, 4 * h + q + 1)
                    s.activation(g.f1[:, h, q * 512:(q + 1) * 512], ps_f[:, q, :], ACT.Copy).then_inc(f1_sb, 1)


def phase_attend(k, g, name, first):
    nc = k.nc
    KEPT = g.KEPT
    M = len(KEPT)
    computed = [j for j in range(NT) if first or j not in KEPT]
    C = len(computed)
    steps = [(q, j) for q in range(2) for j in range(NT)]

    def nth(q, j):
        return q * C + computed.index(j)

    def nth_kept(q, j):
        return q * M + KEPT.index(j)

    with ExitStack() as ctx, nc.Block() as block:
        ps = ctx.enter_context(nc.psum_tensor("ps_att_" + name, [P, 2, N], F32))
        tanh_ready, exp_ready, edge_ready, edge_free = (k.sem(s + name) for s in ("tanh_", "exp_", "edge_r_", "edge_f_"))
        near_ready, sum_free, inv_done = k.sem("near_" + name), k.sem("sum_free_" + name), k.sem("inv_" + name)
        divided, kept_free = k.sem("divided_" + name), k.sem("kept_f_" + name)
        kept_moved = [k.sem(f"kept_moved{u}_{name}") for u in range(2)]

        @block.sync
        def _(sp):
            with sp.Fori(0, H // 2) as hp:
                for q in range(2):
                    for j in KEPT:
                        m = nth_kept(q, j)
                        if first:
                            sp.wait_ge(edge_ready, hp * (2 * NT) + (q * NT + j + 1))
                            sp.dma_start(k.kept_dram[ds(hp * (2 * M) + m, 1)].rearrange("o p t -> p (o t)"), g.kept[:, m % 2, :]).then_inc(kept_moved[m % 2], 16)
                        else:
                            sp.wait_ge(kept_free, hp * (2 * M) + (m + 1))
                            sp.dma_start(g.kept[:, m % 2, :], k.kept_dram[ds(hp * (2 * M) + m, 1)].rearrange("o p t -> p (o t)")).then_inc(kept_moved[m % 2], 16)
            for u in range(2):
                sp.wait_ge(kept_moved[u], 16 * H * M // 2)

        @block.scalar
        def _(act):
            with act.Fori(0, H // 2) as hp:
                def tanh_of(q, j):
                    c = nth(q, j)
                    act.wait_ge(g.f1_sb, 4 * H)
                    act.wait_ge(edge_free, hp * (2 * C) + (c + 1))
                    nc.scalar.activation(g.edge[:, c % g.RING, :], g.f1[:, ds(hp * 2 + q, 1), :].rearrange("p o t -> p (o t)"), ACT.Tanh,
                                         scale=0.5, bias=g.f2_half[:, j, ds(hp * 2 + q, 1)]).then_inc(tanh_ready, 1)

                def exp_of(q, j):
                    c = nth(q, j)
                    act.wait_ge(tanh_ready, hp * (2 * C) + (c + 1))
                    nc.scalar.activation(g.edge[:, c % g.RING, :], g.edge[:, c % g.RING, :], ACT.Exp, scale=0.5).then_inc(exp_ready, 1)

                mine = [(q, j) for q in range(2) for j in computed]
                tanh_of(*mine[0])
                for i, (q, j) in enumerate(mine):
                    if i + 1 < len(mine):
                        tanh_of(*mine[i + 1])
                    exp_of(q, j)

        @block.gpsimd
        def _(pool):
            with pool.Fori(0, H // 2) as hp:
                for i, (q, j) in enumerate(steps):
                    qq, jj = steps[i - g.RING]
                    wrap = 1 if i < g.RING else 0
                    if jj in computed:
                        pool.wait_ge(edge_free, hp * (2 * C) + (nth(qq, jj) - wrap * 2 * C + 1 + g.RING))
                    else:
                        pool.wait_ge(kept_free, hp * (2 * M) + (nth_kept(qq, jj) - wrap * 2 * M + 1 + 2))
                    nc.gpsimd.tensor_copy(g.near[:, j % g.RING, 0:DH], k.xn[:, j, ds((hp * 2 + q) * DH, DH)]).then_inc(near_ready, 1)

        @block.tensor
        def _(pe):
            pe.sem_inc(edge_free, g.RING)
            pe.sem_inc(kept_free, 2)
            with pe.Fori(0, H // 2) as hp:
                for q, j in steps:
                    if j == 0:
                        pe.wait_ge(sum_free, hp * 2 + (q + 1))
                    pe.wait_ge(near_ready, hp * (2 * NT) + (q * NT + j + 1))
                    if j in computed:
                        pe.wait_ge(edge_ready, hp * (2 * C) + (nth(q, j) + 1))
                    else:
                        m = nth_kept(q, j)
                        pe.wait_ge(kept_moved[m % 2], hp * (16 * M) + 16 * (m // 2 + 1))
                    edge = g.kept[:, nth_kept(q, j) % 2, :] if j in KEPT else g.edge[:, nth(q, j) % g.RING, :]
                    for i in range(4):
                        chunk = slice(i * 512, (i + 1) * 512)
                        if first:
                            ins = nc.tensor.matmul(ps[:, q, chunk], g.near[:, j % g.RING, :], edge[:, chunk],
                                                   start=(j == 0), stop=(j == NT - 1))
                        else:
                            half = slice(i % 2 * DH, i % 2 * DH + DH)
                            ins = nc.tensor.matmul(ps[half, q, chunk], g.near[:, j % g.RING, 0:DH], edge[:, chunk],
                                                   start=(j == 0), stop=(j == NT - 1))
                    ins.then_inc(edge_free if j in computed else kept_free, 1)

        @block.vector
        def _(dve):
            v = nc.vector
            dve.sem_inc(sum_free, 2)
            chain = Chain(dve, inv_done)
            CH = 256

            def copy_out(hp, q):
                dve.wait_ge(edge_free, (2 * hp + q + 1) * C + g.RING)
                rows = slice(q * DH, (q + 1) * DH)
                if first:
                    chain.did(v.tensor_scalar(g.inv[rows, hp, :], ps[DH:2 * DH, q, :], 1e-30, None, ALU.max))
                    v.tensor_copy(k.xnT[rows, hp, :], ps[0:DH, q, :]).then_inc(sum_free, 1)
                else:
                    chunks = lambda t, odd: t.rearrange("p (a b t) -> p a b t", b=2, t=512)[:, :, odd, :]
                    for odd in range(2):
                        ins = v.tensor_tensor(chunks(k.xnT[rows, hp, :], odd), chunks(ps[odd * DH:(odd + 1) * DH, q, :], odd),
                                              chunks(g.inv[rows, hp, :], odd), ALU.mult)
                    ins.then_inc(sum_free, 1)

            def invert(hp, piece):
                part = slice(piece * CH, (piece + 1) * CH)
                chain.did(v.reciprocal(g.inv[:, hp, part], g.inv[:, hp, part]))

            def divide(hp):
                chain.settle()
                dve.wait_ge(sum_free, 2 * hp + 4)
                v.tensor_tensor(k.xnT[:, hp, :], k.xnT[:, hp, :], g.inv[:, hp, :], ALU.mult).then_inc(divided, 1)

            for h in range(H):
                for turn, j in enumerate(computed):
                    n = h * C + turn
                    dve.wait_ge(exp_ready, n + 1)
                    slot = g.edge[:, n % g.RING, :]
                    masked = slot
                    if j in KEPT:
                        m = h * M + KEPT.index(j)
                        masked = g.kept[:, m % 2, :]
                        if m >= 2:
                            last = (m - 2) // M * NT + KEPT[(m - 2) % M]
                            dve.wait_ge(edge_free, last + 1 + g.RING)
                            dve.wait_ge(kept_moved[m % 2], 16 * (m // 2))
                    v.tensor_tensor(masked, slot, k.adjT[:, j, :], ALU.mult).then_inc(edge_ready, 1)
                    if h and turn == 2:
                        copy_out((h - 1) // 2, (h - 1) % 2)
                        chain.settle()
                    if first and h == 2 and 4 <= turn < 4 + N // CH:
                        invert(0, turn - 4)
                    if first and h == 2 and turn == 4 + N // CH:
                        divide(0)
            copy_out(1, 1)
            if first:
                chain.settle()
                for piece in range(N // CH):
                    invert(1, piece)
                divide(1)


def phase_mlp(k, g, name, layer, pre_gamma, bias, gamma):
    nc = k.nc
    CH = 512
    pieces = [(q, c) for q in range(N // CH) for c in range(KC)]
    with ExitStack() as ctx, nc.Block() as block:
        stats = ctx.enter_context(nc.sbuf_tensor("stats_" + name, [P, KC, N // CH, 6], F32))
        mv = ctx.enter_context(nc.sbuf_tensor("mv_" + name, [P, KC, 2], F32))
        var = ctx.enter_context(nc.sbuf_tensor("var_" + name, [P, KC], F32))
        std = ctx.enter_context(nc.sbuf_tensor("std_" + name, [P, KC], F32))
        tmp = ctx.enter_context(nc.sbuf_tensor("tmp_" + name, [P, KC], F32))
        scale = ctx.enter_context(nc.sbuf_tensor("scale_" + name, [P, KC], F32))
        shift = ctx.enter_context(nc.sbuf_tensor("shift_" + name, [P, KC], F32))
        ps = ctx.enter_context(nc.psum_tensor("ps_mlp_" + name, [P, KC, N], F32))
        dve_done, var_ready, std_ready = k.sem("dve_done_" + name), k.sem("var_" + name), k.sem("std_" + name)
        neg_ready, neg_exp, x_ready, mlp_ps = k.sem("neg_" + name), k.sem("neg_exp_" + name), k.sem("x_ready_" + name), k.sem("mlp_ps_" + name)
        biased, upper_ready, sum_ready = k.sem("biased_" + name), k.sem("upper_" + name), k.sem("sum_" + name)
        low, high = g.edge[:, 0:KC, :], g.edge[:, KC:2 * KC, :]
        pre_elu = pre_gamma is None
        past = len(pieces) if pre_elu else 0
        part = lambda t, q, c: t[:, c, q * CH:(q + 1) * CH]
        if pre_elu:
            x_back = k.sem("x_back")

            @block.sync
            def _(sp):
                sp.dma_start(k.x[:], k.x_dram).then_inc(x_back, 16)
                sp.wait_ge(x_back, 16)

        @block.vector
        def _(dve):
            v = nc.vector
            chain = Chain(dve, dve_done)
            link = chain.link
            norms = [0]

            def piece_stats(src, q, c):
                chain.did(v.bn_stats(stats[:, c, q, :], part(src, q, c)))

            def scale_and_shift(col):
                chain.settle()
                for c in range(KC):
                    chain.did(v.bn_aggr(mv[:, c, :], stats[:, c]))
                chain.settle()
                v.tensor_scalar(var[:], mv[:, :, 1], BN_EPS, None, ALU.add).then_inc(var_ready, 1)
                norms[0] += 1
                dve.wait_ge(std_ready, norms[0])
                link(v.reciprocal(scale[:], std[:]))
                rstd_of(chain, v, scale[:], var[:], tmp[:], None)
                link(v.tensor_tensor(scale[:], scale[:], k.vec[:, col:col + KC], ALU.mult))
                link(v.tensor_tensor(shift[:], mv[:, :, 0], scale[:], ALU.mult))
                link(v.tensor_tensor(shift[:], k.vec[:, col + KC:col + 2 * KC], shift[:], ALU.subtract))

            if pre_elu:
                maxed = {}

                def open_elu(i):
                    x = part(k.xnT, *pieces[i])
                    v.tensor_scalar(part(low, *pieces[i]), x, 0.0, None, ALU.min).then_inc(neg_ready, 1)
                    chain.did(v.tensor_scalar(x, x, 0.0, None, ALU.max))
                    maxed[i] = chain.count

                open_elu(0)
                for i in range(len(pieces)):
                    if i + 1 < len(pieces):
                        open_elu(i + 1)
                    x = part(k.xnT, *pieces[i])
                    dve.wait_ge(dve_done, maxed[i])
                    dve.wait_ge(neg_exp, i + 1)
                    v.scalar_tensor_tensor(out=x, in0=part(low, *pieces[i]), scalar=-1.0, in1=x, op0=ALU.add, op1=ALU.add).then_inc(x_ready, 1)
            else:
                for q, c in pieces:
                    piece_stats(k.xnT, q, c)
                scale_and_shift(pre_gamma)
                for q, c in pieces:
                    x = part(k.xnT, q, c)
                    v.tensor_scalar(x, x, scale[:, c:c + 1], shift[:, c:c + 1], ALU.mult, ALU.add).then_inc(x_ready, 1)

            def lower(i):
                q, c = pieces[i]
                dve.wait_ge(biased, i + 1)
                if pre_elu and i == 0:
                    dve.wait_ge(x_ready, len(pieces))
                v.tensor_scalar(part(low, q, c), part(high, q, c), 0.0, None, ALU.min).then_inc(neg_ready, 1)
                v.tensor_scalar(part(high, q, c), part(high, q, c), 0.0, None, ALU.max).then_inc(upper_ready, 1)

            summed = {}
            lower(0)
            for i in range(len(pieces)):
                if i + 1 < len(pieces):
                    lower(i + 1)
                y = part(high, *pieces[i])
                dve.wait_ge(sum_ready, i + 1)
                dve.wait_ge(neg_exp, past + i + 1)
                chain.did(v.scalar_tensor_tensor(out=y, in0=part(low, *pieces[i]), scalar=-1.0, in1=y, op0=ALU.add, op1=ALU.add))
                summed[i] = chain.count
                if i:
                    dve.wait_ge(dve_done, summed[i - 1])
                    piece_stats(high, *pieces[i - 1])
            chain.settle()
            piece_stats(high, *pieces[-1])
            scale_and_shift(gamma)
            for c in range(KC):
                chain.did(v.tensor_scalar(k.xnT[:, c, :], high[:, c, :], scale[:, c:c + 1], shift[:, c:c + 1], ALU.mult, ALU.add))
            chain.settle()

        @block.scalar
        def _(act):
            s = nc.scalar
            if pre_elu:
                for i in range(len(pieces)):
                    act.wait_ge(neg_ready, i + 1)
                    s.activation(part(low, *pieces[i]), part(low, *pieces[i]), ACT.Exp).then_inc(neg_exp, 1)
            else:
                act.wait_ge(var_ready, 1)
                s.activation(std[:], var[:], ACT.Sqrt).then_inc(std_ready, 1)
            def add_bias(i):
                q, c = pieces[i]
                act.wait_ge(mlp_ps, i + 1)
                s.activation(part(high, q, c), part(ps, q, c), ACT.Identity, bias=k.vec[:, bias + c:bias + c + 1]).then_inc(biased, 1)

            add_bias(0)
            for i, (q, c) in enumerate(pieces):
                if i + 1 < len(pieces):
                    add_bias(i + 1)
                act.wait_ge(neg_ready, past + i + 1)
                s.activation(part(low, q, c), part(low, q, c), ACT.Exp).then_inc(neg_exp, 1)
            act.wait_ge(var_ready, 1 if pre_elu else 2)
            s.activation(std[:], var[:], ACT.Sqrt).then_inc(std_ready, 1)

        @block.gpsimd
        def _(pool):
            for i, (q, c) in enumerate(pieces):
                pool.wait_ge(upper_ready, i + 1)
                y = part(high, q, c)
                nc.gpsimd.tensor_tensor(y, y, part(k.xnT, q, c), ALU.add).then_inc(sum_ready, 1)

        @block.tensor
        def _(pe):
            for q, c in pieces:
                pe.wait_ge(x_ready, KC * (q + 1))
                for kc in range(KC):
                    ins = nc.tensor.matmul(part(ps, q, c), g.mlp_wT[:, layer, kc, c * P:(c + 1) * P], part(k.xnT, q, kc),
                                           start=(kc == 0), stop=(kc == KC - 1))
                ins.then_inc(mlp_ps, 1)


def phase_back(k, g):
    nc = k.nc
    with ExitStack() as ctx, nc.Block() as block:
        ps = ctx.enter_context(nc.psum_tensor("ps_back", [P, 4, 512], F32))
        back_ps, back_sb = k.sem("back_ps"), k.sem("back_sb")

        @block.tensor
        def _(pe):
            for n in range(NT):
                if n >= 4:
                    pe.wait_ge(back_sb, n - 3)
                for c in range(KC):
                    ins = nc.tensor.matmul(ps[:, n % 4, c * P:(c + 1) * P], k.xnT[:, c, n * P:(n + 1) * P], g.head_wT[:, c, :],
                                           start=True, stop=True)
                ins.then_inc(back_ps, 1)

        @block.scalar
        def _(act):
            for n in range(NT):
                act.wait_ge(back_ps, n + 1)
                nc.scalar.activation(k.xn[:, n, :], ps[:, n % 4, 0:D], ACT.Copy).then_inc(back_sb, 1)


def phase_residual(k):
    nc = k.nc
    with ExitStack() as ctx, nc.Block() as block:
        ps = ctx.enter_context(nc.psum_tensor("ps_res", [P, 4, 512], F32))
        res_ps, res_sb = k.sem("res_ps"), k.sem("res_sb")

        @block.tensor
        def _(pe):
            for n in range(NT):
                if n >= 4:
                    pe.wait_ge(res_sb, n - 3)
                for c in range(KC):
                    ins = nc.tensor.transpose(ps[:, n % 4, c * P:(c + 1) * P], k.xnT[:, c, n * P:(n + 1) * P], k.ident[:])
                ins.then_inc(res_ps, 1)

        @block.vector
        def _(dve):
            for n in range(NT):
                dve.wait_ge(res_ps, n + 1)
                nc.vector.tensor_tensor(k.x[:, n, :], k.x[:, n, :], ps[:, n % 4, 0:D], ALU.add).then_inc(res_sb, 1)


def gnn1(k, I):
    nc = k.nc
    with ExitStack() as ctx:
        def sb(name, shape, dt=F32):
            return ctx.enter_context(nc.sbuf_tensor(name, shape, dt))
        g = Shared()
        g.RING = 4
        g.KEPT = list(range(1, NT - g.RING, 2))
        k.kept_dram = nc.dram_tensor("kept_dram", [H * len(g.KEPT), P, N], F32).ap()
        k.x_dram = nc.dram_tensor("x_dram", [P, NT, D], F32).ap()
        g.kept = k.x[:].rearrange("p (u m) d -> p u (m d)", u=2)
        g.f1 = sb("f1", [P, H, N])
        g.f2_half = sb("f2_half", [P, NT, H])
        g.mlp_wT = sb("mlp_wT", [P, 2, KC, D])
        g.head_wT = sb("head_wT", [P, KC, P])
        g.near = sb("near", [P, g.RING, 2 * DH])
        phase_gnn1_project(k, I, g)
        g.edge = sb("edge", [P, g.RING, N])
        g.inv = sb("inv1", [P, KC, N])
        phase_attend(k, g, "enc", True)
        phase_mlp(k, g, "enc_mlp", 0, VEC_COL["L1_gnn_enc_bn_gamma"], VEC_COL["L1_gnn_enc_mlp_b"], VEC_COL["L1_gnn_enc_mlp_bn_gamma"])
        phase_back(k, g)
        phase_attend(k, g, "dec", False)
        phase_mlp(k, g, "dec_mlp", 1, None, VEC_COL["L1_gnn_dec_mlp_b"], VEC_COL["L1_gnn_dec_mlp_bn_gamma"])
        phase_residual(k)


def build(nc, I, out, stop=99):
    with ExitStack() as ctx:
        def sb(name, shape, dt=F32):
            return ctx.enter_context(nc.sbuf_tensor(name, shape, dt))
        k = Shared()
        k.nc, k.sems = nc, []

        def new_sem(name):
            k.sems.append(nc.alloc_semaphore(name=name))
            return k.sems[-1]

        def clear_sems():
            nc.clear_and_free_semaphores(k.sems)
            nc.all_engine_barrier()
            k.sems = []

        k.sem = new_sem
        k.xn_dram = nc.dram_tensor("xn_dram", [N, D], F32).ap()
        k.results = nc.dram_tensor("results", [TOP * N + NB * BLK, D], F32).ap()
        k.b1_dram = nc.dram_tensor("b1_dram", [P, 2, E * FT], F32).ap()
        k.x = sb("x", [P, NT, D])
        k.xn = sb("xn", [P, NT, D])
        k.xnT = sb("xnT", [P, KC, N])
        k.adjT = sb("adjT", [P, NT, N], BF16)
        k.ident, k.ones, k.before = sb("ident", [P, P]), sb("ones", [P, P]), sb("before", [P, P])
        k.iota = sb("iota", [P, P])
        k.lane_id, k.tile_id, k.spare = sb("lane_id", [P, 1]), sb("tile_id", [P, TOP, NT]), sb("spare", [P, ST])
        k.vec = sb("vec", [P, VEC_ROWS])
        k.gate_w, k.gate_b = sb("gate_w", [P, 2, KC, E]), sb("gate_b", [P, 2, E])
        k.ln_stats, k.ln_mv = sb("ln_stats", [P, NT, 6]), sb("ln_mv", [P, NT, 2])
        k.ln_var, k.ln_std, k.ln_rstd, k.ln_tmp = (sb(n, [P, NT]) for n in ("ln_var", "ln_std", "ln_rstd", "ln_tmp"))
        k.pair_w = sb("pair_w", [P, NT, TOP])
        k.token_of = sb("token_of", [P, ST], I32)
        k.row_of = sb("row_of", [P, ST], I32)
        k.expert = sb("expert", [P, NB], I32)

        with ExitStack() as gctx:
            k.w_cat = gctx.enter_context(nc.sbuf_tensor("w_cat", [P, KC, 2 * D], F32))
            k.a_sa = gctx.enter_context(nc.sbuf_tensor("a_sa", [P, 2 * D], F32))
            k.b_gcnb = gctx.enter_context(nc.sbuf_tensor("b_gcnb", [P, D], F32))
            k.type_bias = gctx.enter_context(nc.sbuf_tensor("type_bias", [P, 2], F32))
            phase_load(k, I)
            if stop > 1:
                phase_gnn0(k, I)
        if stop > 2:
            block_norm(k, "n1")
            phase_route(k, 0)
        if stop > 3:
            phase_experts(k, 0, I["L0_ffn_w1"], I["L0_ffn_w2"], I["L0_ffn_b2"])
        if stop > 4:
            phase_combine(k, 0)
            clear_sems()
        if stop > 5:
            block_norm(k, "n2")
            gnn1(k, I)
        if stop > 6:
            block_norm(k, "n3")
            phase_route(k, 1)
            phase_experts(k, 1, I["L1_ffn_W1"], I["L1_ffn_W2"], I["L1_ffn_b2"])
            phase_combine(k, 1, out)


INPUTS = ["x", "adj", "L0_gnn_W_sa", "L0_gnn_a_sa", "L0_gnn_W_gcnb", "L0_gnn_b_gcnb", "L0_gnn_Wa", "L0_gnn_ba", "L0_gnn_Wb", "L0_gnn_bb",
          "L0_ffn_gate_w", "L0_ffn_gate_b", "L0_ffn_w1", "L0_ffn_b1", "L0_ffn_w2", "L0_ffn_b2", "L1_gnn_W", "L1_gnn_V",
          "L1_gnn_enc_bn_gamma", "L1_gnn_enc_bn_beta", "L1_gnn_enc_mlp_W", "L1_gnn_enc_mlp_b", "L1_gnn_enc_mlp_bn_gamma",
          "L1_gnn_enc_mlp_bn_beta", "L1_gnn_dec_mlp_W", "L1_gnn_dec_mlp_b", "L1_gnn_dec_mlp_bn_gamma", "L1_gnn_dec_mlp_bn_beta",
          "L1_ffn_Wg", "L1_ffn_bg", "L1_ffn_W1", "L1_ffn_b1", "L1_ffn_W2", "L1_ffn_b2"]


def kernel(**inputs):
    import numpy as np
    import concourse.bacc as bacc
    from concourse.bass_utils import run_bass_kernel_spmd

    nc = bacc.Bacc("TRN2", target_bir_lowering=False, num_devices=1)
    arrays, aps = {}, {}
    for name in INPUTS:
        a = np.ascontiguousarray(inputs[name])
        arrays[f"in_{name}"] = a
        aps[name] = nc.dram_tensor(f"in_{name}", a.shape, mybir.dt.from_np(a.dtype), kind="ExternalInput").ap()
    out = nc.dram_tensor("out", (N, D), F32, kind="ExternalOutput").ap()
    build(nc, aps, out)
    result = run_bass_kernel_spmd(nc, [arrays], core_ids=[0])
    return result.results[0]["out"]
```

```python
from contextlib import ExitStack

import concourse.bass as bass
from concourse import mybir

F32 = mybir.dt.float32
BF16 = mybir.dt.bfloat16
F32R = mybir.dt.float32r
I32 = mybir.dt.int32
U32 = mybir.dt.uint32
ALU = mybir.AluOpType
ACT = mybir.ActivationFunctionType
AX_X = mybir.AxisListType.X

P = 128
N = 2048
NT = N // P
D = 256
KC = D // P
E = 8
F = 1024
FT = F // P
TOP = 2
BLK = 256
BT = BLK // P
NB = (TOP * N + E * (BLK - 1)) // BLK
ST = NB * BT
H = 4
DH = D // H
LN_EPS = 1e-5
BN_EPS = 1e-6
ds = bass.ds

VEC_NAMES = ["L1_gnn_enc_bn_gamma", "L1_gnn_enc_bn_beta", "L1_gnn_enc_mlp_b", "L1_gnn_enc_mlp_bn_gamma",
             "L1_gnn_enc_mlp_bn_beta", "L1_gnn_dec_mlp_b", "L1_gnn_dec_mlp_bn_gamma", "L1_gnn_dec_mlp_bn_beta"]
VEC_COL = {name: 8 + KC * i for i, name in enumerate(VEC_NAMES)}
VEC_ROWS = 8 + KC * len(VEC_NAMES)


class Shared:
    pass


class Chain:

    def __init__(self, eng, sem):
        self.eng, self.sem, self.count = eng, sem, 0

    def did(self, ins):
        ins.then_inc(self.sem, 1)
        self.count += 1

    def settle(self):
        self.eng.wait_ge(self.sem, self.count)

    def link(self, ins):
        self.did(ins)
        self.settle()


def rstd_of(chain, nc_vector, out, var, tmp, sqrt_wait):
    chain.link(nc_vector.tensor_tensor(tmp, out, out, ALU.mult))
    chain.link(nc_vector.tensor_tensor(tmp, tmp, var, ALU.mult))
    chain.link(nc_vector.tensor_scalar(tmp, tmp, -0.5, 1.5, ALU.mult, ALU.add))
    chain.link(nc_vector.tensor_tensor(out, out, tmp, ALU.mult))


def layer_norm_vector(k, dve, chain, var_ready, std_ready, tile_ready, x_ready=None, stats_taken=False):
    v = k.nc.vector
    if not stats_taken:
        for n in range(NT):
            if x_ready is not None and n % 4 == 0:
                dve.wait_ge(x_ready[n // 4], 16)
            chain.did(v.bn_stats(k.ln_stats[:, n, :], k.x[:, n, :]))
        chain.settle()
    for n in range(NT):
        chain.did(v.bn_aggr(k.ln_mv[:, n, :], k.ln_stats[:, n, :]))
    chain.settle()
    v.tensor_scalar(k.ln_var[:], k.ln_mv[:, :, 1], LN_EPS, None, ALU.add).then_inc(var_ready, 1)
    dve.wait_ge(std_ready, 1)
    chain.link(v.reciprocal(k.ln_rstd[:], k.ln_std[:]))
    rstd_of(chain, v, k.ln_rstd[:], k.ln_var[:], k.ln_tmp[:], None)
    for n in range(NT):
        v.tensor_scalar(k.xn[:, n, :], k.x[:, n, :], k.ln_mv[:, n, 0:1], k.ln_rstd[:, n:n + 1],
                        ALU.subtract, ALU.mult).then_inc(tile_ready, 1)


def layer_norm_sqrt(k, act, var_ready, std_ready):
    act.wait_ge(var_ready, 1)
    k.nc.scalar.activation(k.ln_std[:], k.ln_var[:], ACT.Sqrt).then_inc(std_ready, 1)


def transpose_xn_tensor(k, pe, ps, tile_ready, pair_ps, pair_sb, use=None):
    for q in range(NT // 2):
        pe.wait_ge(tile_ready, 2 * q + 2)
        if q >= 2:
            pe.wait_ge(pair_sb, q - 1)
        for c in range(KC):
            for t in range(2):
                ins = k.nc.tensor.transpose(ps[:, q % 2, c * 2 * P + t * P:c * 2 * P + (t + 1) * P],
                                            k.xn[:, 2 * q + t, c * P:(c + 1) * P], k.ident[:])
        ins.then_inc(pair_ps, 1)
        if use is not None and q:
            use(q - 1)


def transpose_xn_scalar(k, act, ps, pair_ps, pair_sb):
    for q in range(NT // 2):
        act.wait_ge(pair_ps, q + 1)
        k.nc.scalar.activation(k.xnT[:, :, q * 2 * P:(q + 1) * 2 * P],
                               ps[:, q % 2, :].rearrange("p (c t) -> p c t", c=KC), ACT.Copy).then_inc(pair_sb, 1)


def phase_load(k, I):
    nc = k.nc
    RING = 8
    with ExitStack() as ctx:
        adj_rows = ctx.enter_context(nc.sbuf_tensor("adj_rows", [P, RING, N], F32))
        vec_rows = ctx.enter_context(nc.sbuf_tensor("vec_rows", [VEC_ROWS, P], F32))
        b1_rows = ctx.enter_context(nc.sbuf_tensor("b1_rows", [E * FT, 2, P], F32))
        iota_i = ctx.enter_context(nc.sbuf_tensor("iota_i", [P, P], I32))
        lane_i = ctx.enter_context(nc.sbuf_tensor("lane_i", [P, 1], I32))
        tile_i = ctx.enter_context(nc.sbuf_tensor("tile_i", [P, TOP * NT], I32))
        spare_i = ctx.enter_context(nc.sbuf_tensor("spare_i", [P, ST], I32))
        b1_cols = ctx.enter_context(nc.sbuf_tensor("b1_cols", [P, 2, E * FT], F32))
        ps_adj = ctx.enter_context(nc.psum_tensor("ps_adj", [P, 4, 512], F32))
        ps_xn = ctx.enter_context(nc.psum_tensor("ps_xn_a", [P, 2, 512], F32))
        ps_vec = ctx.enter_context(nc.psum_tensor("ps_vec", [P, 512], F32))
        x_in = [k.sem(f"x_in{q}") for q in range(4)]
        small_in, rows_in = k.sem("small_in"), k.sem("rows_in")
        adj_in = [k.sem(f"adj_in{u}") for u in range(RING)]
        consts, adj_ps, adj_sb_act, adj_sb_dve = k.sem("consts"), k.sem("adj_ps"), k.sem("adj_sb_act"), k.sem("adj_sb_dve")
        vec_ps, vec_sb, b1_sb, b1_out = k.sem("vec_ps"), k.sem("vec_sb"), k.sem("b1_sb"), k.sem("b1_out")
        dve_done, var_ready, std_ready = k.sem("dve_done_a"), k.sem("var_a"), k.sem("std_a")
        tile_ready, pair_ps, pair_sb = k.sem("tile_a"), k.sem("pair_ps_a"), k.sem("pair_sb_a")
        GR = NT // 4

        rows = [("L0_gnn_Wa", 0, 4), ("L0_gnn_Wb", 4, 4)] + [(n, VEC_COL[n], KC) for n in VEC_NAMES]
        small = [
            (k.w_cat[:, :, 0:D], I["L0_gnn_W_sa"].rearrange("(c p) n -> p c n", p=P)),
            (k.w_cat[:, :, D:2 * D], I["L0_gnn_W_gcnb"].rearrange("(c p) n -> p c n", p=P)),
            (k.a_sa[:], I["L0_gnn_a_sa"].to_broadcast([P, 2 * D])),
            (k.b_gcnb[:], I["L0_gnn_b_gcnb"].rearrange("(o n) -> o n", o=1).to_broadcast([P, D])),
            (k.type_bias[:, 0:1], I["L0_gnn_ba"].rearrange("(o n) -> o n", o=1).to_broadcast([P, 1])),
            (k.type_bias[:, 1:2], I["L0_gnn_bb"].rearrange("(o n) -> o n", o=1).to_broadcast([P, 1])),
            (k.gate_w[:, 0], I["L0_ffn_gate_w"].rearrange("(c p) e -> p c e", p=P)),
            (k.gate_w[:, 1], I["L1_ffn_Wg"].rearrange("(c p) e -> p c e", p=P)),
            (k.gate_b[:, 0], I["L0_ffn_gate_b"].rearrange("(o e) -> o e", o=1).to_broadcast([P, E])),
            (k.gate_b[:, 1], I["L1_ffn_bg"].rearrange("(o e) -> o e", o=1).to_broadcast([P, E])),
        ]
        xv = I["x"].rearrange("(n p) d -> p n d", p=P)

        with nc.Block() as block:
            @block.sync
            def _(sp):
                for q in range(4):
                    sp.dma_start(k.x[:, 4 * q:4 * q + 4, :], xv[:, 4 * q:4 * q + 4, :]).then_inc(x_in[q], 16)

                def load(i, u, first):
                    if not first:
                        sp.wait_ge(adj_ps, (i - RING + 1) * GR)
                    sp.dma_start(adj_rows[:, u, :], I["adj"][ds(i * P, P), :]).then_inc(adj_in[u], 16)
                for u in range(RING):
                    load(u, u, True)
                with sp.Fori(1, NT // RING) as g:
                    for u in range(RING):
                        load(g * RING + u, u, False)
                sp.wait_ge(b1_sb, 2)
                sp.dma_start(k.b1_dram, b1_cols[:]).then_inc(b1_out, 16)
                sp.wait_ge(b1_out, 16)

            @block.gpsimd
            def _(pool):
                g = nc.gpsimd
                g.memset(k.ident[:], 0.0).then_inc(consts, 1)
                g.memset(k.ones[:], 1.0).then_inc(consts, 1)
                pool.wait_ge(consts, 2)
                g.affine_select(out=k.ident[:], in_=k.ident[:], compare_op=ALU.not_equal, fill=1.0, base=0,
                                pattern=[[-1, P]], channel_multiplier=1).then_inc(consts, 1)
                g.affine_select(out=k.before[:], in_=k.ones[:], compare_op=ALU.is_gt, fill=0.0, base=0,
                                pattern=[[1, P]], channel_multiplier=-1).then_inc(consts, 1)
                g.iota(iota_i[:], pattern=[[1, P]], base=0, channel_multiplier=0).then_inc(consts, 1)
                g.iota(lane_i[:], pattern=[[1, 1]], base=1, channel_multiplier=1).then_inc(consts, 1)
                g.iota(tile_i[:], pattern=[[1, TOP * NT]], base=0, channel_multiplier=0).then_inc(consts, 1)
                g.iota(spare_i[:], pattern=[[P, ST]], base=TOP * N + 1, channel_multiplier=1).then_inc(consts, 1)
                pool.wait_ge(consts, 8)
                g.tensor_copy(k.iota[:], iota_i[:]).then_inc(consts, 1)
                g.tensor_copy(k.iota_b[:], iota_i[:]).then_inc(consts, 1)
                g.tensor_copy(k.lane_id[:], lane_i[:]).then_inc(consts, 1)
                g.tensor_copy(k.tile_id[:].rearrange("p c n -> p (c n)"), tile_i[:]).then_inc(consts, 1)
                g.tensor_copy(k.spare[:], spare_i[:]).then_inc(consts, 1)

            @block.scalar
            def _(act):
                for name, row, count in rows:
                    src = rows_of(I, name, count)
                    act.dma_start(vec_rows[row:row + count, :], src).then_inc(rows_in, 16)
                act.dma_start(b1_rows[:, 0, :], I["L0_ffn_b1"].rearrange("e (m p) -> (e m) p", p=P)).then_inc(rows_in, 16)
                act.dma_start(b1_rows[:, 1, :], I["L1_ffn_b1"].rearrange("e (m p) -> (e m) p", p=P)).then_inc(rows_in, 16)
                for dst, src in small:
                    act.dma_start(dst, src).then_inc(small_in, 16)
                layer_norm_sqrt(k, act, var_ready, std_ready)
                transpose_xn_scalar(k, act, ps_xn, pair_ps, pair_sb)
                act.wait_ge(vec_ps, 1)
                nc.scalar.activation(k.vec[:], ps_vec[:, 0:VEC_ROWS], ACT.Copy).then_inc(vec_sb, 1)
                for l in range(2):
                    nc.scalar.activation(b1_cols[:, l, :], ps_vec[:, 128 + 64 * l:192 + 64 * l], ACT.Copy).then_inc(b1_sb, 1)

                def evac(i, u):
                    for g in (0, 2):
                        act.wait_ge(vec_sb, 1)
                        act.wait_ge(adj_ps, i * GR + g + 1)
                        nc.scalar.activation(k.adjT[:, 4 * g:4 * g + 4, ds(i * P, P)],
                                             ps_adj[:, g, :].rearrange("p (j t) -> p j t", j=4), ACT.Copy).then_inc(adj_sb_act, 1)
                with act.Fori(0, NT) as i:
                    evac(i, 0)
                act.wait_ge(small_in, 16 * len(small))

            @block.tensor
            def _(pe):
                pe.wait_ge(consts, 3)
                transpose_xn_tensor(k, pe, ps_xn, tile_ready, pair_ps, pair_sb)
                pe.wait_ge(rows_in, 16 * (len(rows) + 2))
                nc.tensor.transpose(ps_vec[:, 0:VEC_ROWS], vec_rows[:], k.ident[0:VEC_ROWS, 0:VEC_ROWS])
                nc.tensor.transpose(ps_vec[:, 128:192], b1_rows[:, 0, :], k.ident[0:64, 0:64])
                nc.tensor.transpose(ps_vec[:, 192:256], b1_rows[:, 1, :], k.ident[0:64, 0:64]).then_inc(vec_ps, 1)

                def turn(i, u, loads, first):
                    pe.wait_ge(adj_in[u], 16 * loads)
                    for g in range(GR):
                        if not first:
                            pe.wait_ge(adj_sb_act if g % 2 == 0 else adj_sb_dve, 2 * (i - 1) + g // 2 + 1)
                        for j in range(4):
                            ins = nc.tensor.transpose(ps_adj[:, g, j * P:(j + 1) * P],
                                                      adj_rows[:, u, (4 * g + j) * P:(4 * g + j + 1) * P], k.ident[:])
                        ins.then_inc(adj_ps, 1)
                for u in range(RING):
                    turn(u, u, 1, u == 0)
                with pe.Fori(1, NT // RING) as g4:
                    for u in range(RING):
                        turn(g4 * RING + u, u, g4 + 1, False)

            @block.vector
            def _(dve):
                chain = Chain(dve, dve_done)
                layer_norm_vector(k, dve, chain, var_ready, std_ready, tile_ready, x_in)

                with dve.Fori(0, NT) as i:
                    for g in (1, 3):
                        dve.wait_ge(adj_ps, i * GR + g + 1)
                        nc.vector.tensor_copy(k.adjT[:, 4 * g:4 * g + 4, ds(i * P, P)],
                                              ps_adj[:, g, :].rearrange("p (j t) -> p j t", j=4)).then_inc(adj_sb_dve, 1)


def rows_of(I, name, count):
    src = I[name]
    if len(src.shape) == 2:
        return src.rearrange("o (r p) -> (o r) p", p=P)
    return src.rearrange("(r p) -> r p", p=P)


def phase_gnn0(k, I):
    nc = k.nc
    HALF = NT // 2
    HW_ = HALF * P
    W = D + 2
    RING = 4
    with ExitStack() as ctx:
        def sb(name, shape, dt=F32):
            return ctx.enter_context(nc.sbuf_tensor(name, shape, dt))
        hA = sb("hA", [P, NT, D + 1])
        conv_hi, conv_lo = sb("conv_hi", [P, NT, W], F32R), sb("conv_lo", [P, NT, W], F32R)
        small = sb("small", [P, NT, 3])
        s_left = sb("s_left", [P, N])
        left_col = sb("left_col", [P, KC])
        zbuf = k.xnT[:, :, 0:HW_]
        mask = sb("mask", [P, 2, HW_], F32R)
        b = k.xn[:, 0:HALF, :]
        a = k.xn[:, HALF:NT, :]
        ebuf = sb("ebuf", [P, RING, HW_])
        left_w = ebuf[:, 0, 0:KC * P].rearrange("p (c t) -> p c t", c=KC)
        junk = ebuf[:, 1, 0:D]
        gate = sb("gate", [P, HALF, 2])
        inv = sb("inv", [P, HALF])
        dve_done = k.sem("dve_done_b")
        vec_ready, proj_ps, proj_sb, proj_h, high_ready = (k.sem(s) for s in ("vec_ready", "proj_ps", "proj_sb", "proj_h", "high_ready"))
        left_ps, left_sb = k.sem("left_ps"), k.sem("left_sb")
        z_ready, leaky_ready, exp_ready = k.sem("z_ready"), k.sem("leaky_ready"), k.sem("exp_ready")
        edge_ready, edge_used = k.sem("edge_ready"), k.sem("edge_used")
        mask_act, mask_dve, mask_used = k.sem("mask_act"), k.sem("mask_dve"), k.sem("mask_used")
        BY_VECTOR = list(range(HALF + 1, NT, 2))
        BY_SCALAR = [j for j in range(NT) if j not in BY_VECTOR]
        conv_ps, conv_sb, att_sb = k.sem("conv_ps"), k.sem("conv_sb"), k.sem("att_sb")
        type_ready, gate_ready, mix_ready, sig_ready = (k.sem(s) for s in ("type_ready", "gate_ready", "mix_ready", "sig_ready"))
        half_chain, sum_ready, x_done, stats_done = k.sem("half_chain"), k.sem("sum_ready_b"), k.sem("x_done"), k.sem("stats_done_b")

        with ExitStack() as pctx, nc.Block() as block:
            ps_h = pctx.enter_context(nc.psum_tensor("ps_h", [P, 2, 512], F32))
            ps_c = pctx.enter_context(nc.psum_tensor("ps_c", [P, 2, 512], F32))
            ps_left = pctx.enter_context(nc.psum_tensor("ps_left", [P, 4, 512], F32))

            @block.vector
            def _(dve):
                v = nc.vector
                chain = Chain(dve, dve_done)
                vec6 = k.w_cat[:, :, 2 * D:2 * D + 6]
                for c in range(KC):
                    chain.did(v.tensor_tensor_reduce(out=junk, in0=k.w_cat[:, c, 0:D], in1=k.a_sa[:, 0:D], scale=1.0,
                                                     scalar=0.0, op0=ALU.mult, op1=ALU.add, accum_out=left_col[:, c:c + 1]))
                    chain.settle()
                    chain.link(v.tensor_tensor_reduce(out=junk, in0=k.w_cat[:, c, 0:D], in1=k.a_sa[:, D:2 * D], scale=1.0,
                                                      scalar=0.0, op0=ALU.mult, op1=ALU.add, accum_out=vec6[:, c, 2:3]))
                for c in range(KC):
                    chain.did(v.tensor_copy(vec6[:, c, 0:1], k.vec[:, c:c + 1]))
                    chain.did(v.tensor_copy(vec6[:, c, 1:2], k.vec[:, 4 + c:5 + c]))
                    chain.did(v.tensor_copy(vec6[:, c, 3:4], k.vec[:, 2 + c:3 + c]))
                    chain.did(v.tensor_copy(vec6[:, c, 4:5], k.vec[:, 6 + c:7 + c]))
                    chain.did(v.tensor_scalar(left_w[:, c, :], k.ones[:], left_col[:, c:c + 1], None, ALU.mult))
                chain.did(v.memset(vec6[:, :, 5:6], 0.0))
                chain.settle()
                v.memset(hA[:, :, D:D + 1], 1.0).then_inc(vec_ready, 1)
                for n in range(NT):
                    dve.wait_ge(proj_ps, n + 1)
                    v.tensor_copy(conv_hi[:, n, :], ps_c[:, n % 2, 0:W]).then_inc(high_ready, 1)
                    v.tensor_copy(small[:, n, :], ps_c[:, n % 2, W:W + 3]).then_inc(high_ready, 1)
                    dve.wait_ge(high_ready, 2 * n + 2)
                    v.tensor_tensor(conv_lo[:, n, :], ps_c[:, n % 2, 0:W], conv_hi[:, n, :].bitcast(F32), ALU.subtract).then_inc(proj_sb, 1)

            @block.tensor
            def _(pe):
                pe.wait_ge(vec_ready, 1)
                for n in range(NT):
                    if n >= 2:
                        pe.wait_ge(proj_h, n - 1)
                    for c in range(KC):
                        nc.tensor.matmul(ps_h[:, n % 2, 0:D], k.xnT[:, c, n * P:(n + 1) * P], k.w_cat[:, c, 0:D],
                                         start=(c == 0), stop=(c == KC - 1))
                    if n >= 2:
                        pe.wait_ge(proj_sb, n - 1)
                    for c in range(KC):
                        ins = nc.tensor.matmul(ps_c[:, n % 2, 0:D + 6], k.xnT[:, c, n * P:(n + 1) * P], k.w_cat[:, c, D:2 * D + 6],
                                               start=(c == 0), stop=(c == KC - 1))
                    ins.then_inc(proj_ps, 1)
                for q in range(4):
                    for c in range(KC):
                        ins = nc.tensor.matmul(ps_left[:, q, :], left_w[:, c, :], k.xnT[:, c, q * 512:(q + 1) * 512],
                                               start=(c == 0), stop=(c == KC - 1))
                    ins.then_inc(left_ps, 1)

            @block.scalar
            def _(act):
                for n in range(NT):
                    act.wait_ge(proj_ps, n + 1)
                    nc.scalar.activation(hA[:, n, 0:D], ps_h[:, n % 2, 0:D], ACT.Copy).then_inc(proj_h, 1)
                for q in range(4):
                    act.wait_ge(left_ps, q + 1)
                    nc.scalar.activation(s_left[:, q * 512:(q + 1) * 512], ps_left[:, q, :], ACT.Copy).then_inc(left_sb, 1)

        with ExitStack() as pctx, nc.Block() as block:
            ps = pctx.enter_context(nc.psum_tensor("ps_half", [P, HALF, 512], F32))

            @block.tensor
            def _(pe):
                pe.sem_inc(att_sb, HALF)
                with pe.Fori(0, 2) as half:
                    for j in range(NT):
                        if j in BY_VECTOR:
                            pe.wait_ge(mask_dve, half * len(BY_VECTOR) + (BY_VECTOR.index(j) + 1))
                        else:
                            pe.wait_ge(mask_act, half * len(BY_SCALAR) + (BY_SCALAR.index(j) + 1))
                        for i in range(HALF):
                            if j == 0:
                                pe.wait_ge(att_sb, half * HALF + (i + 1))
                            nc.tensor.matmul(ps[:, i, 0:W], mask[:, j % 2, i * P:(i + 1) * P], conv_hi[:, j, :],
                                             start=(j == 0), stop=False)
                            ins = nc.tensor.matmul(ps[:, i, 0:W], mask[:, j % 2, i * P:(i + 1) * P], conv_lo[:, j, :],
                                                   start=False, stop=(j == NT - 1))
                            if j == NT - 1:
                                ins.then_inc(conv_ps, 1)
                        if j < NT - 1:
                            ins.then_inc(mask_used, 1)
                    for j in range(NT):
                        pe.wait_ge(edge_ready, half * NT + j + 1)
                        for i in range(HALF):
                            if j == 0:
                                pe.wait_ge(conv_sb, half * HALF + i + 1)
                            ins = nc.tensor.matmul(ps[:, i, 0:D + 1], ebuf[:, j % RING, i * P:(i + 1) * P], hA[:, j, :],
                                                   start=(j == 0), stop=(j == NT - 1))
                        ins.then_inc(edge_used, 1)

            AHEAD = RING - 1

            @block.scalar
            def _(act):
                def cast_mask(half, j):
                    if j >= 2:
                        act.wait_ge(mask_used, half * (NT - 1) + j - 1)
                    elif half:
                        act.wait_ge(conv_ps, half * HALF)
                    nc.scalar.activation(mask[:, j % 2, :], k.adjT[:, j, half * HW_:(half + 1) * HW_], ACT.Copy).then_inc(mask_act, 1)

                def z_of(half, j):
                    if j == 0:
                        act.wait_ge(left_sb, 4)
                    if half * NT + j >= 2:
                        act.wait_ge(leaky_ready, half * NT + j - 1)
                    nc.scalar.activation(zbuf[:, j % 2, :], s_left[:, half * HW_:(half + 1) * HW_], ACT.Identity,
                                         bias=small[:, j, 0:1]).then_inc(z_ready, 1)

                def exp_of(half, j):
                    act.wait_ge(leaky_ready, half * NT + j + 1)
                    nc.scalar.activation(ebuf[:, j % RING, :], ebuf[:, j % RING, :], ACT.Exp, scale=-1.0).then_inc(exp_ready, 1)

                for half in range(2):
                    for j in BY_SCALAR:
                        cast_mask(half, j)
                        if half and 2 <= j + 1 < HALF + 2:
                            i = j - 1
                            act.wait_ge(mix_ready, (half - 1) * HALF + i + 1)
                            nc.scalar.activation(a[:, i, :], a[:, i, :], ACT.Tanh, scale=0.5).then_inc(sig_ready, 1)
                        if j >= HALF and j % 2 == 0:
                            step = (j - HALF) // 2
                            z_of(half, step)
                            if step:
                                exp_of(half, step - 1)
                    for j in range(AHEAD, NT):
                        if j + 1 < NT:
                            z_of(half, j + 1)
                        exp_of(half, j)
                        if j == AHEAD:
                            act.wait_ge(type_ready, half + 1)
                            nc.scalar.activation(gate[:], gate[:], ACT.Tanh, scale=0.5).then_inc(gate_ready, 1)
                for i in range(HALF):
                    act.wait_ge(mix_ready, HALF + i + 1)
                    nc.scalar.activation(a[:, i, :], a[:, i, :], ACT.Tanh, scale=0.5).then_inc(sig_ready, 1)

            @block.vector
            def _(dve):
                v = nc.vector

                def leaky(half, j):
                    dve.wait_ge(z_ready, half * NT + j + 1)
                    if half * NT + j >= RING:
                        dve.wait_ge(edge_used, half * NT + j - RING + 1)
                    v.scalar_tensor_tensor(out=ebuf[:, j % RING, :], in0=zbuf[:, j % 2, :], scalar=0.01,
                                           in1=zbuf[:, j % 2, :], op0=ALU.mult, op1=ALU.max).then_inc(leaky_ready, 1)

                def mask_edge(half, j):
                    dve.wait_ge(exp_ready, half * NT + j + 1)
                    v.tensor_tensor(ebuf[:, j % RING, :], ebuf[:, j % RING, :], k.adjT[:, j, half * HW_:(half + 1) * HW_],
                                    ALU.mult).then_inc(edge_ready, 1)

                def conv_out(half):
                    for i in range(HALF):
                        dve.wait_ge(conv_ps, half * HALF + i + 1)
                        v.tensor_tensor(b[:, i, :], ps[:, i, 0:D], k.b_gcnb[:], ALU.add)
                        v.tensor_tensor(gate[:, i, :], ps[:, i, D:W], small[:, half * HALF + i, 1:3], ALU.add).then_inc(conv_sb, 1)
                    dve.wait_ge(conv_sb, (half + 1) * HALF)
                    v.tensor_tensor(gate[:], gate[:], k.type_bias[:].rearrange("p (o w) -> p o w", o=1).to_broadcast([P, HALF, 2]),
                                    ALU.add).then_inc(type_ready, 1)

                def half_end(half):
                    dve.wait_ge(gate_ready, half + 1)
                    v.tensor_scalar(gate[:], gate[:], 0.5, 0.5, ALU.mult, ALU.add).then_inc(half_chain, 1)
                    dve.wait_ge(edge_used, (half + 1) * NT)
                    v.tensor_scalar(inv[:], ps[:, :, D:D + 1].rearrange("p i o -> p (i o)"), 1e-5, None, ALU.add).then_inc(half_chain, 1)
                    dve.wait_ge(half_chain, half * 4 + 2)
                    v.reciprocal(inv[:], inv[:]).then_inc(half_chain, 1)
                    dve.wait_ge(half_chain, half * 4 + 3)
                    v.tensor_tensor(inv[:], inv[:], gate[:, :, 0], ALU.mult).then_inc(half_chain, 1)
                    dve.wait_ge(half_chain, half * 4 + 4)
                    for i in range(HALF):
                        if half:
                            dve.wait_ge(x_done, (half - 1) * HALF + i + 1)
                        v.tensor_scalar(a[:, i, :], ps[:, i, 0:D], inv[:, i:i + 1], None, ALU.mult).then_inc(att_sb, 1)
                    for i in range(HALF):
                        dve.wait_ge(att_sb, HALF + half * HALF + i + 1)
                        v.scalar_tensor_tensor(out=a[:, i, :], in0=b[:, i, :], scalar=gate[:, i, 1:2], in1=a[:, i, :],
                                               op0=ALU.mult, op1=ALU.add).then_inc(mix_ready, 1)
                    for i in range(HALF):
                        dve.wait_ge(sig_ready, half * HALF + i + 1)
                        v.tensor_scalar(a[:, i, :], a[:, i, :], 0.5, 0.5, ALU.mult, ALU.add).then_inc(sum_ready, 1)

                def stats(n):
                    dve.wait_ge(x_done, n + 1)
                    v.bn_stats(k.ln_stats[:, n, :], k.x[:, n, :]).then_inc(stats_done, 1)

                def cast_mask(half, j):
                    dve.wait_ge(mask_used, half * (NT - 1) + j - 1)
                    v.tensor_copy(mask[:, j % 2, :], k.adjT[:, j, half * HW_:(half + 1) * HW_]).then_inc(mask_dve, 1)

                for half in range(2):
                    cast_mask(half, BY_VECTOR[0])
                    leaky(half, 0)
                    for j in range(NT):
                        if j == AHEAD:
                            conv_out(half)
                        if j + 1 < len(BY_VECTOR):
                            cast_mask(half, BY_VECTOR[j + 1])
                        if j + 1 < NT:
                            leaky(half, j + 1)
                        mask_edge(half, j)
                        if half and j >= NT - HALF:
                            stats(j - (NT - HALF))
                    half_end(half)
                for n in range(HALF, NT):
                    stats(n)
                dve.wait_ge(stats_done, NT)

            @block.gpsimd
            def _(pool):
                for n in range(NT):
                    pool.wait_ge(sum_ready, n + 1)
                    nc.gpsimd.tensor_tensor(k.x[:, n, :], k.x[:, n, :], a[:, n % HALF, :], ALU.add).then_inc(x_done, 1)


def block_norm(k, name, I, g):
    nc = k.nc
    with ExitStack() as ctx, nc.Block() as block:
        ps_xn = ctx.enter_context(nc.psum_tensor("ps_xn_" + name, [P, 2, 512], F32))
        dve_done, var_ready, std_ready = k.sem("dve_done_" + name), k.sem("var_" + name), k.sem("std_" + name)
        tile_ready, pair_ps, pair_sb = k.sem("tile_" + name), k.sem("pair_ps_" + name), k.sem("pair_sb_" + name)
        w_in, x_away = k.sem("w_in_" + name), k.sem("x_away")
        WIN = 5

        @block.sync
        def _(sp):
            sp.dma_start(g.head_w[:], I["L1_gnn_W"].rearrange("(c g) d e -> (g d) c e", g=2)).then_inc(w_in, 16)
            for half in range(2):
                sp.dma_start(g.head_v[half * DH:(half + 1) * DH].rearrange("p c s e -> p c (s e)"),
                             I["L1_gnn_V"].rearrange("(c g) s e o -> g c (s e o)", g=2)[half:half + 1].to_broadcast([DH, KC, 2 * DH])).then_inc(w_in, 16)
            sp.dma_start(g.mlp_rows[:, 0], I["L1_gnn_enc_mlp_W"].rearrange("(c p) n -> p c n", p=P)).then_inc(w_in, 16)
            sp.dma_start(g.mlp_rows[:, 1], I["L1_gnn_dec_mlp_W"].rearrange("(c p) n -> p c n", p=P)).then_inc(w_in, 16)
            sp.dma_start(k.x_dram, k.x[:]).then_inc(x_away, 16)
            sp.wait_ge(w_in, 16 * WIN)
            sp.wait_ge(x_away, 16)

        @block.vector
        def _(dve):
            layer_norm_vector(k, dve, Chain(dve, dve_done), var_ready, std_ready, tile_ready, stats_taken=True)

        @block.scalar
        def _(act):
            layer_norm_sqrt(k, act, var_ready, std_ready)
            transpose_xn_scalar(k, act, ps_xn, pair_ps, pair_sb)

        @block.tensor
        def _(pe):
            transpose_xn_tensor(k, pe, ps_xn, tile_ready, pair_ps, pair_sb)


def expert_weights(k, layer, I):
    name = f"x{layer}"
    w = Shared()
    w.first, w.second, w.b2 = ((I["L0_ffn_w1"], I["L0_ffn_w2"], I["L0_ffn_b2"]) if layer == 0 else
                               (I["L1_ffn_W1"], I["L1_ffn_W2"], I["L1_ffn_b2"]))
    w.layer = layer
    w.w1_sb = k.xn[:].rearrange("p (u c m) d -> p u c (m d)", u=2, c=KC)
    w.w2_sb = k.xnT[:].rearrange("p u (m d) -> p u m d", d=D)
    w.w1_in = [k.sem(f"w1_in{u}_{name}") for u in range(2)]
    w.w2_in = [k.sem(f"w2_in{u}_{name}") for u in range(2)]
    return w


def load_expert(k, w, sp, b, u, before_w1=None, before_b1=None, before_w2=None, before_b2=None):
    e = sp.value_load(k.expert[0:1, ds(b, 1)], min_val=0, max_val=E - 1)
    if before_w1:
        sp.wait_ge(*before_w1)
    sp.dma_start(w.w1_sb[:, u], w.first[ds(e, 1)].rearrange("o (c p) f -> p (o c) f", p=P)).then_inc(w.w1_in[u], 16)
    if before_b1:
        sp.wait_ge(*before_b1)
    sp.dma_start(k.b1_sb[:, u, :], k.b1_dram[:, w.layer, ds(e * FT, FT)]).then_inc(w.w1_in[u], 16)
    if before_w2:
        sp.wait_ge(*before_w2)
    sp.dma_start(w.w2_sb[:, u], w.second[ds(e, 1)].rearrange("o (m p) d -> p (o m) d", p=P)).then_inc(w.w2_in[u], 16)
    if before_b2:
        sp.wait_ge(*before_b2)
    sp.dma_start(k.b2_sb[:, u, :], w.b2[ds(e, 1), :].to_broadcast([P, D])).then_inc(w.w2_in[u], 16)


def phase_route(k, layer, w):
    nc = k.nc
    name = f"r{layer}"
    with ExitStack() as ctx:
        def sb(nm, shape, dt=F32):
            return ctx.enter_context(nc.sbuf_tensor(f"{nm}_{name}", shape, dt))
        prob = sb("prob", [P, NT, E])
        stat = sb("stat", [P, NT])
        top = sb("top", [P, NT, E])
        top_i = sb("top_i", [P, NT, E], U32)
        pick = sb("pick", [P, NT, TOP])
        hot = sb("hot", [P, TOP, NT, E])
        both = sb("both", [P, NT, E])
        ahead = sb("ahead", [P, 2, NT, E])
        total = sb("total", [P, NT, E])
        blocks = sb("blocks", [P, E])
        ends = sb("ends", [P, 2, E])
        cmp8 = sb("cmp8", [P, E, E])
        cmpb = sb("cmpb", [P, NB, E])
        slot_f, place = sb("slot_f", [P, TOP, NT]), sb("place", [P, TOP, NT], BF16)
        tile_b = sb("tile_b", [P, TOP, NT], BF16)
        tile = sb("tile", [P, TOP, NT])
        at_tile = sb("at_tile", [P, TOP, NT, ST], BF16)
        tile_hot = sb("tile_hot", [P, TOP, NT, 2, ST], BF16)
        lane_hot = sb("lane_hot", [P, TOP, NT, P], BF16)
        holder, token_f, wrap = sb("holder", [P, ST]), sb("token_f", [P, ST]), sb("wrap", [P, ST])
        ps_i = ctx.enter_context(nc.psum_tensor("ps_i" + name, [P, 512], F32))
        expert_f = sb("expert_f", [P, NB])
        ps_l = ctx.enter_context(nc.psum_tensor("ps_l" + name, [P, 512], F32))
        ps_c = ctx.enter_context(nc.psum_tensor("ps_c" + name, [P, 2, 512], F32))
        logit_ps, shifted, exped = k.sem("logit_ps_" + name), k.sem("shifted_" + name), k.sem("exped_" + name)
        hot_ready, count_ps, diff_ready, diff_exp = (k.sem(s + name) for s in ("hot_", "count_ps_", "diff_", "diff_exp_"))
        dve_done, lanes_ready, holder_ps = k.sem("dve_done_" + name), k.sem("lanes_" + name), k.sem("holder_ps_" + name)
        xn_out, at_tile_ready, tile_hot_ready, expert_ready = (k.sem(s + name) for s in ("xn_out_", "at_tile_", "tile_hot_", "expert_"))
        ln_done, var_ready, std_ready = k.sem("ln_done_" + name), k.sem("var_" + name), k.sem("std_" + name)
        tile_ready, pair_ps, pair_sb = k.sem("tile_" + name), k.sem("pair_ps_" + name), k.sem("pair_sb_" + name)
        ps_xn = ctx.enter_context(nc.psum_tensor("ps_xn_" + name, [P, 2, 512], F32))
        flat = lambda t: t.rearrange("p n e -> p (n e)")

        over = lambda t, n: t.rearrange("p c (n o) -> p c n o", o=1).to_broadcast([P, TOP, NT, n])
        with nc.Block() as block:
            @block.tensor
            def _(pe):
                def logits(q):
                    pe.wait_ge(pair_sb, q + 1)
                    for n in (2 * q, 2 * q + 1):
                        for c in range(KC):
                            ins = nc.tensor.matmul(ps_l[:, n * E:(n + 1) * E], k.xnT[:, c, n * P:(n + 1) * P],
                                                   k.gate_w[:, layer, c, :], start=(c == 0), stop=(c == KC - 1))
                    return ins

                transpose_xn_tensor(k, pe, ps_xn, tile_ready, pair_ps, pair_sb, logits)
                logits(NT // 2 - 1).then_inc(logit_ps, 1)
                pe.wait_ge(hot_ready, 1)
                nc.tensor.matmul(ps_c[:, 0, 0:NT * E], k.before[:], flat(both[:]), start=True, stop=True)
                nc.tensor.matmul(ps_c[:, 1, 0:NT * E], k.ones[:], flat(both[:]), start=True, stop=True).then_inc(count_ps, 1)
                for c in range(TOP):
                    pe.wait_ge(lanes_ready, c + 1)
                    pe.wait_ge(tile_hot_ready, 1)
                    for n in range(NT):
                        ins = nc.tensor.matmul(ps_i[:, 0:2 * ST], lane_hot[:, c, n, :], tile_hot[:, c, n].rearrange("p h t -> p (h t)"),
                                               start=(c == 0 and n == 0), stop=(c == TOP - 1 and n == NT - 1))
                ins.then_inc(holder_ps, 1)

            @block.scalar
            def _(act):
                layer_norm_sqrt(k, act, var_ready, std_ready)
                transpose_xn_scalar(k, act, ps_xn, pair_ps, pair_sb)
                act.wait_ge(shifted, 1)
                nc.scalar.activation(flat(prob[:]), flat(prob[:]), ACT.Exp).then_inc(exped, 1)
                if layer == 0:
                    act.wait_ge(diff_ready, 1)
                    nc.scalar.activation(k.pair_w[:, :, 1], k.pair_w[:, :, 1], ACT.Exp).then_inc(diff_exp, 1)

            @block.vector
            def _(dve):
                v = nc.vector
                layer_norm_vector(k, dve, Chain(dve, ln_done), var_ready, std_ready, tile_ready, stats_taken=True)
                chain = Chain(dve, dve_done)
                link = chain.link
                dve.wait_ge(logit_ps, 1)
                over_e = lambda t: t.rearrange("p (n o) -> p n o", o=1).to_broadcast([P, NT, E])
                link(v.tensor_tensor(prob[:], ps_l[:, 0:NT * E].rearrange("p (n e) -> p n e", e=E),
                                     k.gate_b[:, layer, :].rearrange("p (o e) -> p o e", o=1).to_broadcast([P, NT, E]), ALU.add))
                link(v.tensor_reduce(stat[:], prob[:], AX_X, ALU.max))
                v.tensor_tensor(prob[:], prob[:], over_e(stat[:]), ALU.subtract).then_inc(shifted, 1)
                dve.wait_ge(exped, 1)
                link(v.tensor_reduce(stat[:], prob[:], AX_X, ALU.add))
                link(v.reciprocal(stat[:], stat[:]))
                link(v.tensor_tensor(prob[:], prob[:], over_e(stat[:]), ALU.mult))
                for n in range(NT):
                    chain.did(v.max(top[:, n, :], prob[:, n, :]))
                chain.settle()
                for n in range(NT):
                    chain.did(v.max_index(top_i[:, n, :], top[:, n, :], prob[:, n, :]))
                chain.settle()
                link(v.tensor_copy(pick[:], top_i[:, :, 0:TOP]))
                for c in range(TOP):
                    chain.did(v.tensor_tensor(hot[:, c], pick[:, :, c:c + 1].to_broadcast([P, NT, E]),
                                              k.iota[:, 0:E].rearrange("p (o e) -> p o e", o=1).to_broadcast([P, NT, E]), ALU.is_equal))
                chain.settle()
                v.tensor_tensor(both[:], hot[:, 0], hot[:, 1], ALU.add).then_inc(hot_ready, 1)
                if layer == 0:
                    v.tensor_tensor(k.pair_w[:, :, 1], top[:, :, 1], top[:, :, 0], ALU.subtract).then_inc(diff_ready, 1)
                    dve.wait_ge(diff_exp, 1)
                    link(v.tensor_scalar(stat[:], k.pair_w[:, :, 1], 1.0, None, ALU.add))
                    link(v.reciprocal(k.pair_w[:, :, 0], stat[:]))
                    link(v.tensor_tensor(k.pair_w[:, :, 1], k.pair_w[:, :, 1], k.pair_w[:, :, 0], ALU.mult))
                else:
                    link(v.tensor_tensor(stat[:], top[:, :, 0], top[:, :, 1], ALU.add))
                    link(v.reciprocal(stat[:], stat[:]))
                    for c in range(TOP):
                        chain.did(v.tensor_tensor(k.pair_w[:, :, c], top[:, :, c], stat[:], ALU.mult))
                dve.wait_ge(count_ps, 1)
                chain.did(v.tensor_copy(total[:], ps_c[:, 1, 0:NT * E].rearrange("p (n e) -> p n e", e=E)))
                link(v.tensor_copy(ahead[:, 0], ps_c[:, 1, 0:NT * E].rearrange("p (n e) -> p n e", e=E)))
                side = 0
                for sh in (1, 2, 4, 8):
                    chain.did(v.tensor_copy(ahead[:, 1 - side, 0:sh], ahead[:, side, 0:sh]))
                    link(v.tensor_tensor(ahead[:, 1 - side, sh:NT], ahead[:, side, sh:NT], ahead[:, side, 0:NT - sh], ALU.add))
                    side = 1 - side
                link(v.tensor_scalar(expert_f[:, 0:E], k.iota[:, 0:E], float(BLK), None, ALU.mult))
                link(v.tensor_tensor(cmp8[:], ahead[:, side, NT - 1, :].rearrange("p (e o) -> p e o", o=1).to_broadcast([P, E, E]),
                                     expert_f[:, 0:E].rearrange("p (o b) -> p o b", o=1).to_broadcast([P, E, E]), ALU.is_gt))
                link(v.tensor_reduce(blocks[:], cmp8[:], AX_X, ALU.add))
                link(v.tensor_copy(ends[:, 0], blocks[:]))
                es = 0
                for sh in (1, 2, 4):
                    chain.did(v.tensor_copy(ends[:, 1 - es, 0:sh], ends[:, es, 0:sh]))
                    link(v.tensor_tensor(ends[:, 1 - es, sh:E], ends[:, es, sh:E], ends[:, es, 0:E - sh], ALU.add))
                    es = 1 - es
                link(v.tensor_tensor(cmpb[:], k.iota[:, 0:NB].rearrange("p (b o) -> p b o", o=1).to_broadcast([P, NB, E]),
                                     ends[:, es].rearrange("p (o e) -> p o e", o=1).to_broadcast([P, NB, E]), ALU.is_ge))
                link(v.tensor_reduce(expert_f[:], cmpb[:], AX_X, ALU.add))
                link(v.tensor_scalar(expert_f[:], expert_f[:], float(E - 1), None, ALU.min))
                v.tensor_copy(k.expert[:], expert_f[:]).then_inc(expert_ready, 1)
                link(v.tensor_tensor(blocks[:], ends[:, es], blocks[:], ALU.subtract))
                link(v.tensor_scalar(blocks[:], blocks[:], float(BLK), None, ALU.mult))
                link(v.tensor_tensor(total[:], ahead[:, side], total[:], ALU.subtract))
                link(v.tensor_tensor(total[:], total[:], blocks[:].rearrange("p (o e) -> p o e", o=1).to_broadcast([P, NT, E]), ALU.add))
                link(v.tensor_tensor(total[:], total[:], ps_c[:, 0, 0:NT * E].rearrange("p (n e) -> p n e", e=E), ALU.add))
                for c in range(TOP):
                    link(v.tensor_tensor(hot[:, c], hot[:, c], total[:], ALU.mult))
                    link(v.tensor_reduce(slot_f[:, c, :], hot[:, c], AX_X, ALU.add))
                link(v.tensor_scalar(tile[:], slot_f[:], 1.0 / P, -(P - 1) / (2.0 * P), ALU.mult, ALU.add))
                link(v.tensor_scalar(tile[:], tile[:], float(3 * 2 ** 22), None, ALU.add))
                link(v.tensor_scalar(tile[:], tile[:], -float(3 * 2 ** 22), None, ALU.add))
                chain.did(v.scalar_tensor_tensor(out=place[:], in0=tile[:], scalar=-float(P), in1=slot_f[:], op0=ALU.mult, op1=ALU.add))
                link(v.tensor_copy(tile_b[:], tile[:]))
                v.tensor_tensor(at_tile[:], over(tile_b[:], ST),
                                k.iota_b[:, 0:ST].rearrange("p (c n t) -> p c n t", c=1, n=1).to_broadcast([P, TOP, NT, ST]),
                                ALU.is_equal).then_inc(at_tile_ready, 1)
                dve.wait_ge(at_tile_ready, 1)
                chain.did(v.tensor_scalar(tile_hot[:, :, :, 0, :], at_tile[:], k.lane_id[:, 0:1], None, ALU.mult))
                chain.settle()
                for c in range(TOP):
                    v.tensor_tensor(lane_hot[:, c], place[:, c, :].rearrange("p (n o) -> p n o", o=1).to_broadcast([P, NT, P]),
                                    k.iota_b[:].rearrange("p (o t) -> p o t", o=1).to_broadcast([P, NT, P]), ALU.is_equal).then_inc(lanes_ready, 1)
                dve.wait_ge(holder_ps, 1)
                link(v.tensor_copy(token_f[:], ps_i[:, 0:ST]))
                link(v.scalar_tensor_tensor(out=holder[:], in0=ps_i[:, ST:2 * ST], scalar=float(P), in1=token_f[:], op0=ALU.mult, op1=ALU.add))
                link(v.tensor_scalar(wrap[:], holder[:], 0.0, None, ALU.is_equal))
                link(v.tensor_tensor(wrap[:], wrap[:], k.spare[:], ALU.mult))
                chain.did(v.scalar_tensor_tensor(out=k.row_of[:], in0=wrap[:], scalar=-1.0, in1=holder[:], op0=ALU.add, op1=ALU.add))
                link(v.tensor_scalar(token_f[:], holder[:], -1.0, 0.0, ALU.add, ALU.max))
                link(v.tensor_scalar(wrap[:], token_f[:], float(N), -float(N), ALU.is_ge, ALU.mult))
                link(v.tensor_tensor(token_f[:], token_f[:], wrap[:], ALU.add))
                link(v.tensor_copy(k.token_of[:], token_f[:]))

            @block.gpsimd
            def _(pool):
                pool.wait_ge(at_tile_ready, 1)
                nc.gpsimd.tensor_tensor(tile_hot[:, :, :, 1, :], at_tile[:], over(k.tile_id[:], ST), ALU.mult).then_inc(tile_hot_ready, 1)

            @block.sync
            def _(sp):
                xd = k.xn_dram.rearrange("(n p) d -> p n d", p=P)
                for q in range(4):
                    sp.wait_ge(tile_ready, 4 * q + 4)
                    sp.dma_start(xd[:, 4 * q:4 * q + 4, :], k.xn[:, 4 * q:4 * q + 4, :]).then_inc(xn_out, 16)
                sp.wait_ge(xn_out, 64)
                sp.wait_ge(logit_ps, 1)
                sp.wait_ge(expert_ready, 1)
                for b in range(2):
                    load_expert(k, w, sp, b, b)


def split_products(nc, out, w_parts, x_parts, start, stop):
    (w_hi, w_lo), (x_hi, x_lo) = w_parts, x_parts
    nc.tensor.matmul(out, w_hi, x_hi, start=start, stop=False)
    nc.tensor.matmul(out, w_hi, x_lo, start=False, stop=False)
    return nc.tensor.matmul(out, w_lo, x_hi, start=False, stop=stop)


def phase_experts(k, layer, w):
    nc = k.nc
    name = f"x{layer}"
    HC = FT // 2
    PAIRS = FT // 2
    with ExitStack() as ctx:
        def sb(nm, shape, dt=F32):
            return ctx.enter_context(nc.sbuf_tensor(f"{nm}_{name}", shape, dt))
        w1_sb, w2_sb, w1_in, w2_in, b1_sb, b2_sb = w.w1_sb, w.w2_sb, w.w1_in, w.w2_in, k.b1_sb, k.b2_sb
        w1_hi, w1_lo = sb("w1_hi", [P, KC, F], F32R), sb("w1_lo", [P, KC, F], F32R)
        w2_hi, w2_lo = sb("w2_hi", [P, FT, D], F32R), sb("w2_lo", [P, FT, D], F32R)
        rows = sb("rows", [P, 2, BT, D])
        token_now, row_now = sb("token_now", [P, 2, BT], I32), sb("row_now", [P, 2, BT], I32)
        rows_hi, rows_lo = sb("rows_hi", [P, 2, KC, BLK], F32R), sb("rows_lo", [P, 2, KC, BLK], F32R)
        hid = sb("hid", [P, FT, BLK])
        hid_hi, hid_lo = sb("hid_hi", [P, FT, BLK], F32R), sb("hid_lo", [P, FT, BLK], F32R)
        res = sb("res", [P, 2, BT, D])
        ps_t = ctx.enter_context(nc.psum_tensor("ps_t" + name, [P, 512], F32))
        ps_h = ctx.enter_context(nc.psum_tensor("ps_h" + name, [P, FT, BLK], F32))
        ps_y = ctx.enter_context(nc.psum_tensor("ps_y" + name, [P, BT, 512], F32))
        rows_in = [k.sem(f"rows_in{u}_{name}") for u in range(2)]
        res_out = [k.sem(f"res_out{u}_{name}") for u in range(2)]
        turned, rows_high, rows_split = (k.sem(s + name) for s in ("turned_", "rows_high_", "rows_split_"))
        w1_high, w1_split, w2_high, w2_split = (k.sem(s + name) for s in ("w1_high_", "w1_split_", "w2_high_", "w2_split_"))
        hid_ps, hid_full, hid_high, hid_split = (k.sem(s + name) for s in ("hid_ps_", "hid_full_", "hid_high_", "hid_split_"))
        y_ps, y_sb = k.sem("y_ps_" + name), k.sem("y_sb_" + name)
        picked, rows_picked = k.sem("picked_" + name), k.sem("rows_picked_" + name)

        with nc.Block() as block:
            @block.sync
            def _(sp):
                def step(b, u):
                    load_expert(k, w, sp, b, u, (w1_split, (b - 1) * 2), (hid_full, (b - 1) * FT), (w2_split, (b - 1) * 2), (y_sb, (b - 1) * BT))

                with sp.Fori(1, NB // 2) as g:
                    step(g * 2, 0)
                    step(g * 2 + 1, 1)
                step(NB - 1, 0)

            @block.tensor
            def _(pe):
                def turn(b, u, past, one):
                    pe.wait_ge(rows_in[u], 16 * BT * (past + 1))
                    if one:
                        pe.wait_ge(rows_split, b)
                    for c in range(KC):
                        for s in range(BT):
                            ins = nc.tensor.transpose(ps_t[:, c * BLK + s * P:c * BLK + (s + 1) * P],
                                                      rows[:, u, s, c * P:(c + 1) * P], k.ident[:])
                    ins.then_inc(turned, 1)

                def products(b, u, past, one, more):
                    pe.wait_ge(rows_split, b + 1)
                    for m in range(FT):
                        if m % HC == 0:
                            pe.wait_ge(w1_split, b * 2 + m // HC + 1)
                        if one and m % 2 == 0:
                            pe.wait_ge(hid_full, (b - 1) * FT + m + 2)
                        part = slice(m * P, (m + 1) * P)
                        for c in range(KC):
                            ins = split_products(nc, ps_h[:, m, :], (w1_hi[:, c, part], w1_lo[:, c, part]),
                                                 (rows_hi[:, u, c, :], rows_lo[:, u, c, :]), c == 0, c == KC - 1)
                        if m % 2 == 1:
                            ins.then_inc(hid_ps, 1)
                    if more:
                        turn(b + 1, 1 - u, past + u, True)
                    for m in range(FT):
                        if m % HC == 0:
                            pe.wait_ge(w2_split, b * 2 + m // HC + 1)
                        if m % 2 == 0:
                            pe.wait_ge(hid_split, b * PAIRS + m // 2 + 1)
                        for s in range(BT):
                            if one and m == 0:
                                pe.wait_ge(y_sb, (b - 1) * BT + s + 1)
                            part = slice(s * P, (s + 1) * P)
                            ins = split_products(nc, ps_y[:, s, 0:D], (hid_hi[:, m, part], hid_lo[:, m, part]),
                                                 (w2_hi[:, m, :], w2_lo[:, m, :]), m == 0, m == FT - 1)
                        if m % HC == HC - 1:
                            ins.then_inc(y_ps, 1)

                turn(0, 0, 0, False)
                products(0, 0, 0, False, True)
                products(1, 1, 0, True, True)
                with pe.Fori(1, NB // 2) as g:
                    products(g * 2, 0, g, True, True)
                    products(g * 2 + 1, 1, g, True, True)
                products(NB - 1, 0, NB // 2, True, False)

            @block.scalar
            def _(act):
                def high_w1(b, u, past, one):
                    act.wait_ge(w1_in[u], 32 * (past + 1))
                    for h in range(2):
                        if one:
                            act.wait_ge(hid_ps, (b - 1) * PAIRS + 2 * h + 2)
                        chunk = slice(h * HC * P, (h + 1) * HC * P)
                        nc.scalar.activation(w1_hi[:, :, chunk], w1_sb[:, u, :, chunk], ACT.Copy).then_inc(w1_high, 1)

                def high_w2(b, u, past, h, one):
                    act.wait_ge(w2_in[u], 32 * (past + 1))
                    if one:
                        act.wait_ge(y_ps, (b - 1) * 2 + h + 1)
                    chunk = slice(h * HC, (h + 1) * HC)
                    nc.scalar.activation(w2_hi[:, chunk, :], w2_sb[:, u, chunk, :], ACT.Copy).then_inc(w2_high, 1)

                def high_rows(b, u, two):
                    act.wait_ge(turned, b + 1)
                    if two:
                        act.wait_ge(hid_ps, (b - 1) * PAIRS)
                    nc.scalar.activation(rows_hi[:, u].rearrange("p c t -> p (c t)"), ps_t[:], ACT.Copy).then_inc(rows_high, 1)

                def step(b, u, past, one, two, more=True):
                    for m in range(FT):
                        if m % 2 == 0:
                            act.wait_ge(hid_ps, b * PAIRS + m // 2 + 1)
                            if one:
                                act.wait_ge(hid_split, (b - 1) * PAIRS + m // 2 + 1)
                        nc.scalar.activation(hid[:, m, :], ps_h[:, m, :], ACT.Relu, bias=b1_sb[:, u, m:m + 1]).then_inc(hid_full, 1)
                        if m == 3:
                            high_w2(b, u, past, 1, one)
                    if more:
                        high_rows(b + 1, 1 - u, one)
                        high_w1(b + 1, 1 - u, past + u, True)
                        high_w2(b + 1, 1 - u, past + u, 0, True)

                high_w1(0, 0, 0, False)
                high_w2(0, 0, 0, 0, False)
                high_rows(0, 0, False)
                step(0, 0, 0, False, False)
                step(1, 1, 0, True, False)
                with act.Fori(1, NB // 2) as g:
                    step(g * 2, 0, g, True, True)
                    step(g * 2 + 1, 1, g, True, True)
                step(NB - 1, 0, NB // 2, True, True, more=False)

            @block.vector
            def _(dve):
                v = nc.vector

                def low_rows(b, u):
                    dve.wait_ge(rows_high, b + 1)
                    hi, lo = (t[:, u].rearrange("p c t -> p (c t)") for t in (rows_hi, rows_lo))
                    v.tensor_tensor(lo, ps_t[:], hi.bitcast(F32), ALU.subtract).then_inc(rows_split, 1)

                def low_w1(b, u, past):
                    for h in range(2):
                        dve.wait_ge(w1_high, b * 2 + h + 1)
                        chunk = slice(h * HC * P, (h + 1) * HC * P)
                        v.tensor_tensor(w1_lo[:, :, chunk], w1_sb[:, u, :, chunk], w1_hi[:, :, chunk].bitcast(F32),
                                        ALU.subtract).then_inc(w1_split, 1)

                def low_w2(b, u, h):
                    dve.wait_ge(w2_high, b * 2 + h + 1)
                    chunk = slice(h * HC, (h + 1) * HC)
                    v.tensor_tensor(w2_lo[:, chunk, :], w2_sb[:, u, chunk, :], w2_hi[:, chunk, :].bitcast(F32),
                                    ALU.subtract).then_inc(w2_split, 1)

                def step(b, u, past, one, two, more=True):
                    for q in range(PAIRS):
                        pair = slice(2 * q, 2 * q + 2)
                        dve.wait_ge(hid_full, b * FT + 2 * q + 2)
                        if one and q == 0:
                            dve.wait_ge(y_ps, b * 2)
                        v.tensor_copy(hid_hi[:, pair, :], hid[:, pair, :]).then_inc(hid_high, 1)
                        dve.wait_ge(hid_high, b * PAIRS + q + 1)
                        v.tensor_tensor(hid_lo[:, pair, :], hid[:, pair, :], hid_hi[:, pair, :].bitcast(F32),
                                        ALU.subtract).then_inc(hid_split, 1)
                        if q == 1:
                            low_w2(b, u, 1)
                    if more:
                        low_rows(b + 1, 1 - u)
                        low_w1(b + 1, 1 - u, past + u)
                        low_w2(b + 1, 1 - u, 0)
                    dve.wait_ge(w2_in[u], 32 * (past + 1))
                    dve.wait_ge(y_ps, b * 2 + 2)
                    if two:
                        dve.wait_ge(res_out[u], 16 * BT * past)
                    for s in range(BT):
                        v.tensor_tensor(res[:, u, s, :], ps_y[:, s, 0:D], b2_sb[:, u, :], ALU.add).then_inc(y_sb, 1)

                low_w1(0, 0, 0)
                low_w2(0, 0, 0)
                low_rows(0, 0)
                step(0, 0, 0, False, False)
                step(1, 1, 0, True, False)
                with dve.Fori(1, NB // 2) as g:
                    step(g * 2, 0, g, True, True)
                    step(g * 2 + 1, 1, g, True, True)
                step(NB - 1, 0, NB // 2, True, True, more=False)

            @block.gpsimd
            def _(pool):
                def pick_tokens(b, u, two):
                    if two:
                        pool.wait_ge(turned, b - 1)
                    nc.gpsimd.tensor_copy(token_now[:, u, :], k.token_of[:, ds(b * BT, BT)]).then_inc(picked, 1)

                def gather(b, u):
                    for s in range(BT):
                        pool.indirect_dma_start(out=rows[:, u, s, :], out_offset=None, in_=k.xn_dram,
                                                in_offset=bass.IndirectOffsetOnAxis(ap=token_now[:, u, s:s + 1], axis=0)).then_inc(rows_in[u], 16)

                def step(b, u, past, two, left=3):
                    pool.wait_ge(picked, b + (3 if left >= 2 else 1 + left))
                    if two:
                        pool.wait_ge(res_out[u], 16 * BT * past)
                    nc.gpsimd.tensor_copy(row_now[:, u, :], k.row_of[:, ds(b * BT, BT)]).then_inc(rows_picked, 1)
                    if left >= 2:
                        gather(b + 2, u)
                    pool.wait_ge(rows_picked, b + 1)
                    pool.wait_ge(y_sb, (b + 1) * BT)
                    if left >= 3:
                        pick_tokens(b + 3, 1 - u, True)
                    for s in range(BT):
                        pool.indirect_dma_start(out=k.results, out_offset=bass.IndirectOffsetOnAxis(ap=row_now[:, u, s:s + 1], axis=0),
                                                in_=res[:, u, s, :], in_offset=None).then_inc(res_out[u], 16)

                pick_tokens(0, 0, False)
                pick_tokens(1, 1, False)
                pool.wait_ge(picked, 2)
                gather(0, 0)
                gather(1, 1)
                pick_tokens(2, 0, True)
                step(0, 0, 0, False)
                step(1, 1, 0, False)
                with pool.Fori(1, NB // 2 - 1) as g:
                    step(g * 2, 0, g, True)
                    step(g * 2 + 1, 1, g, True)
                for b in range(NB // 2 * 2 - 2, NB):
                    step(b, b % 2, b // 2, True, left=min(3, NB - 1 - b))
                pool.wait_ge(res_out[0], 16 * BT * (NB // 2 + 1))
                pool.wait_ge(res_out[1], 16 * BT * (NB // 2))


def phase_combine(k, layer, out=None):
    nc = k.nc
    name = f"c{layer}"
    FOUR = 4
    QS = NT // FOUR
    with ExitStack() as ctx, nc.Block() as block:
        got = ctx.enter_context(nc.sbuf_tensor("got_" + name, [P, QS, TOP, FOUR, D], F32))
        fetched = [k.sem(f"fetched{q}_{name}") for q in range(QS)]
        added, stored, stats_done = k.sem("added_" + name), k.sem("stored_" + name), k.sem("stats_done_" + name)
        scaled, summed = k.sem("scaled_" + name), k.sem("summed_" + name)
        results = k.results[0:TOP * N, :].rearrange("(c n p) d -> p c n d", c=TOP, p=P)

        @block.sync
        def _(sp):
            for q in range(QS):
                for c in (1, 0):
                    sp.dma_start(got[:, q, c], results[:, c, FOUR * q:FOUR * q + FOUR, :]).then_inc(fetched[q], 16)
            if out is not None:
                ov = out.rearrange("(n p) d -> p n d", p=P)
                for q in range(QS):
                    sp.wait_ge(added, FOUR * (q + 1))
                    sp.dma_start(ov[:, FOUR * q:FOUR * q + FOUR, :], k.x[:, FOUR * q:FOUR * q + FOUR, :]).then_inc(stored, 16)
                sp.wait_ge(stored, 16 * QS)

        @block.scalar
        def _(act):
            for n in range(NT):
                if n % FOUR == 0:
                    act.wait_ge(fetched[n // FOUR], 16 * TOP)
                second = got[:, n // FOUR, 1, n % FOUR, :]
                nc.scalar.activation(second, second, ACT.Copy, scale=k.pair_w[:, n, 1:2]).then_inc(scaled, 1)

        @block.gpsimd
        def _(pool):
            for n in range(NT):
                pool.wait_ge(scaled, n + 1)
                second = got[:, n // FOUR, 1, n % FOUR, :]
                nc.gpsimd.tensor_tensor(second, second, k.x[:, n, :], ALU.add).then_inc(summed, 1)

        @block.vector
        def _(dve):
            def stats(n):
                if out is None:
                    dve.wait_ge(added, n + 1)
                    nc.vector.bn_stats(k.ln_stats[:, n, :], k.x[:, n, :]).then_inc(stats_done, 1)

            for n in range(NT):
                if n % FOUR == 0:
                    dve.wait_ge(fetched[n // FOUR], 16 * TOP)
                dve.wait_ge(summed, n + 1)
                nc.vector.scalar_tensor_tensor(out=k.x[:, n, :], in0=got[:, n // FOUR, 0, n % FOUR, :], scalar=k.pair_w[:, n, 0:1],
                                               in1=got[:, n // FOUR, 1, n % FOUR, :], op0=ALU.mult, op1=ALU.add).then_inc(added, 1)
                if n:
                    stats(n - 1)
            stats(NT - 1)
            if out is None:
                dve.wait_ge(stats_done, NT)


def phase_gnn1_project(k, I, g):
    nc = k.nc
    with ExitStack() as ctx, nc.Block() as block:
        def sb(name, shape, dt=F32):
            return ctx.enter_context(nc.sbuf_tensor(name, shape, dt))
        head_w, head_v, mlp_rows = g.head_w, g.head_v, g.mlp_rows
        score_v = sb("score_v", [P, KC, 2])
        junk = sb("junk1", [P, DH])
        f1w = sb("f1w", [P, H, P])
        own_w = sb("own_w", [P, KC, P + 2])
        ps_w = ctx.enter_context(nc.psum_tensor("ps_w", [P, 2, 512], F32))
        ps_p = ctx.enter_context(nc.psum_tensor("ps_p", [P, 2, 512], F32))
        ps_f = ctx.enter_context(nc.psum_tensor("ps_f", [P, 4, 512], F32))
        zeroed, dve_done, w_ready = k.sem("zeroed_p"), k.sem("dve_done_p"), k.sem("w_ready_p")
        turned, turned_sb, proj_ps, proj_sb = k.sem("turned_p"), k.sem("turned_sb_p"), k.sem("proj_ps_p"), k.sem("proj_sb_p")
        f1_ps, f1_sb, ones_ready = k.sem("f1_ps"), k.sem("f1_sb"), k.sem("ones_ready_p")
        g.f1_sb = f1_sb

        @block.gpsimd
        def _(pool):
            nc.gpsimd.memset(f1w[:], 0.0).then_inc(zeroed, 1)
            nc.gpsimd.memset(own_w[:], 0.0).then_inc(zeroed, 1)
            nc.gpsimd.memset(g.near[:, :, DH:2 * DH], 1.0).then_inc(ones_ready, 1)
            pool.wait_ge(ones_ready, 1)

        @block.vector
        def _(dve):
            v = nc.vector
            chain = Chain(dve, dve_done)
            dve.wait_ge(zeroed, 2)
            for c in range(KC):
                for s in range(2):
                    chain.link(v.tensor_tensor_reduce(out=junk[:], in0=head_w[:, c, :], in1=head_v[:, c, s, :], scale=1.0, scalar=0.0,
                                                      op0=ALU.mult, op1=ALU.add, accum_out=score_v[:, c, s:s + 1]))
            for c in range(KC):
                for q in range(2):
                    part = slice(q * DH, (q + 1) * DH)
                    chain.did(v.tensor_copy(own_w[part, c, q * DH:(q + 1) * DH], head_w[part, c, :]))
                    chain.did(v.tensor_copy(own_w[part, c, P + q:P + q + 1], score_v[part, c, 1:2]))
                    chain.did(v.tensor_scalar(f1w[part, 2 * c + q, :], k.ones[part, :], score_v[part, c, 0:1], None, ALU.mult))
            chain.settle()
            v.engine_nop().then_inc(w_ready, 1)
            for n in range(NT):
                dve.wait_ge(proj_ps, n + 1)
                pv = ps_p[:, n % 2, 0:KC * (P + 2)].rearrange("p (c w) -> p c w", c=KC)
                v.tensor_copy(k.xn[:, n, :].rearrange("p (c w) -> p c w", c=KC), pv[:, :, 0:P]).then_inc(dve_done, 1)
                v.tensor_scalar(g.f2_half[:, n, :].rearrange("p (c w) -> p c w", c=KC), pv[:, :, P:P + 2], 0.5, None,
                                ALU.mult).then_inc(proj_sb, 1)

        @block.tensor
        def _(pe):
            pe.wait_ge(w_ready, 1)
            for l in range(2):
                if l:
                    pe.wait_ge(turned_sb, l)
                for kc in range(KC):
                    for oc in range(KC):
                        ins = nc.tensor.transpose(ps_w[:, 0, kc * D + oc * P:kc * D + (oc + 1) * P], mlp_rows[:, l, oc, kc * P:(kc + 1) * P], k.ident[:])
                ins.then_inc(turned, 1)
            for c in range(KC):
                ins = nc.tensor.transpose(ps_w[:, 1, c * P:(c + 1) * P], own_w[:, c, 0:P], k.ident[:])
            ins.then_inc(turned, 1)
            for n in range(NT):
                if n >= 2:
                    pe.wait_ge(proj_sb, n - 1)
                for c in range(KC):
                    ins = nc.tensor.matmul(ps_p[:, n % 2, c * (P + 2):(c + 1) * (P + 2)], k.xnT[:, c, n * P:(n + 1) * P], own_w[:, c, :],
                                           start=True, stop=True)
                ins.then_inc(proj_ps, 1)
            for h in range(H):
                for q in range(4):
                    if h:
                        pe.wait_ge(f1_sb, 4 * (h - 1) + q + 1)
                    nc.tensor.matmul(ps_f[:, q, :], f1w[:, h, :], k.xnT[:, h // 2, q * 512:(q + 1) * 512],
                                     start=True, stop=True).then_inc(f1_ps, 1)

        @block.scalar
        def _(act):
            s = nc.scalar
            for l in range(2):
                act.wait_ge(turned, l + 1)
                s.activation(g.mlp_wT[:, l].rearrange("p c n -> p (c n)"), ps_w[:, 0, :], ACT.Copy).then_inc(turned_sb, 1)
            act.wait_ge(turned, 3)
            s.activation(g.head_wT[:].rearrange("p c n -> p (c n)"), ps_w[:, 1, 0:KC * P], ACT.Copy).then_inc(turned_sb, 1)
            for h in range(H):
                for q in range(4):
                    act.wait_ge(f1_ps, 4 * h + q + 1)
                    s.activation(g.f1[:, h, q * 512:(q + 1) * 512], ps_f[:, q, :], ACT.Copy).then_inc(f1_sb, 1)


def phase_attend(k, g, name, first):
    nc = k.nc
    KEPT = g.KEPT
    M = len(KEPT)
    computed = [j for j in range(NT) if first or j not in KEPT]
    C = len(computed)
    steps = [(q, j) for q in range(2) for j in range(NT)]

    def nth(q, j):
        return q * C + computed.index(j)

    def nth_kept(q, j):
        return q * M + KEPT.index(j)

    with ExitStack() as ctx, nc.Block() as block:
        ps = ctx.enter_context(nc.psum_tensor("ps_att_" + name, [P, 2, N], F32))
        tanh_ready, exp_ready, edge_ready, edge_free = (k.sem(s + name) for s in ("tanh_", "exp_", "edge_r_", "edge_f_"))
        near_ready, sum_free, inv_done = k.sem("near_" + name), k.sem("sum_free_" + name), k.sem("inv_" + name)
        divided, kept_free = k.sem("divided_" + name), k.sem("kept_f_" + name)
        inverted = k.sem("inverted_" + name)
        PIECES = 16
        CH = N // PIECES
        last_ready, last_kept = k.sem("last_ready_" + name), k.sem("last_kept_" + name)
        HT = N // 2
        last_inv = g.edge[:, 0, 0:HT]
        kept_moved = [k.sem(f"kept_moved{u}_{name}") for u in range(2)]

        @block.sync
        def _(sp):
            with sp.Fori(0, H // 2) as hp:
                for q in range(2):
                    for j in KEPT:
                        m = nth_kept(q, j)
                        if first:
                            sp.wait_ge(edge_ready, hp * (2 * NT) + (q * NT + j + 1))
                            sp.dma_start(k.kept_dram[ds(hp * (2 * M) + m, 1)].rearrange("o p t -> p (o t)"), g.kept[:, m % 2, :]).then_inc(kept_moved[m % 2], 16)
                        else:
                            sp.wait_ge(kept_free, hp * (2 * M) + (m + 1))
                            sp.dma_start(g.kept[:, m % 2, :], k.kept_dram[ds(hp * (2 * M) + m, 1)].rearrange("o p t -> p (o t)")).then_inc(kept_moved[m % 2], 16)
            for u in range(2):
                sp.wait_ge(kept_moved[u], 16 * H * M // 2)

        @block.scalar
        def _(act):
            with act.Fori(0, H // 2) as hp:
                def tanh_of(q, j):
                    c = nth(q, j)
                    act.wait_ge(g.f1_sb, 4 * H)
                    act.wait_ge(edge_free, hp * (2 * C) + (c + 1))
                    nc.scalar.activation(g.edge[:, c % g.RING, :], g.f1[:, ds(hp * 2 + q, 1), :].rearrange("p o t -> p (o t)"), ACT.Tanh,
                                         scale=0.5, bias=g.f2_half[:, j, ds(hp * 2 + q, 1)]).then_inc(tanh_ready, 1)

                def exp_of(q, j):
                    c = nth(q, j)
                    act.wait_ge(tanh_ready, hp * (2 * C) + (c + 1))
                    nc.scalar.activation(g.edge[:, c % g.RING, :], g.edge[:, c % g.RING, :], ACT.Exp, scale=0.5).then_inc(exp_ready, 1)

                mine = [(q, j) for q in range(2) for j in computed]
                tanh_of(*mine[0])
                for i, (q, j) in enumerate(mine):
                    if i + 1 < len(mine):
                        tanh_of(*mine[i + 1])
                    exp_of(q, j)
            if first:
                act.wait_ge(last_ready, 2)
                for side in range(2):
                    nc.scalar.activation(g.inv[DH:2 * DH, 1, side * HT:(side + 1) * HT], last_inv[side * DH:(side + 1) * DH, :],
                                         ACT.Copy).then_inc(last_kept, 1)

        @block.gpsimd
        def _(pool):
            def divide(rows, hp, heads):
                pool.wait_ge(inverted, (heads - 1) * PIECES)
                pool.wait_ge(sum_free, 2 + heads)
                nc.gpsimd.tensor_tensor(k.xnT[rows, hp, :], k.xnT[rows, hp, :], g.inv[rows, hp, :], ALU.mult).then_inc(divided, 1)

            def pair_of_heads(hp):
                for i, (q, j) in enumerate(steps):
                    qq, jj = steps[i - g.RING]
                    wrap = 1 if i < g.RING else 0
                    if jj in computed:
                        pool.wait_ge(edge_free, hp * (2 * C) + (nth(qq, jj) - wrap * 2 * C + 1 + g.RING))
                    else:
                        pool.wait_ge(kept_free, hp * (2 * M) + (nth_kept(qq, jj) - wrap * 2 * M + 1 + 2))
                    nc.gpsimd.tensor_copy(g.near[:, j % g.RING, 0:DH], k.xn[:, j, ds((hp * 2 + q) * DH, DH)]).then_inc(near_ready, 1)
                    if first and hp == 1 and (q, j) == (1, g.RING):
                        divide(slice(0, P), 0, 2)

            if first:
                for hp in range(H // 2):
                    pair_of_heads(hp)
                divide(slice(0, DH), 1, 3)
            else:
                with pool.Fori(0, H // 2) as hp:
                    pair_of_heads(hp)

        @block.tensor
        def _(pe):
            pe.sem_inc(edge_free, g.RING)
            pe.sem_inc(kept_free, 2)
            with pe.Fori(0, H // 2) as hp:
                for q, j in steps:
                    if j == 0:
                        pe.wait_ge(sum_free, hp * 2 + (q + 1))
                    pe.wait_ge(near_ready, hp * (2 * NT) + (q * NT + j + 1))
                    if j in computed:
                        pe.wait_ge(edge_ready, hp * (2 * C) + (nth(q, j) + 1))
                    else:
                        m = nth_kept(q, j)
                        pe.wait_ge(kept_moved[m % 2], hp * (16 * M) + 16 * (m // 2 + 1))
                    edge = g.kept[:, nth_kept(q, j) % 2, :] if j in KEPT else g.edge[:, nth(q, j) % g.RING, :]
                    for i in range(4):
                        chunk = slice(i * 512, (i + 1) * 512)
                        if first:
                            ins = nc.tensor.matmul(ps[:, q, chunk], g.near[:, j % g.RING, :], edge[:, chunk],
                                                   start=(j == 0), stop=(j == NT - 1))
                        else:
                            half = slice(i % 2 * DH, i % 2 * DH + DH)
                            ins = nc.tensor.matmul(ps[half, q, chunk], g.near[:, j % g.RING, 0:DH], edge[:, chunk],
                                                   start=(j == 0), stop=(j == NT - 1))
                    ins.then_inc(edge_free if j in computed else kept_free, 1)

        @block.vector
        def _(dve):
            v = nc.vector
            dve.sem_inc(sum_free, 2)
            chain = Chain(dve, inv_done)
            def copy_out(hp, q):
                dve.wait_ge(edge_free, (2 * hp + q + 1) * C + g.RING)
                rows = slice(q * DH, (q + 1) * DH)
                chunks = lambda t, odd: t.rearrange("p (a b t) -> p a b t", b=2, t=512)[:, :, odd, :]
                for odd in range(2):
                    ins = v.tensor_tensor(chunks(k.xnT[rows, hp, :], odd), chunks(ps[odd * DH:(odd + 1) * DH, q, :], odd),
                                          chunks(g.inv[rows, hp, :], odd), ALU.mult)
                ins.then_inc(sum_free, 1)

            def sums_out(h):
                dve.wait_ge(edge_free, (h + 1) * NT + g.RING)
                chain.did(v.tensor_scalar(g.inv[h % 2 * DH:(h % 2 + 1) * DH, h // 2, :], ps[DH:2 * DH, h % 2, :], 1e-30, None, ALU.max))

            def features_out(h):
                v.tensor_copy(k.xnT[h % 2 * DH:(h % 2 + 1) * DH, h // 2, :], ps[0:DH, h % 2, :]).then_inc(sum_free, 1)

            def invert(rows, hp, piece):
                part = slice(piece * CH, (piece + 1) * CH)
                v.reciprocal(g.inv[rows, hp, part], g.inv[rows, hp, part]).then_inc(inverted, 1)

            def divide_last_head():
                dve.wait_ge(edge_free, H * NT + g.RING)
                top = slice(DH, 2 * DH)
                for side in range(2):
                    chain.did(v.tensor_scalar(last_inv[side * DH:(side + 1) * DH, :], ps[top, 1, side * HT:(side + 1) * HT],
                                              1e-30, None, ALU.max))
                chain.settle()
                for piece in range(2):
                    part = slice(piece * HT // 2, (piece + 1) * HT // 2)
                    v.reciprocal(last_inv[:, part], last_inv[:, part]).then_inc(last_ready, 1)
                dve.wait_ge(last_ready, 2)
                for side in range(2):
                    tokens = slice(side * HT, (side + 1) * HT)
                    chain.did(v.tensor_tensor(k.xnT[top, 1, tokens], ps[0:DH, 1, tokens], last_inv[side * DH:(side + 1) * DH, :], ALU.mult))
                chain.settle()

            for h in range(H):
                for turn, j in enumerate(computed):
                    n = h * C + turn
                    dve.wait_ge(exp_ready, n + 1)
                    slot = g.edge[:, n % g.RING, :]
                    masked = slot
                    if j in KEPT:
                        m = h * M + KEPT.index(j)
                        masked = g.kept[:, m % 2, :]
                        if m >= 2:
                            last = (m - 2) // M * NT + KEPT[(m - 2) % M]
                            dve.wait_ge(edge_free, last + 1 + g.RING)
                            dve.wait_ge(kept_moved[m % 2], 16 * (m // 2))
                    v.tensor_tensor(masked, slot, k.adjT[:, j, :], ALU.mult).then_inc(edge_ready, 1)
                    if h and turn == 2:
                        if first:
                            sums_out(h - 1)
                        else:
                            copy_out((h - 1) // 2, (h - 1) % 2)
                    if not first:
                        continue
                    if h and turn == 3:
                        features_out(h - 1)
                        chain.settle()
                    if h >= 2 and turn >= 4:
                        mine = [2 * (turn - 4), 2 * (turn - 4) + 1] if turn < 8 else [turn]
                        for piece in mine:
                            invert(slice(0, P if h == 2 else DH), h - 2, piece)
                    if h == 3 and turn >= 12:
                        dve.wait_ge(divided, 1)
                        part = turn - 12
                        chain.did(v.bn_stats(g.stats[:, 0, part, :], k.xnT[:, 0, part * 512:(part + 1) * 512]))
            if first:
                divide_last_head()
            else:
                copy_out(1, 1)


def phase_mlp(k, g, name, layer, pre_gamma, bias, gamma):
    nc = k.nc
    CH = 512
    pieces = [(q, c) for q in range(N // CH) for c in range(KC)]
    with ExitStack() as ctx, nc.Block() as block:
        stats = g.stats
        mv = ctx.enter_context(nc.sbuf_tensor("mv_" + name, [P, KC, 2], F32))
        var = ctx.enter_context(nc.sbuf_tensor("var_" + name, [P, KC], F32))
        std = ctx.enter_context(nc.sbuf_tensor("std_" + name, [P, KC], F32))
        tmp = ctx.enter_context(nc.sbuf_tensor("tmp_" + name, [P, KC], F32))
        scale = ctx.enter_context(nc.sbuf_tensor("scale_" + name, [P, KC], F32))
        shift = ctx.enter_context(nc.sbuf_tensor("shift_" + name, [P, KC], F32))
        ps = ctx.enter_context(nc.psum_tensor("ps_mlp_" + name, [P, KC, N], F32))
        dve_done, var_ready, std_ready = k.sem("dve_done_" + name), k.sem("var_" + name), k.sem("std_" + name)
        neg_ready, neg_exp, x_ready, mlp_ps = k.sem("neg_" + name), k.sem("neg_exp_" + name), k.sem("x_ready_" + name), k.sem("mlp_ps_" + name)
        biased, upper_ready, sum_ready = k.sem("biased_" + name), k.sem("upper_" + name), k.sem("sum_" + name)
        low, high = g.edge[:, 0:KC, :], g.edge[:, KC:2 * KC, :]
        pre_elu = pre_gamma is None
        past = len(pieces) if pre_elu else 0
        part = lambda t, q, c: t[:, c, q * CH:(q + 1) * CH]
        if pre_elu:
            x_back = k.sem("x_back")

            @block.sync
            def _(sp):
                sp.dma_start(k.x[:], k.x_dram).then_inc(x_back, 16)
                sp.wait_ge(x_back, 16)

        @block.vector
        def _(dve):
            v = nc.vector
            chain = Chain(dve, dve_done)
            link = chain.link
            norms = [0]

            def piece_stats(src, q, c):
                chain.did(v.bn_stats(stats[:, c, q, :], part(src, q, c)))

            def scale_and_shift(col):
                chain.settle()
                for c in range(KC):
                    chain.did(v.bn_aggr(mv[:, c, :], stats[:, c]))
                chain.settle()
                v.tensor_scalar(var[:], mv[:, :, 1], BN_EPS, None, ALU.add).then_inc(var_ready, 1)
                norms[0] += 1
                dve.wait_ge(std_ready, norms[0])
                link(v.reciprocal(scale[:], std[:]))
                rstd_of(chain, v, scale[:], var[:], tmp[:], None)
                link(v.tensor_tensor(scale[:], scale[:], k.vec[:, col:col + KC], ALU.mult))
                link(v.tensor_tensor(shift[:], mv[:, :, 0], scale[:], ALU.mult))
                link(v.tensor_tensor(shift[:], k.vec[:, col + KC:col + 2 * KC], shift[:], ALU.subtract))

            if pre_elu:
                maxed = {}

                def open_elu(i):
                    x = part(k.xnT, *pieces[i])
                    v.tensor_scalar(part(low, *pieces[i]), x, 0.0, None, ALU.min).then_inc(neg_ready, 1)
                    chain.did(v.tensor_scalar(x, x, 0.0, None, ALU.max))
                    maxed[i] = chain.count

                open_elu(0)
                for i in range(len(pieces)):
                    if i + 1 < len(pieces):
                        open_elu(i + 1)
                    x = part(k.xnT, *pieces[i])
                    dve.wait_ge(dve_done, maxed[i])
                    dve.wait_ge(neg_exp, i + 1)
                    v.scalar_tensor_tensor(out=x, in0=part(low, *pieces[i]), scalar=-1.0, in1=x, op0=ALU.add, op1=ALU.add).then_inc(x_ready, 1)
            else:
                for q in range(N // CH):
                    piece_stats(k.xnT, q, 1)
                scale_and_shift(pre_gamma)
                for q, c in pieces:
                    x = part(k.xnT, q, c)
                    v.tensor_scalar(x, x, scale[:, c:c + 1], shift[:, c:c + 1], ALU.mult, ALU.add).then_inc(x_ready, 1)

            def lower(i):
                q, c = pieces[i]
                dve.wait_ge(biased, i + 1)
                if pre_elu and i == 0:
                    dve.wait_ge(x_ready, len(pieces))
                v.tensor_scalar(part(low, q, c), part(high, q, c), 0.0, None, ALU.min).then_inc(neg_ready, 1)
                v.tensor_scalar(part(high, q, c), part(high, q, c), 0.0, None, ALU.max).then_inc(upper_ready, 1)

            summed = {}
            lower(0)
            for i in range(len(pieces)):
                if i + 1 < len(pieces):
                    lower(i + 1)
                y = part(high, *pieces[i])
                dve.wait_ge(sum_ready, i + 1)
                dve.wait_ge(neg_exp, past + i + 1)
                chain.did(v.scalar_tensor_tensor(out=y, in0=part(low, *pieces[i]), scalar=-1.0, in1=y, op0=ALU.add, op1=ALU.add))
                summed[i] = chain.count
                if i:
                    dve.wait_ge(dve_done, summed[i - 1])
                    piece_stats(high, *pieces[i - 1])
            chain.settle()
            piece_stats(high, *pieces[-1])
            scale_and_shift(gamma)
            for c in range(KC):
                chain.did(v.tensor_scalar(k.xnT[:, c, :], high[:, c, :], scale[:, c:c + 1], shift[:, c:c + 1], ALU.mult, ALU.add))
            chain.settle()

        @block.scalar
        def _(act):
            s = nc.scalar
            if pre_elu:
                for i in range(len(pieces)):
                    act.wait_ge(neg_ready, i + 1)
                    s.activation(part(low, *pieces[i]), part(low, *pieces[i]), ACT.Exp).then_inc(neg_exp, 1)
            else:
                act.wait_ge(var_ready, 1)
                s.activation(std[:], var[:], ACT.Sqrt).then_inc(std_ready, 1)
            def add_bias(i):
                q, c = pieces[i]
                act.wait_ge(mlp_ps, i + 1)
                s.activation(part(high, q, c), part(ps, q, c), ACT.Identity, bias=k.vec[:, bias + c:bias + c + 1]).then_inc(biased, 1)

            add_bias(0)
            for i, (q, c) in enumerate(pieces):
                if i + 1 < len(pieces):
                    add_bias(i + 1)
                act.wait_ge(neg_ready, past + i + 1)
                s.activation(part(low, q, c), part(low, q, c), ACT.Exp).then_inc(neg_exp, 1)
            act.wait_ge(var_ready, 1 if pre_elu else 2)
            s.activation(std[:], var[:], ACT.Sqrt).then_inc(std_ready, 1)

        @block.gpsimd
        def _(pool):
            for i, (q, c) in enumerate(pieces):
                pool.wait_ge(upper_ready, i + 1)
                y = part(high, q, c)
                nc.gpsimd.tensor_tensor(y, y, part(k.xnT, q, c), ALU.add).then_inc(sum_ready, 1)

        @block.tensor
        def _(pe):
            for q, c in pieces:
                pe.wait_ge(x_ready, KC * (q + 1))
                for kc in range(KC):
                    ins = nc.tensor.matmul(part(ps, q, c), g.mlp_wT[:, layer, kc, c * P:(c + 1) * P], part(k.xnT, q, kc),
                                           start=(kc == 0), stop=(kc == KC - 1))
                ins.then_inc(mlp_ps, 1)


def phase_back(k, g):
    nc = k.nc
    with ExitStack() as ctx, nc.Block() as block:
        ps = ctx.enter_context(nc.psum_tensor("ps_back", [P, 4, 512], F32))
        back_ps, back_sb = k.sem("back_ps"), k.sem("back_sb")

        @block.tensor
        def _(pe):
            for n in range(NT):
                if n >= 4:
                    pe.wait_ge(back_sb, n - 3)
                for c in range(KC):
                    ins = nc.tensor.matmul(ps[:, n % 4, c * P:(c + 1) * P], k.xnT[:, c, n * P:(n + 1) * P], g.head_wT[:, c, :],
                                           start=True, stop=True)
                ins.then_inc(back_ps, 1)

        @block.scalar
        def _(act):
            for n in range(NT):
                act.wait_ge(back_ps, n + 1)
                nc.scalar.activation(k.xn[:, n, :], ps[:, n % 4, 0:D], ACT.Copy).then_inc(back_sb, 1)


def phase_residual(k):
    nc = k.nc
    with ExitStack() as ctx, nc.Block() as block:
        ps = ctx.enter_context(nc.psum_tensor("ps_res", [P, 4, 512], F32))
        res_ps, res_sb, stats_done = k.sem("res_ps"), k.sem("res_sb"), k.sem("stats_done_res")

        @block.tensor
        def _(pe):
            for n in range(NT):
                if n >= 4:
                    pe.wait_ge(res_sb, n - 3)
                for c in range(KC):
                    ins = nc.tensor.transpose(ps[:, n % 4, c * P:(c + 1) * P], k.xnT[:, c, n * P:(n + 1) * P], k.ident[:])
                ins.then_inc(res_ps, 1)

        @block.vector
        def _(dve):
            def stats(n):
                dve.wait_ge(res_sb, n + 1)
                nc.vector.bn_stats(k.ln_stats[:, n, :], k.x[:, n, :]).then_inc(stats_done, 1)

            for n in range(NT):
                dve.wait_ge(res_ps, n + 1)
                nc.vector.tensor_tensor(k.x[:, n, :], k.x[:, n, :], ps[:, n % 4, 0:D], ALU.add).then_inc(res_sb, 1)
                if n:
                    stats(n - 1)
            stats(NT - 1)
            dve.wait_ge(stats_done, NT)


def gnn1(k, I):
    nc = k.nc
    with ExitStack() as ctx:
        def sb(name, shape, dt=F32):
            return ctx.enter_context(nc.sbuf_tensor(name, shape, dt))
        g = Shared()
        g.RING = 4
        g.KEPT = list(range(1, NT - g.RING, 2))
        k.kept_dram = nc.dram_tensor("kept_dram", [H * len(g.KEPT), P, N], F32).ap()
        k.x_dram = nc.dram_tensor("x_dram", [P, NT, D], F32).ap()
        g.kept = k.x[:].rearrange("p (u m) d -> p u (m d)", u=2)
        g.f1 = sb("f1", [P, H, N])
        g.f2_half = sb("f2_half", [P, NT, H])
        g.mlp_wT = sb("mlp_wT", [P, 2, KC, D])
        g.head_wT = sb("head_wT", [P, KC, P])
        g.near = sb("near", [P, g.RING, 2 * DH])
        with ExitStack() as wctx:
            g.head_w = wctx.enter_context(nc.sbuf_tensor("head_w", [P, KC, DH], F32))
            g.head_v = wctx.enter_context(nc.sbuf_tensor("head_v", [P, KC, 2, DH], F32))
            g.mlp_rows = wctx.enter_context(nc.sbuf_tensor("mlp_rows", [P, 2, KC, D], F32))
            block_norm(k, "n2", I, g)
            phase_gnn1_project(k, I, g)
        g.edge = sb("edge", [P, g.RING, N])
        g.inv = sb("inv1", [P, KC, N])
        g.stats = sb("stats1", [P, KC, 4, 6])
        phase_attend(k, g, "enc", True)
        phase_mlp(k, g, "enc_mlp", 0, VEC_COL["L1_gnn_enc_bn_gamma"], VEC_COL["L1_gnn_enc_mlp_b"], VEC_COL["L1_gnn_enc_mlp_bn_gamma"])
        phase_back(k, g)
        phase_attend(k, g, "dec", False)
        phase_mlp(k, g, "dec_mlp", 1, None, VEC_COL["L1_gnn_dec_mlp_b"], VEC_COL["L1_gnn_dec_mlp_bn_gamma"])
        phase_residual(k)


def build(nc, I, out, stop=99):
    with ExitStack() as ctx:
        def sb(name, shape, dt=F32):
            return ctx.enter_context(nc.sbuf_tensor(name, shape, dt))
        k = Shared()
        k.nc, k.sems = nc, []

        def new_sem(name):
            k.sems.append(nc.alloc_semaphore(name=name))
            return k.sems[-1]

        def clear_sems():
            nc.clear_and_free_semaphores(k.sems)
            nc.all_engine_barrier()
            k.sems = []

        k.sem = new_sem
        k.xn_dram = nc.dram_tensor("xn_dram", [N, D], F32).ap()
        k.results = nc.dram_tensor("results", [TOP * N + NB * BLK, D], F32).ap()
        k.b1_dram = nc.dram_tensor("b1_dram", [P, 2, E * FT], F32).ap()
        k.x = sb("x", [P, NT, D])
        k.xn = sb("xn", [P, NT, D])
        k.xnT = sb("xnT", [P, KC, N])
        k.adjT = sb("adjT", [P, NT, N], BF16)
        k.ident, k.ones, k.before = sb("ident", [P, P]), sb("ones", [P, P]), sb("before", [P, P])
        k.iota, k.iota_b = sb("iota", [P, P]), sb("iota_b", [P, P], BF16)
        k.lane_id, k.tile_id, k.spare = sb("lane_id", [P, 1]), sb("tile_id", [P, TOP, NT], BF16), sb("spare", [P, ST])
        k.vec = sb("vec", [P, VEC_ROWS])
        k.gate_w, k.gate_b = sb("gate_w", [P, 2, KC, E]), sb("gate_b", [P, 2, E])
        k.ln_stats, k.ln_mv = sb("ln_stats", [P, NT, 6]), sb("ln_mv", [P, NT, 2])
        k.ln_var, k.ln_std, k.ln_rstd, k.ln_tmp = (sb(n, [P, NT]) for n in ("ln_var", "ln_std", "ln_rstd", "ln_tmp"))
        k.pair_w = sb("pair_w", [P, NT, TOP])
        k.token_of = sb("token_of", [P, ST], I32)
        k.row_of = sb("row_of", [P, ST], I32)
        k.expert = sb("expert", [P, NB], I32)
        k.b1_sb, k.b2_sb = sb("b1_sb", [P, 2, FT]), sb("b2_sb", [P, 2, D])

        with ExitStack() as gctx:
            k.w_cat = gctx.enter_context(nc.sbuf_tensor("w_cat", [P, KC, 2 * D + 6], F32))
            k.a_sa = gctx.enter_context(nc.sbuf_tensor("a_sa", [P, 2 * D], F32))
            k.b_gcnb = gctx.enter_context(nc.sbuf_tensor("b_gcnb", [P, D], F32))
            k.type_bias = gctx.enter_context(nc.sbuf_tensor("type_bias", [P, 2], F32))
            phase_load(k, I)
            if stop > 1:
                phase_gnn0(k, I)
        if stop > 2:
            weights = expert_weights(k, 0, I)
            phase_route(k, 0, weights)
        if stop > 3:
            phase_experts(k, 0, weights)
        if stop > 4:
            phase_combine(k, 0)
            clear_sems()
        if stop > 5:
            gnn1(k, I)
        if stop > 6:
            weights = expert_weights(k, 1, I)
            phase_route(k, 1, weights)
            phase_experts(k, 1, weights)
            phase_combine(k, 1, out)


INPUTS = ["x", "adj", "L0_gnn_W_sa", "L0_gnn_a_sa", "L0_gnn_W_gcnb", "L0_gnn_b_gcnb", "L0_gnn_Wa", "L0_gnn_ba", "L0_gnn_Wb", "L0_gnn_bb",
          "L0_ffn_gate_w", "L0_ffn_gate_b", "L0_ffn_w1", "L0_ffn_b1", "L0_ffn_w2", "L0_ffn_b2", "L1_gnn_W", "L1_gnn_V",
          "L1_gnn_enc_bn_gamma", "L1_gnn_enc_bn_beta", "L1_gnn_enc_mlp_W", "L1_gnn_enc_mlp_b", "L1_gnn_enc_mlp_bn_gamma",
          "L1_gnn_enc_mlp_bn_beta", "L1_gnn_dec_mlp_W", "L1_gnn_dec_mlp_b", "L1_gnn_dec_mlp_bn_gamma", "L1_gnn_dec_mlp_bn_beta",
          "L1_ffn_Wg", "L1_ffn_bg", "L1_ffn_W1", "L1_ffn_b1", "L1_ffn_W2", "L1_ffn_b2"]


def kernel(**inputs):
    import numpy as np
    import concourse.bacc as bacc
    from concourse.bass_utils import run_bass_kernel_spmd

    nc = bacc.Bacc("TRN2", target_bir_lowering=False, num_devices=1)
    arrays, aps = {}, {}
    for name in INPUTS:
        a = np.ascontiguousarray(inputs[name])
        arrays[f"in_{name}"] = a
        aps[name] = nc.dram_tensor(f"in_{name}", a.shape, mybir.dt.from_np(a.dtype), kind="ExternalInput").ap()
    out = nc.dram_tensor("out", (N, D), F32, kind="ExternalOutput").ap()
    build(nc, aps, out)
    result = run_bass_kernel_spmd(nc, [arrays], core_ids=[0])
    return result.results[0]["out"]
```
